# Optimizing a Trainium2 kernel written in Bass

```python
import numpy as np
import jax
import jax.numpy as jnp

def _softmax(x, axis=-1):
    return jax.nn.softmax(x, axis=axis)

def _gelu(x):
    return jax.nn.gelu(x, approximate=True)

def _silu(x):
    return jax.nn.silu(x)

def _sigmoid(x):
    return jax.nn.sigmoid(x)

def _layernorm(x, axis=-1, eps=1e-05):
    m = jnp.mean(x, axis=axis, keepdims=True)
    v = jnp.var(x, axis=axis, keepdims=True)
    return (x - m) / jnp.sqrt(v + eps)

def _scatter_add(tgt, idx, src, axis=0):
    return tgt.at[idx].add(src)

def _segment_sum(src, seg, n):
    return jax.ops.segment_sum(src, seg, n)
kernel_name = 'mk_adaln_d1_jaxref_r8_06623f'

def setup_inputs(seed: int=0):
    np.random.seed(seed)
    _w = jnp.asarray

    def _L0_attn_setup():
        import jax, jax.numpy as jnp
        import numpy as np
        import math
        B, L, D = (2, 256, 256)
        H, DH = (16, 128)
        R = 16
        WIN = 64
        EPS = 1e-06

        def _lora_proj(h, Wb, A, Bm, scale):
            return h @ Wb.T + h @ A.T @ Bm.T * scale

        def _rope_freqs(seq_len, d_head):
            half = d_head // 2
            theta = 1.0 / 10000.0 ** (jnp.arange(half, dtype=jnp.float32) / half)
            freqs = jnp.arange(seq_len, dtype=jnp.float32)[:, None] * theta[None, :]
            emb = jnp.concatenate([freqs, freqs], axis=-1)
            return (jnp.cos(emb), jnp.sin(emb))

        def _apply_rope(x, cos, sin):
            half = x.shape[-1] // 2
            x1, x2 = (x[..., :half], x[..., half:])
            rotated = jnp.concatenate([-x2, x1], axis=-1)
            return x * cos[None, None] + rotated * sin[None, None]
        key = jax.random.key(seed)
        ks = jax.random.split(key, 16)

        def rn(k, shape, s=1.0):
            return jax.random.normal(k, shape, dtype=jnp.float32) * s
        d_in_std = 1.0 / math.sqrt(D)
        return {'x': rn(ks[0], (B, L, D)), 'norm_w': jnp.ones((D,), jnp.float32), 'wq': rn(ks[1], (H * DH, D), d_in_std), 'wk': rn(ks[2], (H * DH, D), d_in_std), 'wv': rn(ks[3], (H * DH, D), d_in_std), 'wo': rn(ks[4], (D, H * DH), d_in_std), 'qA': rn(ks[5], (R, D), 0.02), 'qB': rn(ks[6], (H * DH, R), 0.02), 'kA': rn(ks[7], (R, D), 0.02), 'kB': rn(ks[8], (H * DH, R), 0.02), 'vA': rn(ks[9], (R, D), 0.02), 'vB': rn(ks[10], (H * DH, R), 0.02), 'oA': rn(ks[11], (R, H * DH), 0.02), 'oB': rn(ks[12], (D, R), 0.02)}
    _L0_attn_in = _L0_attn_setup()

    def _L0_ffn_setup():
        import jax, jax.numpy as jnp
        import numpy as np
        B, S, H = (2, 256, 256)
        E, I, K = (8, 176, 2)
        SHARED_I = 176 * 2

        def _moe_forward(hidden_states, gate_w, w1, w3, w2, sw1, sw3, sw2):
            x = hidden_states.reshape(-1, H)
            T = x.shape[0]
            logits = x @ gate_w.T
            scores = jax.nn.softmax(logits, axis=-1)
            topk_w, topk_idx = jax.lax.top_k(scores, K)
            topk_w = topk_w / jnp.sum(topk_w, axis=-1, keepdims=True)
            h = jnp.einsum('th,ehi->eti', x, w1)
            g = jnp.einsum('th,ehi->eti', x, w3)
            y_all = jnp.einsum('eti,eih->eth', jax.nn.silu(h) * g, w2)
            tok = jnp.arange(T)[:, None]
            y_sel = y_all[topk_idx, tok]
            y = jnp.sum(y_sel * topk_w[..., None], axis=1)
            shared = jax.nn.silu(x @ sw1) * (x @ sw3) @ sw2
            return (y + shared).reshape(hidden_states.shape)
        key = jax.random.key(seed)
        ks = jax.random.split(key, 8)
        s = 0.02
        return {'hidden_states': jax.random.normal(ks[0], (B, S, H), jnp.float32), 'gate_w': jax.random.normal(ks[1], (E, H), jnp.float32) * s, 'w1': jax.random.normal(ks[2], (E, H, I), jnp.float32) * s, 'w3': jax.random.normal(ks[3], (E, H, I), jnp.float32) * s, 'w2': jax.random.normal(ks[4], (E, I, H), jnp.float32) * s, 'sw1': jax.random.normal(ks[5], (H, SHARED_I), jnp.float32) * s, 'sw3': jax.random.normal(ks[6], (H, SHARED_I), jnp.float32) * s, 'sw2': jax.random.normal(ks[7], (SHARED_I, H), jnp.float32) * s}
    _L0_ffn_in = _L0_ffn_setup()
    _L0_c = _w((lambda *s: np.random.randn(*s).astype(np.float32) * 0.05)(1, 256))
    _L0_wmod = _w((lambda *s: np.random.randn(*s).astype(np.float32) * 0.05)(256, 6 * 256) * 256 ** (-0.5))
    _d = {'L0_attn_x': _L0_attn_in['x'], 'L0_attn_norm_w': _L0_attn_in['norm_w'], 'L0_attn_wq': _L0_attn_in['wq'], 'L0_attn_wk': _L0_attn_in['wk'], 'L0_attn_wv': _L0_attn_in['wv'], 'L0_attn_wo': _L0_attn_in['wo'], 'L0_attn_qA': _L0_attn_in['qA'], 'L0_attn_qB': _L0_attn_in['qB'], 'L0_attn_kA': _L0_attn_in['kA'], 'L0_attn_kB': _L0_attn_in['kB'], 'L0_attn_vA': _L0_attn_in['vA'], 'L0_attn_vB': _L0_attn_in['vB'], 'L0_attn_oA': _L0_attn_in['oA'], 'L0_attn_oB': _L0_attn_in['oB'], 'L0_ffn_gate_w': _L0_ffn_in['gate_w'], 'L0_ffn_w1': _L0_ffn_in['w1'], 'L0_ffn_w3': _L0_ffn_in['w3'], 'L0_ffn_w2': _L0_ffn_in['w2'], 'L0_ffn_sw1': _L0_ffn_in['sw1'], 'L0_ffn_sw3': _L0_ffn_in['sw3'], 'L0_ffn_sw2': _L0_ffn_in['sw2'], 'L0_c': _L0_c, 'L0_wmod': _L0_wmod}
    _x0 = _d['L0_attn_x']
    _d['L0_attn_x'] = jax.random.normal(jax.random.fold_in(jax.random.key(seed), 1), (1, 1024, 256), dtype=_x0.dtype)
    del _x0
    return _d

def reference(L0_attn_x, L0_attn_norm_w, L0_attn_wq, L0_attn_wk, L0_attn_wv, L0_attn_wo, L0_attn_qA, L0_attn_qB, L0_attn_kA, L0_attn_kB, L0_attn_vA, L0_attn_vB, L0_attn_oA, L0_attn_oB, L0_ffn_gate_w, L0_ffn_w1, L0_ffn_w3, L0_ffn_w2, L0_ffn_sw1, L0_ffn_sw3, L0_ffn_sw2, L0_c, L0_wmod):

    def _L0_attn_ref(x, norm_w, wq, wk, wv, wo, qA, qB, kA, kB, vA, vB, oA, oB):
        import jax, jax.numpy as jnp
        import numpy as np
        import math
        B, L, D = (2, 256, 256)
        H, DH = (16, 128)
        R = 16
        WIN = 64
        EPS = 1e-06

        def _lora_proj(h, Wb, A, Bm, scale):
            return h @ Wb.T + h @ A.T @ Bm.T * scale

        def _rope_freqs(seq_len, d_head):
            half = d_head // 2
            theta = 1.0 / 10000.0 ** (jnp.arange(half, dtype=jnp.float32) / half)
            freqs = jnp.arange(seq_len, dtype=jnp.float32)[:, None] * theta[None, :]
            emb = jnp.concatenate([freqs, freqs], axis=-1)
            return (jnp.cos(emb), jnp.sin(emb))

        def _apply_rope(x, cos, sin):
            half = x.shape[-1] // 2
            x1, x2 = (x[..., :half], x[..., half:])
            rotated = jnp.concatenate([-x2, x1], axis=-1)
            return x * cos[None, None] + rotated * sin[None, None]
        lora_scale = 1.0 / qA.shape[0]
        residual = x
        h = x * jax.lax.rsqrt(jnp.mean(x * x, axis=-1, keepdims=True) + EPS) * norm_w
        Q = _lora_proj(h, wq, qA, qB, lora_scale)
        K = _lora_proj(h, wk, kA, kB, lora_scale)
        V = _lora_proj(h, wv, vA, vB, lora_scale)
        b, l, _ = x.shape
        Q = Q.reshape(b, l, H, DH).transpose(0, 2, 1, 3)
        K = K.reshape(b, l, H, DH).transpose(0, 2, 1, 3)
        V = V.reshape(b, l, H, DH).transpose(0, 2, 1, 3)
        cos, sin = _rope_freqs(l, DH)
        Q = _apply_rope(Q, cos, sin)
        K = _apply_rope(K, cos, sin)
        i = jnp.arange(l)[:, None]
        j = jnp.arange(l)[None, :]
        valid = (j <= i) & (j >= i - WIN + 1)
        mask = jnp.where(valid, 0.0, -jnp.inf).astype(x.dtype)
        scores = jnp.einsum('bhqd,bhkd->bhqk', Q, K) / math.sqrt(DH)
        attn = jax.nn.softmax(scores + mask[None, None], axis=-1)
        out = jnp.einsum('bhqk,bhkd->bhqd', attn, V)
        out = out.transpose(0, 2, 1, 3).reshape(b, l, H * DH)
        out = _lora_proj(out, wo, oA, oB, lora_scale)
        return residual + out

    def _L0_ffn_ref(hidden_states, gate_w, w1, w3, w2, sw1, sw3, sw2):
        import jax, jax.numpy as jnp
        import numpy as np
        B, S, H = (2, 256, 256)
        E, I, K = (8, 176, 2)
        SHARED_I = 176 * 2

        def _moe_forward(hidden_states, gate_w, w1, w3, w2, sw1, sw3, sw2):
            x = hidden_states.reshape(-1, H)
            T = x.shape[0]
            logits = x @ gate_w.T
            scores = jax.nn.softmax(logits, axis=-1)
            topk_w, topk_idx = jax.lax.top_k(scores, K)
            topk_w = topk_w / jnp.sum(topk_w, axis=-1, keepdims=True)
            h = jnp.einsum('th,ehi->eti', x, w1)
            g = jnp.einsum('th,ehi->eti', x, w3)
            y_all = jnp.einsum('eti,eih->eth', jax.nn.silu(h) * g, w2)
            tok = jnp.arange(T)[:, None]
            y_sel = y_all[topk_idx, tok]
            y = jnp.sum(y_sel * topk_w[..., None], axis=1)
            shared = jax.nn.silu(x @ sw1) * (x @ sw3) @ sw2
            return (y + shared).reshape(hidden_states.shape)
        return _moe_forward(hidden_states, gate_w, w1, w3, w2, sw1, sw3, sw2)
    x = L0_attn_x
    mod = (_silu(L0_c) @ L0_wmod).reshape(L0_c.shape[0], 6, 1, -1)
    sa, ca, ga, sb, cb, gb = (mod[:, 0], mod[:, 1], mod[:, 2], mod[:, 3], mod[:, 4], mod[:, 5])
    ga = (2 * (ga >= 0) - 1) * jnp.maximum(jnp.abs(ga), 0.25)
    gb = (2 * (gb >= 0) - 1) * jnp.maximum(jnp.abs(gb), 0.25)
    h = _layernorm(x, axis=-1) * (1 + ca) + sa
    x = x + ga * _L0_attn_ref(h, L0_attn_norm_w, L0_attn_wq, L0_attn_wk, L0_attn_wv, L0_attn_wo, L0_attn_qA, L0_attn_qB, L0_attn_kA, L0_attn_kB, L0_attn_vA, L0_attn_vB, L0_attn_oA, L0_attn_oB)
    h = _layernorm(x, axis=-1) * (1 + cb) + sb
    x = x + gb * _L0_ffn_ref(h, L0_ffn_gate_w, L0_ffn_w1, L0_ffn_w3, L0_ffn_w2, L0_ffn_sw1, L0_ffn_sw3, L0_ffn_sw2)
    return x

_drawn_inputs = setup_inputs


def setup_inputs(seed=0):
    import zlib

    import numpy as np

    out = dict(_drawn_inputs(seed))
    spreads = {'L0_attn_norm_w': (1.0, 0.2)}
    factors = {'L0_attn_qA': 8.0,
     'L0_attn_qB': 8.0,
     'L0_attn_kA': 8.0,
     'L0_attn_kB': 8.0,
     'L0_attn_vA': 8.0,
     'L0_attn_vB': 8.0,
     'L0_attn_oA': 8.0,
     'L0_attn_oB': 8.0,
     'L0_ffn_gate_w': 8.0,
     'L0_ffn_w1': 8.0,
     'L0_ffn_w3': 8.0,
     'L0_ffn_w2': 8.0,
     'L0_ffn_sw1': 8.0,
     'L0_ffn_sw3': 8.0,
     'L0_ffn_sw2': 8.0}
    for name, (base, spread) in spreads.items():
        noise = np.random.default_rng([zlib.crc32(name.encode()), seed]).standard_normal(out[name].shape)
        drawn = base * np.exp(spread * noise) if base else spread * noise
        out[name] = jnp.asarray(drawn.astype(out[name].dtype))
    for name, factor in factors.items():
        out[name] = (out[name] * factor).astype(out[name].dtype)
    return out
```

```python
import concourse.bass as bass
from concourse import mybir
from contextlib import ExitStack

T = 1024
D = 256
KD = D // 128
H = 16
DH = 128
WIN = 64
R = 16
PAIRS = H // 2
PW = 3 * 2 * DH
NB = T // 128
E = 8
FI = 176
CH = 14
GK = 2 * E + 1
UPW = 5 * 128
SCALE = DH ** -0.5
LORA_SCALE = 1.0 / R
LN_EPS = 1e-5
RMS_EPS = 1e-6

PE_STEP = [("S", 0), ("Q", 0), ("V", 0), ("S", 1), ("Q", 1), ("T", 0), ("V", 1), ("O", 0), ("Q", 2),
           ("S", 2), ("T", 1), ("V", 2), ("O", 1), ("X", 0), ("Q", 3), ("S", 3), ("T", 2), ("V", 3),
           ("X", 1), ("O", 2), ("Q", 4), ("W", 0), ("P", 0), ("W", 1), ("T", 3), ("X", 2), ("Q", 5),
           ("O", 3), ("Q", 6), ("G", 0), ("X", 3), ("Q", 7), ("G", 1), ("W", 2), ("G", 2), ("W", 3)]
ACT_STEP = [("Q", 0), ("E", 0), ("V", 0), ("Q", 1), ("E", 1), ("T", 0), ("V", 1), ("O", 0), ("Q", 2),
            ("T", 1), ("E", 2), ("V", 2), ("O", 1), ("X", 0), ("Q", 3), ("T", 2), ("E", 3), ("V", 3),
            ("X", 1), ("O", 2), ("Q", 4), ("P", 0), ("T", 3), ("PH", 0), ("X", 2), ("Q", 5), ("O", 3),
            ("Q", 6), ("G", 0), ("X", 3), ("GH", 0), ("Q", 7), ("G", 1), ("G", 2), ("GH", 1),
            ("GH", 2)]
DVE_STEP = [("M", 0), ("QA", 0), ("M", 1), ("QA", 1), ("QR", 0), ("N", 0), ("QR", 1), ("QA", 2),
            ("M", 2), ("N", 1), ("QR", 2), ("XL", 0), ("QA", 3), ("M", 3), ("N", 2), ("XL", 1),
            ("QR", 3), ("QA", 4), ("W", 0), ("P", 0), ("W", 1), ("N", 3), ("QR", 4), ("XL", 2),
            ("QA", 5), ("QA", 6), ("QR", 5), ("G", 0), ("XL", 3), ("QR", 6), ("QA", 7), ("G", 1),
            ("W", 2), ("G", 2), ("QR", 7), ("W", 3)]
POOL_STEP = [("QB", 0), ("QB", 1), ("QB", 2), ("QB", 3), ("QB", 4), ("PL", 0), ("QB", 5), ("QB", 6),
             ("GL", 0), ("QB", 7), ("GL", 1), ("GL", 2)]
FILL_KINDS = "QVGP"
FILL_AT = {e: j for j, e in enumerate(e for e in PE_STEP if e[0] in FILL_KINDS)}
FILL_AT_6 = {e: j for j, e in enumerate(e for e in FILL_AT if e[0] != "G")}
AHEAD = ([("G", m) for m in range(3)] + [("Q", t) for t in range(8)] + [("V", v) for v in range(4)]
         + [("P", 0)] + [("G1", m) for m in range(3)])
FILLS_AHEAD = len(AHEAD)
FILLS = len(FILL_AT)


def build(nc, x, cos_t, sin_t, mask, ident, c_col, w_mod, norm_w, w_qkv, b_qkv, a_qkv, w_o, a_o,
          b_o, gate_w, w_up, w_down, tie, out):
    f32, f32r, bf16 = mybir.dt.float32, mybir.dt.float32r, mybir.dt.bfloat16
    ALU, ACT, AX = mybir.AluOpType, mybir.ActivationFunctionType, mybir.AxisListType

    ctx = ExitStack()
    with ctx:
        def sb(name, shape, dt=f32):
            return ctx.enter_context(nc.sbuf_tensor(name, shape, dt))

        def sem(name):
            return ctx.enter_context(nc.semaphore(name))

        x_sb = sb("x_sb", [128, NB, D])
        res = sb("res", [128, NB, D])
        hi_t = sb("hi_t", [128, KD, T], f32r)
        lo_t = sb("lo_t", [128, KD, T], f32r)
        cos_sb = sb("cos_sb", [128, T])
        sin_sb = sb("sin_sb", [128, T])
        mask_sb = sb("mask_sb", [128, 2, 512], bf16)
        id_sb = sb("id_sb", [128, 128])
        id_bf = sb("id_bf", [128, 128], bf16)
        w_raw = sb("w_raw", [128, 2, KD, PW])
        w_hi = sb("w_hi", [128, 2, KD, PW], f32r)
        w_lo = sb("w_lo", [128, 2, KD, PW], f32r)
        bq_sb = sb("bq_sb", [96, 2, 2 * DH])
        aq_sb = sb("aq_sb", [96, D])
        wo_raw = sb("wo_raw", [128, 2, 2, D])
        wo_hi = sb("wo_hi", [128, 2, 2, D], f32r)
        wo_lo = sb("wo_lo", [128, 2, 2, D], f32r)
        ao_sb = sb("ao_sb", [R, 2, 2 * DH])
        bo_sb = sb("bo_sb", [R, D])
        q_t = sb("q_t", [128, 2, 2, T])
        k_t = sb("k_t", [128, 2, 2, WIN + T])
        v_sb = sb("v_sb", [128, 2, NB, 2 * DH])
        v_off = sb("v_off", [128, 2, NB, 2 * DH])
        fold_tmp = sb("fold_tmp", [128, 2, 512])
        qk_raw = sb("qk_raw", [128, 4, 512])
        rot_a = sb("rot_a", [128, 2, 512])
        rot_b = sb("rot_b", [128, 2, 512])
        probs = sb("probs", [128, 2, 512])
        probs_t = sb("probs_t", [128, 2, 512])
        o_norm = sb("o_norm", [128, 2, 512])
        o_hi = sb("o_hi", [128, 2, 512], f32r)
        o_lo = sb("o_lo", [128, 2, 512], f32r)
        neg_max = sb("neg_max", [128, 2, 4])
        row_sum = sb("row_sum", [128, 2, 4])
        row_inv = sb("row_inv", [128, 2, 4])
        mod_b = sb("mod_b", [128, 2, D])
        mod_c = sb("mod_c", [128, 2, KD])
        small = sb("small", [128, 512])
        zero_bf = sb("zero_bf", [128, 128], bf16)
        gate_t = w_hi[0:GK, :, 1, 0:512]
        g_hi = w_hi[:, 0, 1, 512:512 + NB * E]
        wm_sb = v_off[:, :, :, :].rearrange("p s b d -> p (s b d)")[:, 0:KD * 6 * D].rearrange(
            "p (k n) -> p k n", k=KD)
        c_rep = v_sb[:, 1, 0, 0:KD * 128].rearrange("p (k n) -> p k n", k=KD)
        sq_out = v_sb[:, 0, :, :]
        sgn_g = v_sb[:, 1, 2:4, :].rearrange("p b d -> p (b d)")
        mod_a = v_sb[:, 1, 4:6, :]
        h_norm = q_t[:, 0, :, :].rearrange("p h t -> p (h t)").rearrange("p (b d) -> p b d", d=D)
        stats = small[:, 0:6 * NB].rearrange("p (b s) -> p b s", s=6)
        mean_var = small[:, 48:48 + 2 * NB].rearrange("p (b s) -> p b s", s=2)
        rstd = small[:, 64:72]
        tmp8 = small[:, 72:80]
        nw_sb = small[:, 80:82]
        c_sb = small[:, 82:84]
        sil_c = small[:, 86:88]
        ssq = small[:, 88:96]
        lg = small[:, 96:160]
        sc = small[:, 160:224]
        oh1 = small[:, 224:288]
        oh2 = small[:, 288:352]
        t64 = small[:, 352:416]
        tie_sb = small[:, 416:480]
        m8 = small[:, 480:488]
        g_cat = q_t[:, 1, 0, 0:NB * GK].rearrange("p (b g) -> p b g", g=GK)
        h2_t = k_t[:, :, :, 0:T].rearrange("p s h t -> p (s h) t")[:, 0:KD, :]
        gw_sb = small[:, 488:504].rearrange("p (k e) -> p k e", k=KD)
        z_sb = q_t[:, 0, :, :].rearrange("p h t -> p (h t)").rearrange("p (b d) -> p b d", d=D)
        y_out = v_sb[:, 0, :, :]

        bank = [ctx.enter_context(nc.psum_tensor(f"bank{i}", [128, 512], f32)) for i in range(8)]
        S_BANK, PT_BANK, O_BANK, OT_BANK, W_BANK = bank[0:2], bank[2], bank[3], bank[4], bank[5]
        FILL_BANK = bank[6:8]

        ld_x, ld_tab, ld_mod, ld_small, ld_lora = (
            sem("ld_x"), sem("ld_tab"), sem("ld_mod"), sem("ld_small"), sem("ld_lora"))
        ld_raw = [sem("ld_raw0"), sem("ld_raw1")]
        ld_wo = [sem("ld_wo0"), sem("ld_wo1")]
        ld_up = [sem("ld_up0"), sem("ld_up1")]
        ld_down = [sem("ld_down0"), sem("ld_down1")]
        v_moved = [sem("v_moved0"), sem("v_moved1")]
        zeroed, silu_c, c_spread, mod_ready, mod_kept = (
            sem("zeroed"), sem("silu_c"), sem("c_spread"), sem("mod_ready"), sem("mod_kept"))
        stats_done, var_done, std_done, rstd_done = (
            sem("stats_done"), sem("var_done"), sem("std_done"), sem("rstd_done"))
        h_done, squared, ms_done, rms_done, h_normed = (
            sem("h_done"), sem("squared"), sem("ms_done"), sem("rms_done"), sem("h_normed"))
        h_turned, h_hi, h_lo, id_done = sem("h_turned"), sem("h_hi"), sem("h_lo"), sem("id_done")
        x_normed, rot_b_half = sem("x_normed"), sem("rot_b_half")
        scored, maxed, exped = sem("scored"), sem("maxed"), sem("exped")
        p_turned, p_kept, summed = sem("p_turned"), sem("p_kept"), sem("summed")
        o_ready, o_kept, o_turned = sem("o_ready"), sem("o_kept"), sem("o_turned")
        oh_kept, ol_kept, w_ready, w_added = (
            sem("oh_kept"), sem("ol_kept"), sem("w_ready"), sem("w_added"))
        filled, fill_kept = sem("filled"), sem("fill_kept")
        rot_a_done, rot_b_done, rotated = sem("rot_a_done"), sem("rot_b_done"), sem("rotated")
        folded, w_hi_done, w_lo_done = sem("folded"), sem("w_hi_done"), sem("w_lo_done")
        folo_done, wo_hi_done, wo_lo_done = sem("folo_done"), sem("wo_hi_done"), sem("wo_lo_done")
        x1_done, z_done, z_turned, z_kept, z_hi, z_lo = (
            sem("x1_done"), sem("z_done"), sem("z_turned"), sem("z_kept"), sem("z_hi"), sem("z_lo"))
        logits, lg_done, lg_exp, gating, gates_done, g_turned, gates_kept, g_hi_done = (
            sem("logits"), sem("lg_done"), sem("lg_exp"), sem("gating"), sem("gates_done"),
            sem("g_turned"), sem("gates_kept"), sem("g_hi_done"))
        up_ready, silu_done, mul_done, act_done, act_hi, act_lo = (
            sem("up_ready"), sem("silu_done"), sem("mul_done"), sem("act_done"), sem("act_hi"),
            sem("act_lo"))
        up_w_hi, up_w_lo, down_w_hi, down_w_lo = (
            sem("up_w_hi"), sem("up_w_lo"), sem("down_w_hi"), sem("down_w_lo"))
        down_done, y_scaled, y_done, stored = (
            sem("down_done"), sem("y_scaled"), sem("y_done"), sem("stored"))

        block = ctx.enter_context(nc.Block())

        def steps(eng, order, step):
            with eng.Fori(0, PAIRS // 2 - 1) as i:
                for slot in range(2):
                    step(i * 2 + slot, slot, i, order, FILL_AT)
            step(PAIRS - 2, 0, PAIRS // 2 - 1, [e for e in order if e[0][0] != "G"], FILL_AT_6)
            step(PAIRS - 1, 1, PAIRS // 2 - 1,
                 [e for e in order if e[0] in ("S", "T", "O", "X", "W", "E", "M", "N", "XL")], {})

        def fill_no(p, j):
            return p * FILLS + (FILLS_AHEAD + j)

        def fill_bank(j):
            return FILL_BANK[(FILLS_AHEAD + j) % 2][:, :]

        def place(t, slot):
            head, cols = t // 2 % 2, (t % 2) * 512
            if t < 4:
                return q_t[:, slot, head, cols:cols + 512]
            return k_t[:, slot, head, WIN + cols:WIN + cols + 512]

        @block.sync
        def _(sp):
            sp.dma_start(x_sb[:, :, :], x.rearrange("(b p) d -> p b d", p=128)).then_inc(ld_x, 16)
            sp.dma_start(wm_sb, w_mod).then_inc(ld_mod, 16)

            def load_pair(p, slot):
                sp.dma_start(w_raw[:, slot], w_qkv[bass.ds(p, 1)].rearrange("o p k n -> (o p) k n")) \
                    .then_inc(ld_raw[slot], 16)
                sp.dma_start(bq_sb[:, slot], b_qkv[bass.ds(p, 1)].rearrange("o r n -> (o r) n")) \
                    .then_inc(ld_raw[slot], 16)

            def load_wo(p, slot):
                sp.dma_start(wo_raw[:, slot], w_o[bass.ds(p, 1)].rearrange("o p h n -> (o p) h n")) \
                    .then_inc(ld_wo[slot], 16)
                sp.dma_start(ao_sb[:, slot], a_o[bass.ds(p, 1)].rearrange("o r n -> (o r) n")) \
                    .then_inc(ld_wo[slot], 16)

            def move_values(slot):
                sp.dma_start(v_off[0:64, slot, 1:NB], v_sb[64:128, slot, 0:NB - 1]) \
                    .then_inc(v_moved[slot], 16)
                sp.dma_start(v_off[64:128, slot, :], v_sb[0:64, slot, :]).then_inc(v_moved[slot], 16)

            load_pair(0, 0)
            load_wo(0, 0)
            load_pair(1, 1)
            load_wo(1, 1)
            sp.wait_ge(fill_kept, AHEAD.index(("V", 3)) + 3)
            sp.wait_ge(mod_ready, 1)
            move_values(0)

            def step(p, slot, half, order, at):
                kinds = {k for k, _ in order}
                if "G" in kinds:
                    sp.wait_ge(w_lo_done, p * 3 + 3)
                    load_pair(p + 2, slot)
                    sp.wait_ge(wo_lo_done, p + 1)
                    load_wo(p + 2, slot)
                if "V" in kinds:
                    sp.wait_ge(fill_kept, fill_no(p, at["V", 3] + 3))
                    move_values(1 - slot)

            steps(sp, PE_STEP, step)

            def load_up(c, slot):
                sp.dma_start(w_raw[:, slot, 0, 0:UPW],
                             w_up[bass.ds(c, 1)].rearrange("o p n -> (o p) n")) \
                    .then_inc(ld_up[slot], 16)

            def load_down(c, slot):
                sp.dma_start(wo_raw[:, slot, 0],
                             w_down[bass.ds(c, 1)].rearrange("o p n -> (o p) n")) \
                    .then_inc(ld_down[slot], 16)

            sp.wait_ge(w_lo_done, 3 * PAIRS)
            sp.wait_ge(wo_lo_done, PAIRS)
            for slot in range(2):
                load_up(slot, slot)
                load_down(slot, slot)

            def next_chunk(n, c, slot):
                sp.wait_ge(up_w_lo, n - 1)
                load_up(c, slot)
                sp.wait_ge(down_w_lo, n - 1)
                load_down(c, slot)

            for first in (0, CH):
                with sp.Fori(0, CH // 2 - 1) as i:
                    for slot in range(2):
                        next_chunk(i * 2 + (first + 2 + slot), i * 2 + (2 + slot), slot)
                if first == 0:
                    for slot in range(2):
                        next_chunk(CH + slot, slot, slot)
            for j in range(NB // 2):
                sp.wait_ge(y_done, j + 1)
                sp.dma_start(out[j * 256:j * 256 + 256].rearrange("(b p) d -> p b d", p=128),
                             y_out[:, 2 * j:2 * j + 2]).then_inc(stored, 16)
            sp.wait_ge(stored, 16 * NB // 2)

        @block.gpsimd
        def _(pool):
            pool.memset(k_t[:, :, :, 0:WIN], 0.0).then_inc(zeroed, 1)
            pool.memset(zero_bf[:, :], 0.0).then_inc(zeroed, 1)
            pool.wait_ge(zeroed, 2)

            def lo_of_weights(count, slot, m):
                pool.wait_ge(w_hi_done, count)
                cols = slice(m * 256, m * 256 + 256)
                pool.tensor_tensor(out=w_lo[:, slot, :, cols], in0=w_raw[:, slot, :, cols],
                                   in1=w_hi[:, slot, :, cols].bitcast(f32), op=ALU.subtract) \
                    .then_inc(w_lo_done, 1)
                pool.wait_ge(w_lo_done, count)

            def lo_of_wo(count, slot):
                pool.wait_ge(wo_hi_done, count)
                pool.tensor_tensor(out=wo_lo[:, slot], in0=wo_raw[:, slot],
                                   in1=wo_hi[:, slot].bitcast(f32), op=ALU.subtract) \
                    .then_inc(wo_lo_done, 1)
                pool.wait_ge(wo_lo_done, count)

            def rotate_b(count, kept, free, t):
                cols = slice((t % 2) * 512, (t % 2) * 512 + 512)
                pool.wait_ge(fill_kept, kept)
                pool.wait_ge(rotated, free)
                pool.tensor_tensor(out=rot_b[0:64, t % 2], in0=qk_raw[64:128, t % 4],
                                   in1=sin_sb[64:128, cols], op=ALU.mult).then_inc(rot_b_half, 1)
                pool.wait_ge(rot_b_half, count)
                pool.tensor_tensor(out=rot_b[64:128, t % 2], in0=qk_raw[0:64, t % 4],
                                   in1=sin_sb[0:64, cols], op=ALU.mult).then_inc(rot_b_done, 1)
                pool.wait_ge(rot_b_done, count)

            for m in range(3):
                lo_of_weights(m + 1, 0, m)
            pool.wait_ge(ld_tab, 64)
            for t in range(8):
                rotate_b(t + 1, AHEAD.index(("Q", t)) + 3, t + 3, t)
            pool.wait_ge(mod_ready, 1)
            pool.memset(v_off[0:64, :, 0, :], 0.0).then_inc(zeroed, 1)
            pool.wait_ge(zeroed, 3)
            lo_of_wo(1, 0)
            for m in range(3):
                lo_of_weights(m + 4, 1, m)

            def step(p, slot, half, order, at):
                for kind, n in order:
                    if kind == "QB":
                        rotate_b(p * 8 + (9 + n), fill_no(p, at["Q", n] + 3), p * 8 + (11 + n), n)
                    if kind == "GL":
                        lo_of_weights(p * 3 + (7 + n), slot, n)
                    if kind == "PL":
                        lo_of_wo(p + 2, 1 - slot)

            steps(pool, POOL_STEP, step)

            def lo_of_up(count, slot):
                pool.wait_ge(up_w_hi, count)
                pool.tensor_tensor(out=w_lo[:, slot, 0, 0:UPW], in0=w_raw[:, slot, 0, 0:UPW],
                                   in1=w_hi[:, slot, 0, 0:UPW].bitcast(f32), op=ALU.subtract) \
                    .then_inc(up_w_lo, 1)
                pool.wait_ge(up_w_lo, count)

            def lo_of_down(count, slot):
                pool.wait_ge(down_w_hi, count)
                pool.tensor_tensor(out=wo_lo[:, slot, 0], in0=wo_raw[:, slot, 0],
                                   in1=wo_hi[:, slot, 0].bitcast(f32), op=ALU.subtract) \
                    .then_inc(down_w_lo, 1)
                pool.wait_ge(down_w_lo, count)

            for slot in range(2):
                lo_of_up(1 + slot, slot)
            with pool.Fori(0, CH - 1) as i:
                for slot in range(2):
                    lo_of_up(i * 2 + (3 + slot), slot)
                    lo_of_down(i * 2 + (1 + slot), slot)
            for slot in range(2):
                lo_of_down(2 * CH - 1 + slot, slot)

        @block.scalar
        def _(act):
            for dst, src in ((c_sb, c_col), (nw_sb, norm_w), (tie_sb, tie), (gw_sb, gate_w)):
                act.dma_start(dst, src).then_inc(ld_small, 16)
            for dst, src in ((aq_sb[:, :], a_qkv), (bo_sb[:, :], b_o)):
                act.dma_start(dst, src).then_inc(ld_lora, 16)
            for dst, src in ((id_sb[:, :], ident), (mask_sb[:, :, :], mask), (cos_sb[:, :], cos_t),
                             (sin_sb[:, :], sin_t)):
                act.dma_start(dst, src).then_inc(ld_tab, 16)
            act.sem_inc(exped, 2)
            act.sem_inc(fill_kept, 2)
            act.sem_inc(p_kept, 1)
            act.sem_inc(o_kept, 1)

            act.wait_ge(ld_small, 64)
            act.activation(sil_c, c_sb, ACT.Silu).then_inc(silu_c, 1)
            act.wait_ge(ld_tab, 64)
            act.activation(id_bf[:, :], id_sb[:, :], ACT.Copy).then_inc(id_done, 1)
            act.wait_ge(var_done, 1)
            act.activation(rstd, tmp8, ACT.Sqrt).then_inc(std_done, 1)
            for b in range(NB):
                act.wait_ge(h_done, 1 + b // 4)
                act.activation(sq_out[:, b], res[:, b], ACT.Square,
                               accum_out=ssq[:, b:b + 1]).then_inc(squared, 1)
            def keep(number, view, dst, scale):
                act.wait_ge(filled, number)
                act.activation(dst, view, ACT.Copy, scale=scale).then_inc(fill_kept, 1)

            def keep_projection(number, view, t, free):
                act.wait_ge(rotated, free)
                keep(number, view, qk_raw[:, t % 4], SCALE if t < 4 else 1.0)

            def keep_values(number, view, v, slot):
                keep(number, view,
                     v_sb[:, slot, 2 * v:2 * v + 2].rearrange("p b d -> p (b d)"), 1.0)

            def hi_of_weights(count, slot, m):
                act.wait_ge(folded, count)
                cols = slice(m * 256, m * 256 + 256)
                act.activation(w_hi[:, slot, :, cols], w_raw[:, slot, :, cols], ACT.Copy) \
                    .then_inc(w_hi_done, 1)

            def hi_of_wo(count, slot):
                act.wait_ge(folo_done, count)
                act.activation(wo_hi[:, slot], wo_raw[:, slot], ACT.Copy).then_inc(wo_hi_done, 1)

            for m in range(3):
                if m == 2:
                    act.wait_ge(folded, 1)
                keep(m + 1, fill_bank(m - FILLS_AHEAD), fold_tmp[:, m % 2], LORA_SCALE)
            act.wait_ge(ms_done, 1)
            act.activation(rstd, tmp8, ACT.Sqrt).then_inc(rms_done, 1)
            for m in range(3):
                hi_of_weights(m + 1, 0, m)
            for n in range(4):
                k, half = n % 2, n // 2
                act.wait_ge(h_turned, n + 1)
                act.activation(hi_t[:, k, half * 512:half * 512 + 512], bank[2 + n][:, :],
                               ACT.Identity, scale=nw_sb[:, k:k + 1]).then_inc(h_hi, 1)
            act.wait_ge(squared, NB)
            for j, (kind, n) in enumerate(AHEAD[3:], 3):
                view = fill_bank(j - FILLS_AHEAD)
                if kind == "Q":
                    keep_projection(j + 1, view, n, n + 1)
                if kind == "V":
                    keep_values(j + 1, view, n, 0)
                if kind == "P":
                    act.wait_ge(folded, 2)
                    keep(j + 1, view, fold_tmp[:, 1], LORA_SCALE)
                    hi_of_wo(1, 0)
                if kind == "G1":
                    if n == 1:
                        act.wait_ge(folo_done, 1)
                    else:
                        act.wait_ge(folded, 3 + n // 2)
                    keep(j + 1, view, fold_tmp[:, n % 2], LORA_SCALE)
            for m in range(3):
                hi_of_weights(m + 4, 1, m)

            def step(p, slot, half, order, at):
                if at:
                    act.wait_ge(scored, p * 4 + 1)
                for kind, n in order:
                    unit = p * 4 + n
                    if kind in FILL_KINDS:
                        j = at[kind, n]
                        number, view = fill_no(p, j + 1), fill_bank(j)
                    if kind == "Q":
                        keep_projection(number, view, n, p * 8 + (9 + n))
                    if kind == "V":
                        keep_values(number, view, n, 1 - slot)
                    if kind == "P":
                        act.wait_ge(folded, p * 3 + 5)
                        keep(number, view, fold_tmp[:, 1], LORA_SCALE)
                    if kind == "PH":
                        hi_of_wo(p + 2, 1 - slot)
                    if kind == "G":
                        if n == 1:
                            act.wait_ge(folo_done, p + 2)
                        else:
                            act.wait_ge(folded, p * 3 + (6 + n // 2))
                        keep(number, view, fold_tmp[:, n % 2], LORA_SCALE)
                    if kind == "GH":
                        hi_of_weights(p * 3 + (7 + n), slot, n)
                    if kind == "E":
                        act.wait_ge(maxed, unit + 1)
                        for b in range(4):
                            last = act.activation(probs[:, n % 2, b * 128:b * 128 + 128],
                                                  S_BANK[n % 2][:, b * 128:b * 128 + 128], ACT.Exp,
                                                  bias=neg_max[:, n % 2, b:b + 1],
                                                  accum_out=row_sum[:, n % 2, b:b + 1])
                        last.then_inc(exped, 1)
                    if kind == "T":
                        act.wait_ge(p_turned, unit + 1)
                        act.activation(probs_t[:, n % 2], PT_BANK[:, :], ACT.Copy).then_inc(p_kept, 1)
                    if kind == "O":
                        act.wait_ge(o_ready, unit + 1)
                        act.wait_ge(summed, unit + 1)
                        for b in range(4):
                            last = act.activation(o_norm[:, n % 2, b * 128:b * 128 + 128],
                                                  O_BANK[:, b * 128:b * 128 + 128], ACT.Identity,
                                                  scale=row_inv[:, n % 2, b:b + 1])
                        last.then_inc(o_kept, 1)
                    if kind == "X":
                        act.wait_ge(o_turned, unit + 1)
                        act.activation(o_hi[:, n % 2], OT_BANK[:, :], ACT.Copy).then_inc(oh_kept, 1)

            steps(act, ACT_STEP, step)

            def hi_of_up(count, slot):
                act.wait_ge(ld_up[slot], count)
                act.activation(w_hi[:, slot, 0, 0:UPW], w_raw[:, slot, 0, 0:UPW], ACT.Copy) \
                    .then_inc(up_w_hi, 1)

            def hi_of_down(count, slot):
                act.wait_ge(ld_down[slot], count)
                act.activation(wo_hi[:, slot, 0], wo_raw[:, slot, 0], ACT.Copy) \
                    .then_inc(down_w_hi, 1)

            for slot in range(2):
                hi_of_up(16, slot)
            act.wait_ge(var_done, 2)
            act.activation(rstd, tmp8, ACT.Sqrt).then_inc(std_done, 1)
            for n in range(4):
                k, half = n % 2, n // 2
                cols = slice(half * 512, half * 512 + 512)
                act.wait_ge(z_turned, n + 1)
                act.activation(h2_t[:, k, cols], bank[2 + n][:, :], ACT.Identity,
                               bias=mod_c[:, 0, k:k + 1], scale=mod_c[:, 1, k:k + 1]) \
                    .then_inc(z_kept, 1)
                act.activation(hi_t[:, k, cols], bank[2 + n][:, :], ACT.Identity,
                               bias=mod_c[:, 0, k:k + 1], scale=mod_c[:, 1, k:k + 1]) \
                    .then_inc(z_hi, 1)
            act.wait_ge(lg_done, 1)
            act.activation(sc, lg, ACT.Exp).then_inc(lg_exp, 1)
            act.wait_ge(gates_done, 1)
            act.activation(g_hi, t64, ACT.Copy).then_inc(g_hi_done, 1)
            for n in range(2):
                act.wait_ge(g_turned, n + 1)
                act.activation(gate_t[:, n], FILL_BANK[n][0:GK, :], ACT.Copy) \
                    .then_inc(gates_kept, 1)

            def chunk(c, slot, i, more, free):
                act.wait_ge(up_ready, c + 1)
                act.activation(qk_raw[:, slot], bank[2 + slot][:, :], ACT.Silu) \
                    .then_inc(silu_done, 1)
                if more:
                    hi_of_up(i * 16 + 32, slot)
                act.wait_ge(act_done, c + 1)
                if free:
                    act.wait_ge(down_done, c - 1)
                act.activation(o_hi[:, slot], probs[:, slot], ACT.Copy).then_inc(act_hi, 1)
                hi_of_down(i * 16 + 16, slot)

            for slot in range(2):
                chunk(slot, slot, 0, True, False)
            with act.Fori(1, CH - 1) as i:
                for slot in range(2):
                    chunk(i * 2 + slot, slot, i, True, True)
            for slot in range(2):
                chunk(2 * CH - 2 + slot, slot, CH - 1, False, True)

        @block.vector
        def _(dve):
            dve.sem_inc(ol_kept, 1)
            dve.sem_inc(w_added, 1)
            dve.sem_inc(rotated, 4)

            def mean_and_variance(base):
                for b in range(NB):
                    dve.bn_stats(stats[:, b], x_sb[:, b]).then_inc(stats_done, 1)
                dve.wait_ge(stats_done, base + NB)
                for b in range(NB):
                    dve.bn_aggr(mean_var[:, b], stats[:, b]).then_inc(stats_done, 1)
                dve.wait_ge(stats_done, base + 2 * NB)
                dve.tensor_scalar(out=tmp8, in0=mean_var[:, :, 1], scalar1=LN_EPS, scalar2=None,
                                  op0=ALU.add).then_inc(var_done, 1)

            def normalise(dst, count, done):
                dve.wait_ge(std_done, count)
                dve.reciprocal(rstd, rstd).then_inc(rstd_done, 1)
                dve.wait_ge(rstd_done, count)
                for b in range(NB):
                    dve.tensor_scalar(out=dst[:, b], in0=x_sb[:, b],
                                      scalar1=mean_var[:, b, 0:1], scalar2=rstd[:, b:b + 1],
                                      op0=ALU.subtract, op1=ALU.mult).then_inc(done, 1)

            def per_column(rows, row, n):
                return rows[:, row:row + 1, :].broadcast_to([128, n, D])

            dve.wait_ge(silu_c, 1)
            dve.tensor_copy(c_rep, sil_c.rearrange("p (k o) -> p k o", o=1)
                            .broadcast_to([128, KD, 128])).then_inc(c_spread, 1)
            dve.wait_ge(ld_x, 16)
            mean_and_variance(0)
            normalise(res, 1, x_normed)
            dve.wait_ge(mod_ready, 1)
            gates = mod_b[:, :].rearrange("p a d -> p (a d)")
            dve.tensor_copy(mod_a[:, 0], bank[0][:, 0:D])
            dve.tensor_scalar(out=mod_a[:, 1], in0=bank[0][:, D:2 * D], scalar1=1.0, scalar2=None,
                              op0=ALU.add)
            dve.tensor_scalar(out=sgn_g, in0=bank[1][:, :], scalar1=0.0, scalar2=2.0,
                              op0=ALU.is_ge, op1=ALU.mult).then_inc(mod_kept, 1)
            dve.wait_ge(mod_kept, 1)
            dve.scalar_tensor_tensor(out=gates, in0=sgn_g, scalar=-1.0, in1=bank[1][:, :],
                                     op0=ALU.add, op1=ALU.mult).then_inc(mod_kept, 1)
            dve.wait_ge(mod_kept, 2)
            dve.tensor_scalar(out=gates, in0=gates, scalar1=0.25, scalar2=None,
                              op0=ALU.max).then_inc(mod_kept, 1)
            dve.tensor_copy(mod_c[:, 0], bank[2][:, 0:KD])
            dve.tensor_scalar(out=mod_c[:, 1], in0=bank[2][:, KD:2 * KD], scalar1=1.0, scalar2=None,
                              op0=ALU.add)
            dve.wait_ge(mod_kept, 3)
            dve.scalar_tensor_tensor(out=gates, in0=sgn_g, scalar=-1.0, in1=gates, op0=ALU.add,
                                     op1=ALU.mult).then_inc(mod_kept, 1)
            dve.wait_ge(mod_kept, 4)
            for half in range(2):
                view = res[:, 4 * half:4 * half + 4]
                dve.wait_ge(x_normed, 4 * half + 4)
                dve.tensor_tensor(out=view, in0=view, in1=per_column(mod_a, 1, 4), op=ALU.mult) \
                    .then_inc(mod_kept, 1)
                dve.wait_ge(mod_kept, 5 + half)
                dve.tensor_tensor(out=view, in0=view, in1=per_column(mod_a, 0, 4), op=ALU.add) \
                    .then_inc(h_done, 1)

            def fold(kept, slot, m):
                dve.wait_ge(fill_kept, kept)
                view = w_raw[:, slot, :, m * 256:m * 256 + 256]
                dve.tensor_tensor(out=view,
                                  in0=fold_tmp[:, m % 2].rearrange("p (k n) -> p k n", k=KD),
                                  in1=view, op=ALU.add).then_inc(folded, 1)

            def fold_wo(kept, slot):
                dve.wait_ge(fill_kept, kept)
                view = wo_raw[:, slot]
                dve.tensor_tensor(out=view, in0=fold_tmp[:, 1].rearrange("p (h n) -> p h n", h=2),
                                  in1=view, op=ALU.add).then_inc(folo_done, 1)

            def rotate_a(kept, free, t):
                dve.wait_ge(fill_kept, kept)
                dve.wait_ge(rotated, free)
                dve.tensor_tensor(out=rot_a[:, t % 2], in0=qk_raw[:, t % 4],
                                  in1=cos_sb[:, (t % 2) * 512:(t % 2) * 512 + 512], op=ALU.mult) \
                    .then_inc(rot_a_done, 1)

            def rotate(count, t, slot):
                dve.wait_ge(rot_a_done, count)
                dve.wait_ge(rot_b_done, count)
                dve.tensor_tensor(out=place(t, slot), in0=rot_a[:, t % 2], in1=rot_b[:, t % 2],
                                  op=ALU.add).then_inc(rotated, 1)

            for m in range(3):
                fold(m + 3, 0, m)
            dve.wait_ge(squared, NB)
            dve.tensor_scalar(out=tmp8, in0=ssq, scalar1=1.0 / D, scalar2=RMS_EPS, op0=ALU.mult,
                              op1=ALU.add).then_inc(ms_done, 1)
            dve.wait_ge(rms_done, 1)
            dve.reciprocal(rstd, rstd).then_inc(ms_done, 1)
            dve.wait_ge(ms_done, 2)
            for b in range(NB):
                dve.tensor_scalar(out=h_norm[:, b], in0=res[:, b], scalar1=rstd[:, b:b + 1],
                                  scalar2=None, op0=ALU.mult).then_inc(h_normed, 1)
            for n in range(4):
                k, half = n % 2, n // 2
                cols = slice(half * 512, half * 512 + 512)
                dve.wait_ge(h_hi, n + 1)
                dve.scalar_tensor_tensor(out=lo_t[:, k, cols], in0=bank[2 + n][:, :],
                                         scalar=nw_sb[:, k:k + 1],
                                         in1=hi_t[:, k, cols].bitcast(f32), op0=ALU.mult,
                                         op1=ALU.subtract).then_inc(h_lo, 1)
            dve.wait_ge(ld_tab, 64)
            for t in range(8):
                if t >= 2:
                    rotate(t - 1, t - 2, 0)
                rotate_a(AHEAD.index(("Q", t)) + 3, t + 3, t)
            rotate(7, 6, 0)
            rotate(8, 7, 0)
            dve.wait_ge(ld_wo[0], 32)
            fold_wo(AHEAD.index(("P", 0)) + 3, 0)
            for m in range(3):
                fold(AHEAD.index(("G1", m)) + 3, 1, m)

            def step(p, slot, half, order, at):
                if at:
                    dve.wait_ge(scored, p * 4 + 1)
                for kind, n in order:
                    unit = p * 4 + n
                    if kind == "M":
                        dve.wait_ge(scored, unit + 1)
                        dve.tensor_reduce(out=neg_max[:, n % 2],
                                          in_=S_BANK[n % 2][:, :].rearrange("p (b k) -> p b k", b=4),
                                          axis=AX.X, op=ALU.max, negate=True).then_inc(maxed, 1)
                    if kind == "N":
                        dve.wait_ge(exped, unit + 3)
                        dve.reciprocal(row_inv[:, n % 2], row_sum[:, n % 2]).then_inc(summed, 1)
                    if kind == "XL":
                        dve.wait_ge(oh_kept, unit + 1)
                        dve.tensor_tensor(out=o_lo[:, n % 2], in0=OT_BANK[:, :],
                                          in1=o_hi[:, n % 2].bitcast(f32), op=ALU.subtract) \
                            .then_inc(ol_kept, 1)
                    if kind == "W":
                        dve.wait_ge(w_ready, unit + 1)
                        dve.wait_ge(w_added, unit + 1)
                        view = res[:, 2 * n:2 * n + 2].rearrange("p b d -> p (b d)")
                        dve.tensor_tensor(out=view, in0=W_BANK[:, :], in1=view, op=ALU.add) \
                            .then_inc(w_added, 1)
                    if kind == "QA":
                        rotate_a(fill_no(p, at["Q", n] + 3), p * 8 + (11 + n), n)
                    if kind == "QR":
                        rotate(p * 8 + (9 + n), n, 1 - slot)
                    if kind == "P":
                        fold_wo(fill_no(p, at["P", 0] + 3), 1 - slot)
                    if kind == "G":
                        fold(fill_no(p, at["G", n] + 3), slot, n)

            steps(dve, DVE_STEP, step)

            dve.wait_ge(w_added, 4 * PAIRS + 1)
            for half in range(2):
                view, to = res[:, 4 * half:4 * half + 4], x_sb[:, 4 * half:4 * half + 4]
                dve.tensor_tensor(out=view, in0=view, in1=per_column(mod_b, 0, 4), op=ALU.mult) \
                    .then_inc(x1_done, 1)
                dve.wait_ge(x1_done, 2 * half + 1)
                dve.tensor_tensor(out=to, in0=to, in1=view, op=ALU.add).then_inc(x1_done, 1)
            dve.wait_ge(x1_done, 4)
            mean_and_variance(2 * NB)
            normalise(z_sb, 2, z_done)
            for n in range(4):
                k, half = n % 2, n // 2
                cols = slice(half * 512, half * 512 + 512)
                dve.wait_ge(z_hi, n + 1)
                dve.tensor_tensor(out=lo_t[:, k, cols], in0=h2_t[:, k, cols],
                                  in1=hi_t[:, k, cols].bitcast(f32), op=ALU.subtract) \
                    .then_inc(z_lo, 1)

            def by_block(view):
                return view.rearrange("p (b e) -> p b e", e=E)

            def spread(view):
                return view.rearrange("p (b o) -> p b o", o=1).broadcast_to([128, NB, E])

            done = [0]

            def then_wait(ins):
                done[0] += 1
                ins.then_inc(gating, 1)
                dve.wait_ge(gating, done[0])

            dve.wait_ge(logits, 1)
            then_wait(dve.tensor_reduce(out=m8, in_=by_block(bank[0][:, 0:NB * E]), axis=AX.X,
                                        op=ALU.max))
            dve.tensor_tensor(out=by_block(lg), in0=by_block(bank[0][:, 0:NB * E]), in1=spread(m8),
                              op=ALU.subtract).then_inc(lg_done, 1)
            dve.wait_ge(lg_exp, 1)
            then_wait(dve.tensor_reduce(out=m8, in_=by_block(sc), axis=AX.X, op=ALU.add))
            then_wait(dve.reciprocal(m8, m8))
            then_wait(dve.tensor_tensor(out=by_block(sc), in0=by_block(sc), in1=spread(m8),
                                        op=ALU.mult))
            for left, one_hot in ((sc, oh1), (lg, oh2)):
                then_wait(dve.tensor_reduce(out=m8, in_=by_block(left), axis=AX.X, op=ALU.max))
                then_wait(dve.tensor_tensor(out=by_block(t64), in0=by_block(left), in1=spread(m8),
                                            op=ALU.is_equal))
                then_wait(dve.tensor_tensor(out=t64, in0=t64, in1=tie_sb, op=ALU.mult))
                then_wait(dve.tensor_reduce(out=m8, in_=by_block(t64), axis=AX.X, op=ALU.max))
                then_wait(dve.tensor_tensor(out=by_block(one_hot), in0=by_block(t64),
                                            in1=spread(m8), op=ALU.is_equal))
                if left is sc:
                    then_wait(dve.scalar_tensor_tensor(out=lg, in0=oh1, scalar=-2.0, in1=sc,
                                                       op0=ALU.mult, op1=ALU.add))
            then_wait(dve.tensor_tensor(out=oh1, in0=oh1, in1=oh2, op=ALU.add))
            then_wait(dve.tensor_tensor(out=sc, in0=sc, in1=oh1, op=ALU.mult))
            then_wait(dve.tensor_reduce(out=m8, in_=by_block(sc), axis=AX.X, op=ALU.add))
            then_wait(dve.reciprocal(m8, m8))
            dve.tensor_tensor(out=by_block(t64), in0=by_block(sc), in1=spread(m8), op=ALU.mult) \
                .then_inc(gates_done, 1)
            dve.wait_ge(g_hi_done, 1)
            high = by_block(g_hi.bitcast(f32))
            dve.tensor_copy(g_cat[:, :, 0:E], high)
            dve.tensor_tensor(out=g_cat[:, :, E:2 * E], in0=by_block(t64), in1=high,
                              op=ALU.subtract)
            dve.memset(g_cat[:, :, 2 * E:GK], 1.0).then_inc(gates_done, 1)

            def chunk(c, slot):
                dve.wait_ge(silu_done, c + 1)
                dve.tensor_tensor(out=rot_a[:, slot], in0=qk_raw[:, slot], in1=bank[4 + slot][:, :],
                                  op=ALU.mult).then_inc(mul_done, 1)
                dve.wait_ge(mul_done, c + 1)
                dve.tensor_tensor(out=probs[:, slot], in0=rot_a[:, slot], in1=bank[6 + slot][:, :],
                                  op=ALU.mult).then_inc(act_done, 1)
                dve.wait_ge(act_hi, c + 1)
                dve.tensor_tensor(out=o_lo[:, slot], in0=probs[:, slot],
                                  in1=o_hi[:, slot].bitcast(f32), op=ALU.subtract) \
                    .then_inc(act_lo, 1)

            def output(half):
                dve.wait_ge(down_done, CH * (half + 1))
                for j in range(2):
                    b = 4 * half + 2 * j
                    dve.tensor_tensor(out=y_out[:, b:b + 2],
                                      in0=bank[j][:, :].rearrange("p (b d) -> p b d", b=2),
                                      in1=per_column(mod_b, 1, 2), op=ALU.mult).then_inc(y_scaled, 1)
                for j in range(2):
                    b = 4 * half + 2 * j
                    dve.wait_ge(y_scaled, 2 * half + 1 + j)
                    dve.tensor_tensor(out=y_out[:, b:b + 2], in0=y_out[:, b:b + 2],
                                      in1=x_sb[:, b:b + 2], op=ALU.add).then_inc(y_done, 1)

            with dve.Fori(0, CH // 2 + 1) as i:
                for slot in range(2):
                    chunk(i * 2 + slot, slot)
            output(0)
            with dve.Fori(CH // 2 + 1, CH) as i:
                for slot in range(2):
                    chunk(i * 2 + slot, slot)
            output(1)

        @block.tensor
        def _(pe):
            def three(dst, lhs, rhs, contraction, **more):
                n = 0
                for at in contraction:
                    for a, b in ((0, 0), (0, 1), (1, 0)):
                        n += 1
                        last = pe.matmul(dst, lhs(a, at), rhs(b, at), start=n == 1,
                                         stop=n == 3 * len(contraction), **more)
                return last

            t_parts, w_parts, wo_parts, o_parts = (
                (hi_t, lo_t), (w_hi, w_lo), (wo_hi, wo_lo), (o_hi, o_lo))

            pe.wait_ge(ld_mod, 16)
            pe.wait_ge(c_spread, 1)
            for dst, col, n in ((bank[0][:, :], 0, 512), (bank[1][:, 0:D], 2 * D, D),
                                (bank[1][:, D:2 * D], 5 * D, D)):
                for k in range(KD):
                    pe.matmul(dst, c_rep[:, k], wm_sb[:, k, col:col + n], start=k == 0,
                              stop=k == KD - 1)
            for j in range(2 * KD):
                col = 3 * D + j * 128
                for k in range(KD):
                    last = pe.matmul(bank[2][:, j:j + 1], wm_sb[:, k, col:col + 128],
                                     sil_c[:, k:k + 1], start=k == 0, stop=k == KD - 1)
            last.then_inc(mod_ready, 1)

            def lora(j, number, slot, m, loaded):
                pe.wait_ge(ld_raw[slot], loaded)
                pe.wait_ge(fill_kept, number)
                for k in range(KD):
                    last = pe.matmul(fill_bank(j)[:, k * 256:k * 256 + 256],
                                     aq_sb[32 * m:32 * m + R, k * 128:k * 128 + 128],
                                     bq_sb[32 * m:32 * m + R, slot], start=True, stop=True)
                last.then_inc(filled, 1)

            def lora_wo(j, number, slot, loaded):
                pe.wait_ge(ld_wo[slot], loaded)
                pe.wait_ge(fill_kept, number)
                for h in range(2):
                    last = pe.matmul(fill_bank(j)[:, h * 256:h * 256 + 256],
                                     ao_sb[:, slot, h * 128:h * 128 + 128], bo_sb[:, :],
                                     start=True, stop=True)
                last.then_inc(filled, 1)

            def project(j, number, slot, t):
                head, half = t // 2 % 2, t % 2
                col = (t // 4) * 256 + head * 128
                pe.wait_ge(fill_kept, number)
                three(fill_bank(j), lambda a, k: w_parts[a][:, slot, k, col:col + 128],
                      lambda b, k: t_parts[b][:, k, half * 512:half * 512 + 512], range(KD)) \
                    .then_inc(filled, 1)

            def values(j, number, slot, v):
                pe.wait_ge(fill_kept, number)
                for i in range(2):
                    at = (2 * v + i) * 128
                    last = three(fill_bank(j)[:, i * 256:i * 256 + 256],
                                 lambda a, k: t_parts[a][:, k, at:at + 128],
                                 lambda b, k: w_parts[b][:, slot, k, 512:768], range(KD))
                last.then_inc(filled, 1)

            pe.wait_ge(ld_lora, 32)
            for m in range(3):
                lora(m - FILLS_AHEAD, m + 1, 0, m, 32)
            pe.wait_ge(mod_kept, 4)
            pe.wait_ge(ld_tab, 64)
            for n in range(4):
                k, half = n % 2, n // 2
                pe.wait_ge(h_normed, 4 * half + 4)
                for b in range(4):
                    last = pe.transpose(bank[2 + n][:, b * 128:b * 128 + 128],
                                        h_norm[:, 4 * half + b, k * 128:k * 128 + 128], id_sb[:, :])
                last.then_inc(h_turned, 1)
            pe.wait_ge(w_lo_done, 3)
            pe.wait_ge(h_lo, 4)
            for j, (kind, n) in enumerate(AHEAD[3:], 3):
                at = j - FILLS_AHEAD
                if kind == "Q":
                    project(at, j + 1, 0, n)
                if kind == "V":
                    values(at, j + 1, 0, n)
                if kind == "P":
                    lora_wo(at, j + 1, 0, 32)
                if kind == "G1":
                    lora(at, j + 1, 1, n, 32)
            pe.wait_ge(zeroed, 3)
            pe.wait_ge(id_done, 1)

            def step(p, slot, half, order, at):
                for kind, n in order:
                    unit, group, head = p * 4 + n, n // 2, n % 2
                    if kind in FILL_KINDS:
                        j = at[kind, n]
                        number = fill_no(p, j + 1)
                    if kind == "S":
                        if n == 0:
                            pe.wait_ge(rotated, p * 8 + 12)
                        pe.wait_ge(exped, unit + 1)
                        pe.matmul(S_BANK[n % 2][:, :], id_bf[:, :], mask_sb[:, group], start=True,
                                  stop=False, skip_group_check=True)
                        for b in range(4):
                            for c in range(2):
                                q0 = (group * 8 + 2 * b + c) * 64
                                last = pe.matmul(
                                    S_BANK[n % 2][64 * c:64 * c + 64, b * 128:b * 128 + 128],
                                    q_t[:, slot, head, q0:q0 + 64],
                                    k_t[:, slot, head, q0:q0 + 128], start=False, stop=True,
                                    skip_group_check=True)
                        last.then_inc(scored, 1)
                    if kind == "T":
                        pe.wait_ge(exped, unit + 3)
                        pe.wait_ge(p_kept, unit + 1)
                        for b in range(4):
                            last = pe.transpose(PT_BANK[:, b * 128:b * 128 + 128],
                                                probs[:, n % 2, b * 128:b * 128 + 128], id_sb[:, :])
                        last.then_inc(p_turned, 1)
                    if kind == "O":
                        if n == 0:
                            pe.wait_ge(v_moved[slot], half * 32 + 32)
                        pe.wait_ge(p_kept, unit + 2)
                        pe.wait_ge(o_kept, unit + 1)
                        for b in range(4):
                            for c, source in enumerate((v_off, v_sb)):
                                q0 = b * 128 + 64 * c
                                last = pe.matmul(
                                    O_BANK[64 * c:64 * c + 64, b * 128:b * 128 + 128],
                                    probs_t[:, n % 2, q0:q0 + 64],
                                    source[:, slot, group * 4 + b, head * 128:head * 128 + 128],
                                    start=True, stop=True)
                        last.then_inc(o_ready, 1)
                    if kind == "X":
                        pe.wait_ge(o_kept, unit + 2)
                        pe.wait_ge(ol_kept, unit + 1)
                        for b in range(4):
                            last = pe.transpose(OT_BANK[:, b * 128:b * 128 + 128],
                                                o_norm[:, n % 2, b * 128:b * 128 + 128],
                                                id_sb[:, :])
                        last.then_inc(o_turned, 1)
                    if kind == "W":
                        if n == 0:
                            pe.wait_ge(wo_lo_done, p + 1)
                        pe.wait_ge(ol_kept, p * 4 + (2 * group + 3))
                        pe.wait_ge(w_added, unit + 1)
                        for i in range(2):
                            col = (2 * (n % 2) + i) * 128
                            last = three(W_BANK[:, i * 256:i * 256 + 256],
                                         lambda a, h: o_parts[a][:, h, col:col + 128],
                                         lambda b, h: wo_parts[b][:, slot, h], range(2))
                        last.then_inc(w_ready, 1)
                    if kind == "Q":
                        if n == 0:
                            pe.wait_ge(w_lo_done, p * 3 + 6)
                        project(j, number, 1 - slot, n)
                    if kind == "V":
                        values(j, number, 1 - slot, n)
                    if kind == "G":
                        lora(j, number, slot, n, half * 32 + 64)
                    if kind == "P":
                        lora_wo(j, number, 1 - slot, half * 32 + (32 + 32 * slot))

            steps(pe, PE_STEP, step)

            for n in range(4):
                k, half = n % 2, n // 2
                pe.wait_ge(z_done, 4 * half + 4)
                for b in range(4):
                    last = pe.transpose(bank[2 + n][:, b * 128:b * 128 + 128],
                                        z_sb[:, 4 * half + b, k * 128:k * 128 + 128], id_sb[:, :])
                last.then_inc(z_turned, 1)
            pe.wait_ge(z_kept, 4)
            for b in range(NB):
                for k in range(KD):
                    last = pe.matmul(bank[0][:, b * E:b * E + E], h2_t[:, k, b * 128:b * 128 + 128],
                                     gw_sb[:, k], start=k == 0, stop=k == KD - 1)
            last.then_inc(logits, 1)
            pe.wait_ge(gates_done, 2)
            for n in range(2):
                for b in range(4):
                    last = pe.transpose(FILL_BANK[n][0:GK, b * 128:b * 128 + 128],
                                        g_cat[:, 4 * n + b], id_sb[:, :])
                last.then_inc(g_turned, 1)
            pe.wait_ge(z_lo, 4)
            pe.wait_ge(gates_kept, 2)

            def clear():
                for j in range(2):
                    pe.matmul(bank[j][:, :], zero_bf[:, :], mask_sb[:, 0], start=True,
                              stop=False, skip_group_check=True)

            def up(c, slot, half, free):
                cols = slice(half * 512, half * 512 + 512)
                pe.wait_ge(up_w_lo, c + 1)
                if free:
                    pe.wait_ge(act_done, c - 1)
                pe.matmul(bank[6 + slot][:, :], w_hi[0:GK, slot, 0, 512:UPW], gate_t[:, half],
                          start=True, stop=True)
                for m in range(2):
                    last = three(bank[2 + 2 * m + slot][:, :],
                                 lambda a, k: w_parts[a][:, slot, 0, m * 256 + k * 128:
                                                         m * 256 + k * 128 + 128],
                                 lambda b, k: t_parts[b][:, k, cols], range(KD))
                last.then_inc(up_ready, 1)

            def down(c, slot):
                pe.wait_ge(down_w_lo, c + 1)
                pe.wait_ge(act_lo, c + 1)
                for b in range(4):
                    dst = bank[b // 2][:, (b % 2) * 256:(b % 2) * 256 + 256]
                    for a, w in ((0, 0), (0, 1), (1, 0)):
                        last = pe.matmul(dst, o_parts[a][:, slot, b * 128:b * 128 + 128],
                                         wo_parts[w][:, slot, 0], start=False, stop=True,
                                         skip_group_check=True)
                last.then_inc(down_done, 1)

            clear()
            up(0, 0, 0, False)
            up(1, 1, 0, False)
            with pe.Fori(0, CH // 2 - 1) as i:
                for slot in range(2):
                    up(i * 2 + (slot + 2), slot, 0, True)
                    down(i * 2 + slot, slot)
            for slot in range(2):
                up(CH + slot, slot, 1, True)
                down(CH - 2 + slot, slot)
            pe.wait_ge(y_scaled, 2)
            clear()
            with pe.Fori(CH // 2, CH - 1) as i:
                for slot in range(2):
                    up(i * 2 + (slot + 2), slot, 1, True)
                    down(i * 2 + slot, slot)
            for slot in range(2):
                down(2 * CH - 2 + slot, slot)


def kernel(**inputs):
    import numpy as np
    import concourse.bacc as bacc
    from concourse.bass_utils import run_bass_kernel_spmd

    a = {k[3:]: np.asarray(v) for k, v in inputs.items()}
    f32 = np.float32

    theta = f32(1.0) / np.power(f32(10000.0), np.arange(DH // 2, dtype=f32) / f32(DH // 2))
    freqs = np.arange(T, dtype=f32)[:, None] * theta[None, :]
    cos_t = np.cos(np.concatenate([freqs, freqs], 1)).T
    sin = np.sin(freqs).T
    sin_t = np.concatenate([sin, -sin], 0)
    row, key = np.arange(64)[:, None], np.arange(128)[None, :]
    open_ = (key >= row + 1) & (key <= row + WIN)
    mask = np.zeros((2, 128, 4, 128), f32)
    for g in range(2):
        for c in range(2):
            for b in range(4):
                seen = open_ & (key >= WIN) if g == b == c == 0 else open_
                mask[g, 64 * c:64 * c + 64, b] = np.where(seen, 0.0, -1e30)
    from concourse import mybir as _mybir
    mask = mask.transpose(1, 0, 2, 3).reshape(128, 2, 512).astype(_mybir.dt.np(_mybir.dt.bfloat16))
    sel = np.zeros((CH, 128, 128), f32)
    for c in range(CH):
        for i in range(128):
            n = c * 128 + i
            for r in ((n // FI, E + n // FI) if n < E * FI else (2 * E,)):
                sel[c, r, i] = 1.0
    tie = np.tile(np.arange(E, 0, -1, dtype=f32), (128, NB))

    def by_pair(w):
        return w.reshape(PAIRS, 2 * DH, -1).transpose(0, 2, 1)

    w_qkv = np.concatenate([by_pair(a["attn_w" + m]) for m in "qkv"], 2)
    w_qkv = w_qkv.reshape(PAIRS, KD, 128, PW).transpose(0, 2, 1, 3)
    gap = 32 - R
    b_qkv = np.concatenate([np.pad(by_pair(a["attn_" + m + "B"]), ((0, 0), (0, gap), (0, 0)))
                            for m in "qkv"], 1)
    a_qkv = np.concatenate([np.pad(a["attn_" + m + "A"], ((0, gap), (0, 0))) for m in "qkv"])
    w_o = a["attn_wo"].T.reshape(PAIRS, 2, DH, D).transpose(0, 2, 1, 3)
    a_o = a["attn_oA"].reshape(R, PAIRS, 2 * DH).transpose(1, 0, 2)

    def chunks(experts, shared):
        w = np.concatenate([experts.transpose(1, 0, 2).reshape(D, E * FI), shared,
                            np.zeros((D, CH * 128 - (E + 2) * FI), f32)], 1)
        return w.reshape(KD, 128, CH, 128).transpose(2, 1, 0, 3).reshape(CH, 128, KD * 128)

    w_up = np.concatenate([chunks(a["ffn_w1"], a["ffn_sw1"]), chunks(a["ffn_w3"], a["ffn_sw3"]),
                           sel], 2)
    w_down = np.concatenate([a["ffn_w2"].reshape(E * FI, D), a["ffn_sw2"],
                             np.zeros((CH * 128 - (E + 2) * FI, D), f32)]).reshape(CH, 128, D)

    arrays = {
        "x": a["attn_x"].reshape(T, D), "cos_t": cos_t, "sin_t": sin_t, "mask": mask,
        "ident": np.eye(128, dtype=f32), "c_col": a["c"].reshape(KD, 128).T,
        "w_mod": a["wmod"].reshape(KD, 128, 6 * D).transpose(1, 0, 2),
        "norm_w": a["attn_norm_w"].reshape(KD, 128).T,
        "w_qkv": w_qkv, "b_qkv": b_qkv, "a_qkv": a_qkv, "w_o": w_o, "a_o": a_o,
        "b_o": a["attn_oB"].T,
        "gate_w": a["ffn_gate_w"].T.reshape(KD, 128, E).transpose(1, 0, 2),
        "w_up": w_up, "w_down": w_down, "tie": tie,
    }
    nc = bacc.Bacc("TRN2", target_bir_lowering=False, num_devices=1)
    args, given = {}, {}
    for name, array in arrays.items():
        array = np.ascontiguousarray(array)
        given[f"in_{name}"] = array
        args[name] = nc.dram_tensor(f"in_{name}", array.shape, mybir.dt.from_np(array.dtype),
                                    kind="ExternalInput").ap()
    args["out"] = nc.dram_tensor("out_y", (T, D), mybir.dt.float32, kind="ExternalOutput").ap()
    build(nc, **args)
    result = run_bass_kernel_spmd(nc, [given], core_ids=[0])
    return result.results[0]["out_y"].reshape(1, T, D)
```

```python
import concourse.bass as bass
from concourse import mybir
from contextlib import ExitStack

T = 1024
D = 256
KD = D // 128
H = 16
DH = 128
WIN = 64
R = 16
PAIRS = H // 2
PW = 3 * 2 * DH
NB = T // 128
E = 8
FI = 176
CH = 14
SHARED = 3
GK = 2 * E + 1
UPW = 5 * 128
SCALE = DH ** -0.5
LORA_SCALE = 1.0 / R
LN_EPS = 1e-5
RMS_EPS = 1e-6

PE_STEP = [("S", 0), ("Q", 0), ("S", 1), ("Q", 1), ("T", 0), ("V", 0), ("G", 0), ("O", 0),
           ("S", 2), ("Q", 2), ("T", 1), ("X", 0), ("V", 1), ("Q", 3), ("O", 1), ("S", 3),
           ("G", 1), ("Q", 4), ("T", 2), ("X", 1), ("V", 2), ("O", 2), ("Q", 5), ("W", 0),
           ("T", 3), ("G", 2), ("W", 1), ("X", 2), ("Q", 6), ("O", 3), ("Q", 7), ("X", 3),
           ("V", 3), ("W", 2), ("P", 0), ("W", 3)]
ACT_STEP = [("E", 0), ("Q", 0), ("E", 1), ("Q", 1), ("T", 0), ("V", 0), ("G", 0), ("O", 0),
            ("E", 2), ("Q", 2), ("GH", 0), ("T", 1), ("X", 0), ("V", 1), ("Q", 3), ("O", 1),
            ("G", 1), ("E", 3), ("Q", 4), ("T", 2), ("X", 1), ("GH", 1), ("V", 2), ("O", 2),
            ("Q", 5), ("T", 3), ("G", 2), ("X", 2), ("Q", 6), ("GH", 2), ("O", 3), ("Q", 7),
            ("X", 3), ("V", 3), ("P", 0), ("PH", 0)]
DVE_STEP = [("M", 0), ("QA", 0), ("M", 1), ("QA", 1), ("N", 0), ("G", 0), ("QR", 0), ("M", 2),
            ("QA", 2), ("XL", 0), ("N", 1), ("QR", 1), ("QA", 3), ("M", 3), ("G", 1), ("QR", 2),
            ("QA", 4), ("N", 2), ("XL", 1), ("W", 0), ("QR", 3), ("QA", 5), ("N", 3), ("G", 2),
            ("W", 1), ("XL", 2), ("QR", 4), ("QA", 6), ("QR", 5), ("QA", 7), ("XL", 3), ("W", 2),
            ("QR", 6), ("QR", 7), ("P", 0), ("W", 3)]
POOL_STEP = [("QB", 0), ("QB", 1), ("GL", 0), ("QB", 2), ("QB", 3), ("GL", 1), ("QB", 4),
             ("QB", 5), ("QB", 6), ("GL", 2), ("QB", 7), ("PL", 0)]
PE_LAST = [("S", 0), ("S", 1), ("T", 0), ("S", 2), ("O", 0), ("S", 3), ("T", 1), ("X", 0),
           ("O", 1), ("T", 2), ("X", 1), ("O", 2), ("W", 0), ("T", 3), ("W", 1), ("X", 2),
           ("O", 3), ("X", 3), ("W", 2), ("W", 3), ("Z", 0), ("Z", 1)]
ACT_LAST = [("E", 0), ("E", 1), ("T", 0), ("E", 2), ("O", 0), ("T", 1), ("E", 3), ("X", 0),
            ("O", 1), ("T", 2), ("X", 1), ("O", 2), ("T", 3), ("X", 2), ("O", 3), ("X", 3),
            ("U", 0), ("ZR", 0), ("U", 1), ("ZH", 0), ("ZH", 1)]
DVE_LAST = [("M", 0), ("M", 1), ("N", 0), ("M", 2), ("N", 1), ("M", 3), ("XL", 0), ("N", 2),
            ("XL", 1), ("N", 3), ("W", 0), ("W", 1), ("XL", 2), ("XL", 3), ("W", 2), ("ZX", 0),
            ("W", 3), ("ZN", 0), ("ZX", 1), ("ZL", 0), ("ZL", 1)]
FILL_KINDS = "QVGP"
FILL_AT = {e: j for j, e in enumerate(e for e in PE_STEP if e[0] in FILL_KINDS)}
FILL_AT_6 = {e: j for j, e in enumerate(e for e in FILL_AT if e[0] != "G")}
AHEAD = ([("G", m) for m in range(3)] + [("Q", t) for t in range(8)] + [("V", v) for v in range(4)]
         + [("P", 0)] + [("G1", m) for m in range(3)])
FILLS_AHEAD = len(AHEAD)
FILLS = len(FILL_AT)


def build(nc, x, cos_t, sin_t, mask, ident, c_col, w_mod, norm_w, w_qkv, b_qkv, a_qkv, w_o, a_o,
          b_o, gate_w, w_up, w_down, tie, out):
    f32, f32r, bf16 = mybir.dt.float32, mybir.dt.float32r, mybir.dt.bfloat16
    ALU, ACT, AX = mybir.AluOpType, mybir.ActivationFunctionType, mybir.AxisListType

    ctx = ExitStack()
    with ctx:
        def sb(name, shape, dt=f32):
            return ctx.enter_context(nc.sbuf_tensor(name, shape, dt))

        def sem(name):
            return ctx.enter_context(nc.semaphore(name))

        x_sb = sb("x_sb", [128, NB, D])
        res = sb("res", [128, NB, D])
        hi_t = sb("hi_t", [128, KD, T], f32r)
        lo_t = sb("lo_t", [128, KD, T], f32r)
        cos_sb = sb("cos_sb", [128, T])
        sin_sb = sb("sin_sb", [128, T])
        mask_sb = sb("mask_sb", [128, 2, 512], bf16)
        id_sb = sb("id_sb", [128, 128])
        id_bf = sb("id_bf", [128, 128], bf16)
        w_raw = sb("w_raw", [128, 2, KD, PW])
        w_hi = sb("w_hi", [128, 2, KD, PW], f32r)
        w_lo = sb("w_lo", [128, 2, KD, PW], f32r)
        bq_sb = sb("bq_sb", [96, 2, 2 * DH])
        aq_sb = sb("aq_sb", [96, D])
        wo_raw = sb("wo_raw", [128, 2, 2, D])
        wo_hi = sb("wo_hi", [128, 2, 2, D], f32r)
        wo_lo = sb("wo_lo", [128, 2, 2, D], f32r)
        ao_sb = sb("ao_sb", [R, 2, 2 * DH])
        bo_sb = sb("bo_sb", [R, D])
        q_t = sb("q_t", [128, 2, 2, T])
        k_t = sb("k_t", [128, 2, 2, WIN + T])
        v_sb = sb("v_sb", [128, 2, NB, 2 * DH])
        v_off = sb("v_off", [128, 2, NB, 2 * DH])
        fold_tmp = sb("fold_tmp", [128, 2, 512])
        qk_raw = sb("qk_raw", [128, 4, 512])
        rot_a = sb("rot_a", [128, 2, 512])
        rot_b = sb("rot_b", [128, 2, 512])
        probs = sb("probs", [128, 2, 512])
        probs_t = sb("probs_t", [128, 2, 512])
        o_norm = sb("o_norm", [128, 2, 512])
        o_hi = sb("o_hi", [128, 2, 512], f32r)
        o_lo = sb("o_lo", [128, 2, 512], f32r)
        neg_max = sb("neg_max", [128, 2, 4])
        row_sum = sb("row_sum", [128, 2, 4])
        row_inv = sb("row_inv", [128, 2, 4])
        mod_b = sb("mod_b", [128, 2, D])
        mod_c = sb("mod_c", [128, 2, KD])
        small = sb("small", [128, 512])
        zero_bf = sb("zero_bf", [128, 128], bf16)
        gate_t = w_hi[0:GK, :, 1, 0:512]
        g_hi = w_hi[:, 0, 1, 512:512 + NB * E]
        wm_sb = v_off[:, :, :, :].rearrange("p s b d -> p (s b d)")[:, 0:KD * 6 * D].rearrange(
            "p (k n) -> p k n", k=KD)
        c_rep = v_sb[:, 1, 0, 0:KD * 128].rearrange("p (k n) -> p k n", k=KD)
        sq_out = v_sb[:, 0, :, :]
        sgn_g = v_sb[:, 1, 2:4, :].rearrange("p b d -> p (b d)")
        mod_a = v_sb[:, 1, 4:6, :]
        h_norm = q_t[:, 0, :, :].rearrange("p h t -> p (h t)").rearrange("p (b d) -> p b d", d=D)
        stats = small[:, 0:6 * NB].rearrange("p (b s) -> p b s", s=6)
        mean_var = small[:, 48:48 + 2 * NB].rearrange("p (b s) -> p b s", s=2)
        rstd = small[:, 64:72]
        tmp8 = small[:, 72:80]
        nw_sb = small[:, 80:82]
        c_sb = small[:, 82:84]
        sil_c = small[:, 86:88]
        ssq = small[:, 88:96]
        lg = small[:, 96:160]
        sc = small[:, 160:224]
        oh1 = small[:, 224:288]
        oh2 = small[:, 288:352]
        t64 = small[:, 352:416]
        tie_sb = small[:, 416:480]
        m8 = small[:, 480:488]
        g_cat = q_t[:, 1, 0, 0:NB * GK].rearrange("p (b g) -> p b g", g=GK)
        h2_t = k_t[:, :, :, 0:T].rearrange("p s h t -> p (s h) t")[:, 0:KD, :]
        gw_sb = small[:, 488:504].rearrange("p (k e) -> p k e", k=KD)
        z_sb = q_t[:, 0, :, :].rearrange("p h t -> p (h t)").rearrange("p (b d) -> p b d", d=D)
        y_out = v_sb[:, 0, :, :]

        bank = [ctx.enter_context(nc.psum_tensor(f"bank{i}", [128, 512], f32)) for i in range(8)]
        S_BANK, PT_BANK, O_BANK, OT_BANK, W_BANK = bank[0:2], bank[2], bank[3], bank[4], bank[5]
        FILL_BANK = bank[6:8]
        LG_BANK = bank[0]

        ld_x, ld_tab, ld_mod, ld_small, ld_lora = (
            sem("ld_x"), sem("ld_tab"), sem("ld_mod"), sem("ld_small"), sem("ld_lora"))
        ld_raw = [sem("ld_raw0"), sem("ld_raw1")]
        ld_wo = [sem("ld_wo0"), sem("ld_wo1")]
        ld_up = [sem(f"ld_up{i}") for i in range(4)]
        ld_down = [sem(f"ld_down{i}") for i in range(4)]
        v_moved = [sem("v_moved0"), sem("v_moved1")]
        zeroed, silu_c, c_spread, mod_ready, mod_kept = (
            sem("zeroed"), sem("silu_c"), sem("c_spread"), sem("mod_ready"), sem("mod_kept"))
        stats_done, var_done, std_done, rstd_done = (
            sem("stats_done"), sem("var_done"), sem("std_done"), sem("rstd_done"))
        h_done, squared, ms_done, rms_done, h_normed = (
            sem("h_done"), sem("squared"), sem("ms_done"), sem("rms_done"), sem("h_normed"))
        h_turned, h_hi, h_lo, id_done = sem("h_turned"), sem("h_hi"), sem("h_lo"), sem("id_done")
        x_normed, rot_b_half = sem("x_normed"), sem("rot_b_half")
        scored, maxed, exped = sem("scored"), sem("maxed"), sem("exped")
        p_turned, p_kept, summed = sem("p_turned"), sem("p_kept"), sem("summed")
        o_ready, o_kept, o_turned = sem("o_ready"), sem("o_kept"), sem("o_turned")
        oh_kept, ol_kept, w_ready, w_added = (
            sem("oh_kept"), sem("ol_kept"), sem("w_ready"), sem("w_added"))
        filled, fill_kept = sem("filled"), sem("fill_kept")
        rot_a_done, rot_b_done, rotated = sem("rot_a_done"), sem("rot_b_done"), sem("rotated")
        folded, w_hi_done, w_lo_done = sem("folded"), sem("w_hi_done"), sem("w_lo_done")
        folo_done, wo_hi_done, wo_lo_done = sem("folo_done"), sem("wo_hi_done"), sem("wo_lo_done")
        x1_done, z_done, z_turned, z_kept, z_hi, z_lo = (
            sem("x1_done"), sem("z_done"), sem("z_turned"), sem("z_kept"), sem("z_hi"), sem("z_lo"))
        logits, lg_done, lg_exp, gating, gates_done, g_turned, gates_kept, g_hi_done = (
            sem("logits"), sem("lg_done"), sem("lg_exp"), sem("gating"), sem("gates_done"),
            sem("g_turned"), sem("gates_kept"), sem("g_hi_done"))
        up_ready, silu_done, mul_done, act_done, act_hi, act_lo = (
            sem("up_ready"), sem("silu_done"), sem("mul_done"), sem("act_done"), sem("act_hi"),
            sem("act_lo"))
        up_w_hi, up_w_lo, down_w_hi, down_w_lo = (
            sem("up_w_hi"), sem("up_w_lo"), sem("down_w_hi"), sem("down_w_lo"))
        down_done, y_scaled, y_done, stored = (
            sem("down_done"), sem("y_scaled"), sem("y_done"), sem("stored"))

        block = ctx.enter_context(nc.Block())

        def steps(eng, order, last_order, step):
            with eng.Fori(0, PAIRS // 2 - 1) as i:
                for slot in range(2):
                    step(i * 2 + slot, slot, i, order, FILL_AT)
            step(PAIRS - 2, 0, PAIRS // 2 - 1, [e for e in order if e[0][0] != "G"], FILL_AT_6)
            step(PAIRS - 1, 1, PAIRS // 2 - 1, last_order, {})

        def fill_no(p, j):
            return p * FILLS + (FILLS_AHEAD + j)

        def fill_bank(j):
            return FILL_BANK[(FILLS_AHEAD + j) % 2][:, :]

        def place(t, slot):
            head, cols = t // 2 % 2, (t % 2) * 512
            if t < 4:
                return q_t[:, slot, head, cols:cols + 512]
            return k_t[:, slot, head, WIN + cols:WIN + cols + 512]

        def raw_up(s):
            return w_raw[:, s % 2, s // 2, 0:UPW]

        def raw_down(s):
            return wo_raw[:, s % 2, s // 2]

        @block.sync
        def _(sp):
            sp.dma_start(x_sb[:, :, :], x.rearrange("(b p) d -> p b d", p=128)).then_inc(ld_x, 16)
            sp.dma_start(wm_sb, w_mod).then_inc(ld_mod, 16)

            def load_pair(p, slot):
                sp.dma_start(w_raw[:, slot], w_qkv[bass.ds(p, 1)].rearrange("o p k n -> (o p) k n")) \
                    .then_inc(ld_raw[slot], 16)
                sp.dma_start(bq_sb[:, slot], b_qkv[bass.ds(p, 1)].rearrange("o r n -> (o r) n")) \
                    .then_inc(ld_raw[slot], 16)

            def load_wo(p, slot):
                sp.dma_start(wo_raw[:, slot], w_o[bass.ds(p, 1)].rearrange("o p h n -> (o p) h n")) \
                    .then_inc(ld_wo[slot], 16)
                sp.dma_start(ao_sb[:, slot], a_o[bass.ds(p, 1)].rearrange("o r n -> (o r) n")) \
                    .then_inc(ld_wo[slot], 16)

            def move_values(slot):
                sp.dma_start(v_off[0:64, slot, 1:NB], v_sb[64:128, slot, 0:NB - 1]) \
                    .then_inc(v_moved[slot], 16)
                sp.dma_start(v_off[64:128, slot, :], v_sb[0:64, slot, :]).then_inc(v_moved[slot], 16)

            load_pair(0, 0)
            load_wo(0, 0)
            load_pair(1, 1)
            load_wo(1, 1)
            sp.wait_ge(fill_kept, AHEAD.index(("V", 3)) + 3)
            sp.wait_ge(mod_ready, 1)
            move_values(0)

            def step(p, slot, half, order, at):
                kinds = {k for k, _ in order}
                if "G" in kinds:
                    sp.wait_ge(w_lo_done, p * 3 + 3)
                    load_pair(p + 2, slot)
                    sp.wait_ge(wo_lo_done, p + 1)
                    load_wo(p + 2, slot)
                if "V" in kinds:
                    sp.wait_ge(fill_kept, fill_no(p, at["V", 3] + 3))
                    move_values(1 - slot)

            steps(sp, PE_STEP, [], step)

            def load_up(c, s):
                sp.dma_start(raw_up(s), w_up[bass.ds(c, 1)].rearrange("o p n -> (o p) n")) \
                    .then_inc(ld_up[s], 16)

            def load_down(c, s):
                sp.dma_start(raw_down(s), w_down[bass.ds(c, 1)].rearrange("o p n -> (o p) n")) \
                    .then_inc(ld_down[s], 16)

            sp.wait_ge(w_lo_done, 3 * PAIRS)
            sp.wait_ge(wo_lo_done, PAIRS)
            for s in range(4):
                load_up(s, s)
                load_down(s, s)

            def next_chunk(n, c, s):
                sp.wait_ge(up_w_lo, n - 3)
                load_up(c, s)
                sp.wait_ge(down_w_lo, n - 3)
                load_down(c, s)

            with sp.Fori(1, 3) as i:
                for s in range(4):
                    next_chunk(i * 4 + s, i * 4 + s, s)
            for s in range(4):
                next_chunk(12 + s, (12 + s) % CH, s)
            with sp.Fori(4, 7) as i:
                for s in range(4):
                    next_chunk(i * 4 + s, i * 4 + (s - CH), s)
            for j in range(NB // 2):
                sp.wait_ge(y_done, j + 1)
                sp.dma_start(out[j * 256:j * 256 + 256].rearrange("(b p) d -> p b d", p=128),
                             y_out[:, 2 * j:2 * j + 2]).then_inc(stored, 16)
            sp.wait_ge(stored, 16 * NB // 2)

        @block.gpsimd
        def _(pool):
            pool.memset(k_t[:, :, :, 0:WIN], 0.0).then_inc(zeroed, 1)
            pool.memset(zero_bf[:, :], 0.0).then_inc(zeroed, 1)
            pool.wait_ge(zeroed, 2)

            def lo_of_weights(count, slot, m):
                pool.wait_ge(w_hi_done, count)
                cols = slice(m * 256, m * 256 + 256)
                pool.tensor_tensor(out=w_lo[:, slot, :, cols], in0=w_raw[:, slot, :, cols],
                                   in1=w_hi[:, slot, :, cols].bitcast(f32), op=ALU.subtract) \
                    .then_inc(w_lo_done, 1)
                pool.wait_ge(w_lo_done, count)

            def lo_of_wo(count, slot):
                pool.wait_ge(wo_hi_done, count)
                pool.tensor_tensor(out=wo_lo[:, slot], in0=wo_raw[:, slot],
                                   in1=wo_hi[:, slot].bitcast(f32), op=ALU.subtract) \
                    .then_inc(wo_lo_done, 1)
                pool.wait_ge(wo_lo_done, count)

            def rotate_b(count, kept, free, t):
                cols = slice((t % 2) * 512, (t % 2) * 512 + 512)
                pool.wait_ge(fill_kept, kept)
                pool.wait_ge(rotated, free)
                pool.tensor_tensor(out=rot_b[0:64, t % 2], in0=qk_raw[64:128, t % 4],
                                   in1=sin_sb[64:128, cols], op=ALU.mult).then_inc(rot_b_half, 1)
                pool.wait_ge(rot_b_half, count)
                pool.tensor_tensor(out=rot_b[64:128, t % 2], in0=qk_raw[0:64, t % 4],
                                   in1=sin_sb[0:64, cols], op=ALU.mult).then_inc(rot_b_done, 1)
                pool.wait_ge(rot_b_done, count)

            for m in range(3):
                lo_of_weights(m + 1, 0, m)
            pool.wait_ge(ld_tab, 64)
            for t in range(8):
                rotate_b(t + 1, AHEAD.index(("Q", t)) + 3, t + 3, t)
            pool.wait_ge(mod_ready, 1)
            pool.memset(v_off[0:64, :, 0, :], 0.0).then_inc(zeroed, 1)
            pool.wait_ge(zeroed, 3)
            lo_of_wo(1, 0)
            for m in range(3):
                lo_of_weights(m + 4, 1, m)

            def step(p, slot, half, order, at):
                for kind, n in order:
                    if kind == "QB":
                        rotate_b(p * 8 + (9 + n), fill_no(p, at["Q", n] + 3), p * 8 + (11 + n), n)
                    if kind == "GL":
                        lo_of_weights(p * 3 + (7 + n), slot, n)
                    if kind == "PL":
                        lo_of_wo(p + 2, 1 - slot)

            steps(pool, POOL_STEP, [], step)

            def lo_of_up(count, s):
                pool.wait_ge(up_w_hi, count)
                pool.tensor_tensor(out=w_lo[:, s % 2, 0, 0:UPW], in0=raw_up(s),
                                   in1=w_hi[:, s % 2, 0, 0:UPW].bitcast(f32), op=ALU.subtract) \
                    .then_inc(up_w_lo, 1)
                pool.wait_ge(up_w_lo, count)

            def lo_of_down(count, s):
                pool.wait_ge(down_w_hi, count)
                pool.tensor_tensor(out=wo_lo[:, s % 2, 0], in0=raw_down(s),
                                   in1=wo_hi[:, s % 2, 0].bitcast(f32), op=ALU.subtract) \
                    .then_inc(down_w_lo, 1)
                pool.wait_ge(down_w_lo, count)

            for s in range(2):
                lo_of_up(1 + s, s)
            with pool.Fori(0, CH // 2 - 1) as i:
                for s in range(4):
                    lo_of_up(i * 4 + (3 + s), (2 + s) % 4)
                    lo_of_down(i * 4 + (1 + s), s)
            for s in range(2):
                lo_of_up(2 * CH - 1 + s, 2 + s)
                lo_of_down(2 * CH - 3 + s, s)
            for s in range(2):
                lo_of_down(2 * CH - 1 + s, 2 + s)

        @block.scalar
        def _(act):
            for dst, src in ((c_sb, c_col), (nw_sb, norm_w), (tie_sb, tie), (gw_sb, gate_w)):
                act.dma_start(dst, src).then_inc(ld_small, 16)
            for dst, src in ((aq_sb[:, :], a_qkv), (bo_sb[:, :], b_o)):
                act.dma_start(dst, src).then_inc(ld_lora, 16)
            for dst, src in ((id_sb[:, :], ident), (mask_sb[:, :, :], mask), (cos_sb[:, :], cos_t),
                             (sin_sb[:, :], sin_t)):
                act.dma_start(dst, src).then_inc(ld_tab, 16)
            act.sem_inc(exped, 2)
            act.sem_inc(fill_kept, 2)
            act.sem_inc(p_kept, 1)
            act.sem_inc(o_kept, 1)

            act.wait_ge(ld_small, 64)
            act.activation(sil_c, c_sb, ACT.Silu).then_inc(silu_c, 1)
            act.wait_ge(ld_tab, 64)
            act.activation(id_bf[:, :], id_sb[:, :], ACT.Copy).then_inc(id_done, 1)
            act.wait_ge(var_done, 1)
            act.activation(rstd, tmp8, ACT.Sqrt).then_inc(std_done, 1)
            for b in range(NB):
                act.wait_ge(h_done, 1 + b // 4)
                act.activation(sq_out[:, b], res[:, b], ACT.Square,
                               accum_out=ssq[:, b:b + 1]).then_inc(squared, 1)
            def keep(number, view, dst, scale):
                act.wait_ge(filled, number)
                act.activation(dst, view, ACT.Copy, scale=scale).then_inc(fill_kept, 1)

            def keep_projection(number, view, t, free):
                act.wait_ge(rotated, free)
                keep(number, view, qk_raw[:, t % 4], SCALE if t < 4 else 1.0)

            def keep_values(number, view, v, slot):
                keep(number, view,
                     v_sb[:, slot, 2 * v:2 * v + 2].rearrange("p b d -> p (b d)"), 1.0)

            def hi_of_weights(count, slot, m):
                act.wait_ge(folded, count)
                cols = slice(m * 256, m * 256 + 256)
                act.activation(w_hi[:, slot, :, cols], w_raw[:, slot, :, cols], ACT.Copy) \
                    .then_inc(w_hi_done, 1)

            def hi_of_wo(count, slot):
                act.wait_ge(folo_done, count)
                act.activation(wo_hi[:, slot], wo_raw[:, slot], ACT.Copy).then_inc(wo_hi_done, 1)

            for m in range(3):
                if m == 2:
                    act.wait_ge(folded, 1)
                keep(m + 1, fill_bank(m - FILLS_AHEAD), fold_tmp[:, m % 2], LORA_SCALE)
            act.wait_ge(ms_done, 1)
            act.activation(rstd, tmp8, ACT.Sqrt).then_inc(rms_done, 1)
            for m in range(3):
                hi_of_weights(m + 1, 0, m)
            for n in range(4):
                k, half = n % 2, n // 2
                act.wait_ge(h_turned, n + 1)
                act.activation(hi_t[:, k, half * 512:half * 512 + 512], bank[2 + n][:, :],
                               ACT.Identity, scale=nw_sb[:, k:k + 1]).then_inc(h_hi, 1)
            act.wait_ge(squared, NB)
            for j, (kind, n) in enumerate(AHEAD[3:], 3):
                view = fill_bank(j - FILLS_AHEAD)
                if kind == "Q":
                    keep_projection(j + 1, view, n, n + 1)
                if kind == "V":
                    keep_values(j + 1, view, n, 0)
                if kind == "P":
                    act.wait_ge(folded, 2)
                    keep(j + 1, view, fold_tmp[:, 1], LORA_SCALE)
                    hi_of_wo(1, 0)
                if kind == "G1":
                    if n == 1:
                        act.wait_ge(folo_done, 1)
                    else:
                        act.wait_ge(folded, 3 + n // 2)
                    keep(j + 1, view, fold_tmp[:, n % 2], LORA_SCALE)
            for m in range(3):
                hi_of_weights(m + 4, 1, m)

            def root_after(half):
                act.wait_ge(var_done, 2 + half)
                at = slice(4 * half, 4 * half + 4)
                act.activation(rstd[:, at], tmp8[:, at], ACT.Sqrt).then_inc(std_done, 1)

            def keep_z(n):
                k, half = n % 2, n // 2
                cols = slice(half * 512, half * 512 + 512)
                act.wait_ge(z_turned, n + 1)
                act.activation(h2_t[:, k, cols], FILL_BANK[k][:, :], ACT.Identity,
                               bias=mod_c[:, 0, k:k + 1], scale=mod_c[:, 1, k:k + 1]) \
                    .then_inc(z_kept, 1)
                act.activation(hi_t[:, k, cols], FILL_BANK[k][:, :], ACT.Identity,
                               bias=mod_c[:, 0, k:k + 1], scale=mod_c[:, 1, k:k + 1]) \
                    .then_inc(z_hi, 1)

            def hi_of_up(count, s):
                act.wait_ge(ld_up[s], count)
                act.activation(w_hi[:, s % 2, 0, 0:UPW], raw_up(s), ACT.Copy).then_inc(up_w_hi, 1)

            def step(p, slot, half, order, at):
                act.activation(small[:, 504:505], id_sb[:, 0:1], ACT.Exp)
                if at:
                    act.wait_ge(scored, p * 4 + 1)
                for kind, n in order:
                    unit = p * 4 + n
                    if kind in FILL_KINDS:
                        j = at[kind, n]
                        number, view = fill_no(p, j + 1), fill_bank(j)
                    if kind == "Q":
                        keep_projection(number, view, n, p * 8 + (9 + n))
                    if kind == "V":
                        keep_values(number, view, n, 1 - slot)
                    if kind == "P":
                        act.wait_ge(folded, p * 3 + (8 if ("G", 1) in at else 5))
                        keep(number, view, fold_tmp[:, 1], LORA_SCALE)
                    if kind == "PH":
                        hi_of_wo(p + 2, 1 - slot)
                    if kind == "G":
                        if n == 1:
                            act.wait_ge(folo_done, p + 1)
                        else:
                            act.wait_ge(folded, p * 3 + (6 + n // 2))
                        keep(number, view, fold_tmp[:, n % 2], LORA_SCALE)
                    if kind == "GH":
                        hi_of_weights(p * 3 + (7 + n), slot, n)
                    if kind == "E":
                        act.wait_ge(maxed, unit + 1)
                        for b in range(4):
                            last = act.activation(probs[:, n % 2, b * 128:b * 128 + 128],
                                                  S_BANK[n % 2][:, b * 128:b * 128 + 128], ACT.Exp,
                                                  bias=neg_max[:, n % 2, b:b + 1],
                                                  accum_out=row_sum[:, n % 2, b:b + 1])
                        last.then_inc(exped, 1)
                    if kind == "T":
                        act.wait_ge(p_turned, unit + 1)
                        act.activation(probs_t[:, n % 2], PT_BANK[:, :], ACT.Copy).then_inc(p_kept, 1)
                    if kind == "O":
                        act.wait_ge(o_ready, unit + 1)
                        act.wait_ge(summed, unit + 1)
                        for b in range(4):
                            last = act.activation(o_norm[:, n % 2, b * 128:b * 128 + 128],
                                                  O_BANK[:, b * 128:b * 128 + 128], ACT.Identity,
                                                  scale=row_inv[:, n % 2, b:b + 1])
                        last.then_inc(o_kept, 1)
                    if kind == "X":
                        act.wait_ge(o_turned, unit + 1)
                        act.activation(o_hi[:, n % 2], OT_BANK[:, :], ACT.Copy).then_inc(oh_kept, 1)
                    if kind == "U":
                        hi_of_up(16, n)
                    if kind == "ZR":
                        root_after(n)
                    if kind == "ZH":
                        keep_z(n)

            steps(act, ACT_STEP, ACT_LAST, step)

            def hi_of_down(count, s):
                act.wait_ge(ld_down[s], count)
                act.activation(wo_hi[:, s % 2, 0], raw_down(s), ACT.Copy).then_inc(down_w_hi, 1)

            def silu(c, slot):
                act.wait_ge(up_ready, c + 1)
                act.activation(qk_raw[:, slot], bank[2 + slot][:, :], ACT.Silu) \
                    .then_inc(silu_done, 1)

            def hi(c, slot):
                act.wait_ge(act_done, c + 1)
                act.activation(o_hi[:, slot], probs[:, slot], ACT.Copy).then_inc(act_hi, 1)

            root_after(1)
            for c in range(2):
                silu(c, c)
                hi_of_up(16, 2 + c)
            for n in range(2, 4):
                keep_z(n)
            for c in range(2):
                hi(c, c)
                hi_of_down(16, c)
            act.wait_ge(lg_done, 1)
            act.activation(sc, lg, ACT.Exp).then_inc(lg_exp, 1)
            silu(2, 0)
            hi_of_up(32, 0)
            act.wait_ge(gates_done, 1)
            act.activation(g_hi, t64, ACT.Copy).then_inc(g_hi_done, 1)
            for n in range(2):
                act.wait_ge(g_turned, n + 1)
                act.activation(gate_t[:, n], FILL_BANK[n][0:GK, :], ACT.Copy) \
                    .then_inc(gates_kept, 1)
            act.wait_ge(down_done, 1)
            hi(2, 0)
            hi_of_down(16, 2)

            def chunk(c, s, up_count, down_count):
                silu(c, s % 2)
                if up_count is not None:
                    hi_of_up(up_count, (s + 2) % 4)
                act.wait_ge(act_done, c + 1)
                act.wait_ge(down_done, c - 1)
                hi(c, s % 2)
                hi_of_down(down_count, s)

            chunk(3, 3, 32, 16)
            with act.Fori(1, CH // 2 - 1) as i:
                for s in range(4):
                    chunk(i * 4 + s, s, i * 16 + (16 + 16 * ((s + 2) // 4)), i * 16 + 16)
            for s in range(4):
                chunk(2 * CH - 4 + s, s, 16 * CH // 2 if s < 2 else None, 16 * CH // 2)

        @block.vector
        def _(dve):
            dve.sem_inc(ol_kept, 1)
            dve.sem_inc(w_added, 1)
            dve.sem_inc(rotated, 4)

            def mean_and_variance(blocks, base):
                for b in blocks:
                    dve.bn_stats(stats[:, b], x_sb[:, b]).then_inc(stats_done, 1)
                dve.wait_ge(stats_done, base + len(blocks))
                for b in blocks:
                    dve.bn_aggr(mean_var[:, b], stats[:, b]).then_inc(stats_done, 1)
                dve.wait_ge(stats_done, base + 2 * len(blocks))
                at = slice(blocks[0], blocks[-1] + 1)
                dve.tensor_scalar(out=tmp8[:, at], in0=mean_var[:, at, 1], scalar1=LN_EPS,
                                  scalar2=None, op0=ALU.add).then_inc(var_done, 1)

            def normalise(dst, blocks, count, done):
                dve.wait_ge(std_done, count)
                at = slice(blocks[0], blocks[-1] + 1)
                dve.reciprocal(rstd[:, at], rstd[:, at]).then_inc(rstd_done, 1)
                dve.wait_ge(rstd_done, count)
                for b in blocks:
                    dve.tensor_scalar(out=dst[:, b], in0=x_sb[:, b],
                                      scalar1=mean_var[:, b, 0:1], scalar2=rstd[:, b:b + 1],
                                      op0=ALU.subtract, op1=ALU.mult).then_inc(done, 1)

            def per_column(rows, row, n):
                return rows[:, row:row + 1, :].broadcast_to([128, n, D])

            dve.wait_ge(silu_c, 1)
            dve.tensor_copy(c_rep, sil_c.rearrange("p (k o) -> p k o", o=1)
                            .broadcast_to([128, KD, 128])).then_inc(c_spread, 1)
            dve.wait_ge(ld_x, 16)
            mean_and_variance(range(NB), 0)
            normalise(res, range(NB), 1, x_normed)
            dve.wait_ge(mod_ready, 1)
            gates = mod_b[:, :].rearrange("p a d -> p (a d)")
            dve.tensor_copy(mod_a[:, 0], bank[0][:, 0:D])
            dve.tensor_scalar(out=mod_a[:, 1], in0=bank[0][:, D:2 * D], scalar1=1.0, scalar2=None,
                              op0=ALU.add)
            dve.tensor_scalar(out=sgn_g, in0=bank[1][:, :], scalar1=0.0, scalar2=2.0,
                              op0=ALU.is_ge, op1=ALU.mult).then_inc(mod_kept, 1)
            dve.wait_ge(mod_kept, 1)
            dve.scalar_tensor_tensor(out=gates, in0=sgn_g, scalar=-1.0, in1=bank[1][:, :],
                                     op0=ALU.add, op1=ALU.mult).then_inc(mod_kept, 1)
            dve.wait_ge(mod_kept, 2)
            dve.tensor_scalar(out=gates, in0=gates, scalar1=0.25, scalar2=None,
                              op0=ALU.max).then_inc(mod_kept, 1)
            dve.tensor_copy(mod_c[:, 0], bank[2][:, 0:KD])
            dve.tensor_scalar(out=mod_c[:, 1], in0=bank[2][:, KD:2 * KD], scalar1=1.0, scalar2=None,
                              op0=ALU.add)
            dve.wait_ge(mod_kept, 3)
            dve.scalar_tensor_tensor(out=gates, in0=sgn_g, scalar=-1.0, in1=gates, op0=ALU.add,
                                     op1=ALU.mult).then_inc(mod_kept, 1)
            dve.wait_ge(mod_kept, 4)
            for half in range(2):
                view = res[:, 4 * half:4 * half + 4]
                dve.wait_ge(x_normed, 4 * half + 4)
                dve.tensor_tensor(out=view, in0=view, in1=per_column(mod_a, 1, 4), op=ALU.mult) \
                    .then_inc(mod_kept, 1)
                dve.wait_ge(mod_kept, 5 + half)
                dve.tensor_tensor(out=view, in0=view, in1=per_column(mod_a, 0, 4), op=ALU.add) \
                    .then_inc(h_done, 1)

            def fold(kept, slot, m):
                dve.wait_ge(fill_kept, kept)
                view = w_raw[:, slot, :, m * 256:m * 256 + 256]
                dve.tensor_tensor(out=view,
                                  in0=fold_tmp[:, m % 2].rearrange("p (k n) -> p k n", k=KD),
                                  in1=view, op=ALU.add).then_inc(folded, 1)

            def fold_wo(kept, slot):
                dve.wait_ge(fill_kept, kept)
                view = wo_raw[:, slot]
                dve.tensor_tensor(out=view, in0=fold_tmp[:, 1].rearrange("p (h n) -> p h n", h=2),
                                  in1=view, op=ALU.add).then_inc(folo_done, 1)

            def rotate_a(kept, free, t):
                dve.wait_ge(fill_kept, kept)
                dve.wait_ge(rotated, free)
                dve.tensor_tensor(out=rot_a[:, t % 2], in0=qk_raw[:, t % 4],
                                  in1=cos_sb[:, (t % 2) * 512:(t % 2) * 512 + 512], op=ALU.mult) \
                    .then_inc(rot_a_done, 1)

            def rotate(count, t, slot):
                dve.wait_ge(rot_a_done, count)
                dve.wait_ge(rot_b_done, count)
                dve.tensor_tensor(out=place(t, slot), in0=rot_a[:, t % 2], in1=rot_b[:, t % 2],
                                  op=ALU.add).then_inc(rotated, 1)

            for m in range(3):
                fold(m + 3, 0, m)
            dve.wait_ge(squared, NB)
            dve.tensor_scalar(out=tmp8, in0=ssq, scalar1=1.0 / D, scalar2=RMS_EPS, op0=ALU.mult,
                              op1=ALU.add).then_inc(ms_done, 1)
            dve.wait_ge(rms_done, 1)
            dve.reciprocal(rstd, rstd).then_inc(ms_done, 1)
            dve.wait_ge(ms_done, 2)
            for b in range(NB):
                dve.tensor_scalar(out=h_norm[:, b], in0=res[:, b], scalar1=rstd[:, b:b + 1],
                                  scalar2=None, op0=ALU.mult).then_inc(h_normed, 1)
            for n in range(4):
                k, half = n % 2, n // 2
                cols = slice(half * 512, half * 512 + 512)
                dve.wait_ge(h_hi, n + 1)
                dve.scalar_tensor_tensor(out=lo_t[:, k, cols], in0=bank[2 + n][:, :],
                                         scalar=nw_sb[:, k:k + 1],
                                         in1=hi_t[:, k, cols].bitcast(f32), op0=ALU.mult,
                                         op1=ALU.subtract).then_inc(h_lo, 1)
            dve.wait_ge(ld_tab, 64)
            for t in range(8):
                if t >= 2:
                    rotate(t - 1, t - 2, 0)
                rotate_a(AHEAD.index(("Q", t)) + 3, t + 3, t)
            rotate(7, 6, 0)
            rotate(8, 7, 0)
            dve.wait_ge(ld_wo[0], 32)
            fold_wo(AHEAD.index(("P", 0)) + 3, 0)
            for m in range(3):
                fold(AHEAD.index(("G1", m)) + 3, 1, m)

            def x_after(half):
                view, to = res[:, 4 * half:4 * half + 4], x_sb[:, 4 * half:4 * half + 4]
                dve.wait_ge(w_added, 4 * PAIRS - 1 + 2 * half)
                dve.tensor_tensor(out=view, in0=view, in1=per_column(mod_b, 0, 4), op=ALU.mult) \
                    .then_inc(x1_done, 1)
                dve.wait_ge(x1_done, 2 * half + 1)
                dve.tensor_tensor(out=to, in0=to, in1=view, op=ALU.add).then_inc(x1_done, 1)

            def normal_after(half):
                blocks = range(4 * half, 4 * half + 4)
                dve.wait_ge(x1_done, 2 * half + 2)
                mean_and_variance(blocks, 2 * NB + 8 * half)
                normalise(z_sb, blocks, 2 + half, z_done)

            def lo_of_z(n):
                k, half = n % 2, n // 2
                cols = slice(half * 512, half * 512 + 512)
                dve.wait_ge(z_hi, n + 1)
                dve.tensor_tensor(out=lo_t[:, k, cols], in0=h2_t[:, k, cols],
                                  in1=hi_t[:, k, cols].bitcast(f32), op=ALU.subtract) \
                    .then_inc(z_lo, 1)

            def step(p, slot, half, order, at):
                if at:
                    dve.wait_ge(scored, p * 4 + 1)
                for kind, n in order:
                    unit = p * 4 + n
                    if kind == "M":
                        dve.wait_ge(scored, unit + 1)
                        dve.tensor_reduce(out=neg_max[:, n % 2],
                                          in_=S_BANK[n % 2][:, :].rearrange("p (b k) -> p b k", b=4),
                                          axis=AX.X, op=ALU.max, negate=True).then_inc(maxed, 1)
                    if kind == "N":
                        dve.wait_ge(exped, unit + 3)
                        dve.reciprocal(row_inv[:, n % 2], row_sum[:, n % 2]).then_inc(summed, 1)
                    if kind == "XL":
                        dve.wait_ge(oh_kept, unit + 1)
                        dve.tensor_tensor(out=o_lo[:, n % 2], in0=OT_BANK[:, :],
                                          in1=o_hi[:, n % 2].bitcast(f32), op=ALU.subtract) \
                            .then_inc(ol_kept, 1)
                    if kind == "W":
                        dve.wait_ge(w_ready, unit + 1)
                        dve.wait_ge(w_added, unit + 1)
                        view = res[:, 2 * n:2 * n + 2].rearrange("p b d -> p (b d)")
                        dve.tensor_tensor(out=view, in0=W_BANK[:, :], in1=view, op=ALU.add) \
                            .then_inc(w_added, 1)
                    if kind == "QA":
                        rotate_a(fill_no(p, at["Q", n] + 3), p * 8 + (11 + n), n)
                    if kind == "QR":
                        rotate(p * 8 + (9 + n), n, 1 - slot)
                    if kind == "P":
                        fold_wo(fill_no(p, at["P", 0] + 3), 1 - slot)
                    if kind == "G":
                        fold(fill_no(p, at["G", n] + 3), slot, n)
                    if kind == "ZX":
                        x_after(n)
                    if kind == "ZN":
                        normal_after(n)
                    if kind == "ZL":
                        lo_of_z(n)

            steps(dve, DVE_STEP, DVE_LAST, step)

            normal_after(1)

            def multiply(c, slot):
                dve.wait_ge(silu_done, c + 1)
                if isinstance(c, int) and c < SHARED:
                    dve.tensor_tensor(out=probs[:, slot], in0=qk_raw[:, slot],
                                      in1=bank[4 + slot][:, :], op=ALU.mult).then_inc(act_done, 1)
                else:
                    dve.tensor_tensor(out=rot_a[:, slot], in0=qk_raw[:, slot],
                                      in1=bank[4 + slot][:, :], op=ALU.mult).then_inc(mul_done, 1)
                    dve.wait_ge(mul_done, c + (1 - SHARED))
                    dve.tensor_tensor(out=probs[:, slot], in0=rot_a[:, slot],
                                      in1=bank[6 + slot][:, :], op=ALU.mult).then_inc(act_done, 1)

            def lo(c, slot):
                dve.wait_ge(act_hi, c + 1)
                dve.tensor_tensor(out=o_lo[:, slot], in0=probs[:, slot],
                                  in1=o_hi[:, slot].bitcast(f32), op=ALU.subtract) \
                    .then_inc(act_lo, 1)

            for c in range(2):
                multiply(c, c)
            for c in range(2):
                lo(c, c)

            def by_block(view):
                return view.rearrange("p (b e) -> p b e", e=E)

            def spread(view):
                return view.rearrange("p (b o) -> p b o", o=1).broadcast_to([128, NB, E])

            done = [0]

            def then_wait(ins):
                done[0] += 1
                ins.then_inc(gating, 1)
                dve.wait_ge(gating, done[0])

            dve.wait_ge(logits, 1)
            then_wait(dve.tensor_reduce(out=m8, in_=by_block(LG_BANK[:, 0:NB * E]), axis=AX.X,
                                        op=ALU.max))
            dve.tensor_tensor(out=by_block(lg), in0=by_block(LG_BANK[:, 0:NB * E]), in1=spread(m8),
                              op=ALU.subtract).then_inc(lg_done, 1)
            dve.wait_ge(lg_exp, 1)
            then_wait(dve.tensor_reduce(out=m8, in_=by_block(sc), axis=AX.X, op=ALU.add))
            then_wait(dve.reciprocal(m8, m8))
            then_wait(dve.tensor_tensor(out=by_block(sc), in0=by_block(sc), in1=spread(m8),
                                        op=ALU.mult))
            for left, one_hot in ((sc, oh1), (lg, oh2)):
                then_wait(dve.tensor_reduce(out=m8, in_=by_block(left), axis=AX.X, op=ALU.max))
                then_wait(dve.tensor_tensor(out=by_block(t64), in0=by_block(left), in1=spread(m8),
                                            op=ALU.is_equal))
                then_wait(dve.tensor_tensor(out=t64, in0=t64, in1=tie_sb, op=ALU.mult))
                then_wait(dve.tensor_reduce(out=m8, in_=by_block(t64), axis=AX.X, op=ALU.max))
                then_wait(dve.tensor_tensor(out=by_block(one_hot), in0=by_block(t64),
                                            in1=spread(m8), op=ALU.is_equal))
                if left is sc:
                    then_wait(dve.scalar_tensor_tensor(out=lg, in0=oh1, scalar=-2.0, in1=sc,
                                                       op0=ALU.mult, op1=ALU.add))
            then_wait(dve.tensor_tensor(out=oh1, in0=oh1, in1=oh2, op=ALU.add))
            then_wait(dve.tensor_tensor(out=sc, in0=sc, in1=oh1, op=ALU.mult))
            then_wait(dve.tensor_reduce(out=m8, in_=by_block(sc), axis=AX.X, op=ALU.add))
            then_wait(dve.reciprocal(m8, m8))
            dve.tensor_tensor(out=by_block(t64), in0=by_block(sc), in1=spread(m8), op=ALU.mult) \
                .then_inc(gates_done, 1)
            dve.wait_ge(g_hi_done, 1)
            high = by_block(g_hi.bitcast(f32))
            dve.tensor_copy(g_cat[:, :, 0:E], high)
            dve.tensor_tensor(out=g_cat[:, :, E:2 * E], in0=by_block(t64), in1=high,
                              op=ALU.subtract)
            dve.memset(g_cat[:, :, 2 * E:GK], 1.0).then_inc(gates_done, 1)

            for n in range(2, 4):
                lo_of_z(n)

            def chunk(c, slot):
                multiply(c, slot)
                lo(c, slot)

            def output(half):
                dve.wait_ge(down_done, CH * (half + 1))
                for j in range(2):
                    b = 4 * half + 2 * j
                    dve.tensor_tensor(out=y_out[:, b:b + 2],
                                      in0=bank[j][:, :].rearrange("p (b d) -> p b d", b=2),
                                      in1=per_column(mod_b, 1, 2), op=ALU.mult).then_inc(y_scaled, 1)
                for j in range(2):
                    b = 4 * half + 2 * j
                    dve.wait_ge(y_scaled, 2 * half + 1 + j)
                    dve.tensor_tensor(out=y_out[:, b:b + 2], in0=y_out[:, b:b + 2],
                                      in1=x_sb[:, b:b + 2], op=ALU.add).then_inc(y_done, 1)

            for c in range(2, 4):
                chunk(c, c % 2)
            with dve.Fori(2, CH // 2 + 1) as i:
                for slot in range(2):
                    chunk(i * 2 + slot, slot)
            output(0)
            with dve.Fori(CH // 2 + 1, CH) as i:
                for slot in range(2):
                    chunk(i * 2 + slot, slot)
            output(1)

        @block.tensor
        def _(pe):
            def three(dst, lhs, rhs, contraction, **more):
                n = 0
                for at in contraction:
                    for a, b in ((0, 0), (0, 1), (1, 0)):
                        n += 1
                        last = pe.matmul(dst, lhs(a, at), rhs(b, at), start=n == 1,
                                         stop=n == 3 * len(contraction), **more)
                return last

            t_parts, w_parts, wo_parts, o_parts = (
                (hi_t, lo_t), (w_hi, w_lo), (wo_hi, wo_lo), (o_hi, o_lo))

            pe.wait_ge(ld_mod, 16)
            pe.wait_ge(c_spread, 1)
            for dst, col, n in ((bank[0][:, :], 0, 512), (bank[1][:, 0:D], 2 * D, D),
                                (bank[1][:, D:2 * D], 5 * D, D)):
                for k in range(KD):
                    pe.matmul(dst, c_rep[:, k], wm_sb[:, k, col:col + n], start=k == 0,
                              stop=k == KD - 1)
            for j in range(2 * KD):
                col = 3 * D + j * 128
                for k in range(KD):
                    last = pe.matmul(bank[2][:, j:j + 1], wm_sb[:, k, col:col + 128],
                                     sil_c[:, k:k + 1], start=k == 0, stop=k == KD - 1)
            last.then_inc(mod_ready, 1)

            def lora(j, number, slot, m, loaded):
                pe.wait_ge(ld_raw[slot], loaded)
                pe.wait_ge(fill_kept, number)
                for k in range(KD):
                    last = pe.matmul(fill_bank(j)[:, k * 256:k * 256 + 256],
                                     aq_sb[32 * m:32 * m + R, k * 128:k * 128 + 128],
                                     bq_sb[32 * m:32 * m + R, slot], start=True, stop=True)
                last.then_inc(filled, 1)

            def lora_wo(j, number, slot, loaded):
                pe.wait_ge(ld_wo[slot], loaded)
                pe.wait_ge(fill_kept, number)
                for h in range(2):
                    last = pe.matmul(fill_bank(j)[:, h * 256:h * 256 + 256],
                                     ao_sb[:, slot, h * 128:h * 128 + 128], bo_sb[:, :],
                                     start=True, stop=True)
                last.then_inc(filled, 1)

            def project(j, number, slot, t):
                head, half = t // 2 % 2, t % 2
                col = (t // 4) * 256 + head * 128
                pe.wait_ge(fill_kept, number)
                three(fill_bank(j), lambda a, k: w_parts[a][:, slot, k, col:col + 128],
                      lambda b, k: t_parts[b][:, k, half * 512:half * 512 + 512], range(KD)) \
                    .then_inc(filled, 1)

            def values(j, number, slot, v):
                pe.wait_ge(fill_kept, number)
                for i in range(2):
                    at = (2 * v + i) * 128
                    last = three(fill_bank(j)[:, i * 256:i * 256 + 256],
                                 lambda a, k: t_parts[a][:, k, at:at + 128],
                                 lambda b, k: w_parts[b][:, slot, k, 512:768], range(KD))
                last.then_inc(filled, 1)

            pe.wait_ge(ld_lora, 32)
            for m in range(3):
                lora(m - FILLS_AHEAD, m + 1, 0, m, 32)
            pe.wait_ge(mod_kept, 4)
            pe.wait_ge(ld_tab, 64)
            for n in range(4):
                k, half = n % 2, n // 2
                pe.wait_ge(h_normed, 4 * half + 4)
                for b in range(4):
                    last = pe.transpose(bank[2 + n][:, b * 128:b * 128 + 128],
                                        h_norm[:, 4 * half + b, k * 128:k * 128 + 128], id_sb[:, :])
                last.then_inc(h_turned, 1)
            pe.wait_ge(w_lo_done, 3)
            pe.wait_ge(h_lo, 4)
            for j, (kind, n) in enumerate(AHEAD[3:], 3):
                at = j - FILLS_AHEAD
                if kind == "Q":
                    project(at, j + 1, 0, n)
                if kind == "V":
                    values(at, j + 1, 0, n)
                if kind == "P":
                    lora_wo(at, j + 1, 0, 32)
                if kind == "G1":
                    lora(at, j + 1, 1, n, 32)
            pe.wait_ge(zeroed, 3)
            pe.wait_ge(id_done, 1)

            def turn_z(n):
                k, half = n % 2, n // 2
                pe.wait_ge(z_done, 4 * half + 4)
                if half:
                    pe.wait_ge(z_hi, k + 1)
                for b in range(4):
                    last = pe.transpose(FILL_BANK[k][:, b * 128:b * 128 + 128],
                                        z_sb[:, 4 * half + b, k * 128:k * 128 + 128], id_sb[:, :])
                last.then_inc(z_turned, 1)

            def step(p, slot, half, order, at):
                for kind, n in order:
                    unit, group, head = p * 4 + n, n // 2, n % 2
                    if kind in FILL_KINDS:
                        j = at[kind, n]
                        number = fill_no(p, j + 1)
                    if kind == "S":
                        if n == 0:
                            pe.wait_ge(rotated, p * 8 + 12)
                        pe.wait_ge(exped, unit + 1)
                        pe.matmul(S_BANK[n % 2][:, :], id_bf[:, :], mask_sb[:, group], start=True,
                                  stop=False, skip_group_check=True)
                        for b in range(4):
                            for c in range(2):
                                q0 = (group * 8 + 2 * b + c) * 64
                                last = pe.matmul(
                                    S_BANK[n % 2][64 * c:64 * c + 64, b * 128:b * 128 + 128],
                                    q_t[:, slot, head, q0:q0 + 64],
                                    k_t[:, slot, head, q0:q0 + 128], start=False, stop=True,
                                    skip_group_check=True)
                        last.then_inc(scored, 1)
                    if kind == "T":
                        pe.wait_ge(exped, unit + 3)
                        pe.wait_ge(p_kept, unit + 1)
                        for b in range(4):
                            last = pe.transpose(PT_BANK[:, b * 128:b * 128 + 128],
                                                probs[:, n % 2, b * 128:b * 128 + 128], id_sb[:, :])
                        last.then_inc(p_turned, 1)
                    if kind == "O":
                        if n == 0:
                            pe.wait_ge(v_moved[slot], half * 32 + 32)
                        pe.wait_ge(p_kept, unit + 2)
                        pe.wait_ge(o_kept, unit + 1)
                        for b in range(4):
                            for c, source in enumerate((v_off, v_sb)):
                                q0 = b * 128 + 64 * c
                                last = pe.matmul(
                                    O_BANK[64 * c:64 * c + 64, b * 128:b * 128 + 128],
                                    probs_t[:, n % 2, q0:q0 + 64],
                                    source[:, slot, group * 4 + b, head * 128:head * 128 + 128],
                                    start=True, stop=True)
                        last.then_inc(o_ready, 1)
                    if kind == "X":
                        pe.wait_ge(o_kept, unit + 2)
                        pe.wait_ge(ol_kept, unit + 1)
                        for b in range(4):
                            last = pe.transpose(OT_BANK[:, b * 128:b * 128 + 128],
                                                o_norm[:, n % 2, b * 128:b * 128 + 128],
                                                id_sb[:, :])
                        last.then_inc(o_turned, 1)
                    if kind == "W":
                        if n == 0:
                            pe.wait_ge(wo_lo_done, p + 1)
                        pe.wait_ge(ol_kept, p * 4 + (2 * group + 3))
                        pe.wait_ge(w_added, unit + 1)
                        for i in range(2):
                            col = (2 * (n % 2) + i) * 128
                            last = three(W_BANK[:, i * 256:i * 256 + 256],
                                         lambda a, h: o_parts[a][:, h, col:col + 128],
                                         lambda b, h: wo_parts[b][:, slot, h], range(2))
                        last.then_inc(w_ready, 1)
                    if kind == "Q":
                        if n == 0:
                            pe.wait_ge(w_lo_done, p * 3 + 6)
                        project(j, number, 1 - slot, n)
                    if kind == "V":
                        values(j, number, 1 - slot, n)
                    if kind == "G":
                        lora(j, number, slot, n, half * 32 + 64)
                    if kind == "P":
                        lora_wo(j, number, 1 - slot, half * 32 + (32 + 32 * slot))
                    if kind == "Z":
                        turn_z(n)

            steps(pe, PE_STEP, PE_LAST, step)

            def clear():
                for j in range(2):
                    pe.matmul(bank[j][:, :], zero_bf[:, :], mask_sb[:, 0], start=True,
                              stop=False, skip_group_check=True)

            def up(c, slot, half):
                cols = slice(half * 512, half * 512 + 512)
                pe.wait_ge(up_w_lo, c + 1)
                for m in range(2):
                    last = three(bank[2 + 2 * m + slot][:, :],
                                 lambda a, k: w_parts[a][:, slot, 0, m * 256 + k * 128:
                                                         m * 256 + k * 128 + 128],
                                 lambda b, k: t_parts[b][:, k, cols], range(KD))
                return last

            def gate(slot, half):
                return pe.matmul(bank[6 + slot][:, :], w_hi[0:GK, slot, 0, 512:UPW],
                                 gate_t[:, half], start=True, stop=True)

            def up_and_gate(c, slot, half):
                pe.wait_ge(act_done, c - 1)
                up(c, slot, half)
                gate(slot, half).then_inc(up_ready, 1)

            def down(c, slot):
                pe.wait_ge(down_w_lo, c + 1)
                pe.wait_ge(act_lo, c + 1)
                for b in range(4):
                    dst = bank[b // 2][:, (b % 2) * 256:(b % 2) * 256 + 256]
                    for a, w in ((0, 0), (0, 1), (1, 0)):
                        last = pe.matmul(dst, o_parts[a][:, slot, b * 128:b * 128 + 128],
                                         wo_parts[w][:, slot, 0], start=False, stop=True,
                                         skip_group_check=True)
                last.then_inc(down_done, 1)

            pe.wait_ge(z_lo, 2)
            up(0, 0, 0).then_inc(up_ready, 1)
            pe.wait_ge(w_added, 4 * PAIRS + 1)
            up(1, 1, 0).then_inc(up_ready, 1)
            for half in range(2):
                if half == 1:
                    turn_z(2)
                    turn_z(3)
                    pe.wait_ge(z_kept, 4)
                for b in range(4 * half, 4 * half + 4):
                    for k in range(KD):
                        last = pe.matmul(LG_BANK[:, b * E:b * E + E],
                                         h2_t[:, k, b * 128:b * 128 + 128], gw_sb[:, k],
                                         start=k == 0, stop=k == KD - 1)
            last.then_inc(logits, 1)
            pe.wait_ge(act_done, 1)
            up(2, 0, 0).then_inc(up_ready, 1)
            pe.wait_ge(lg_done, 1)
            clear()
            down(0, 0)
            pe.wait_ge(act_done, 2)
            up(3, 1, 0)
            down(1, 1)
            pe.wait_ge(gates_done, 2)
            pe.wait_ge(z_hi, 4)
            for n in range(2):
                for b in range(4):
                    last = pe.transpose(FILL_BANK[n][0:GK, b * 128:b * 128 + 128],
                                        g_cat[:, 4 * n + b], id_sb[:, :])
                last.then_inc(g_turned, 1)
            pe.wait_ge(gates_kept, 2)
            gate(1, 0).then_inc(up_ready, 1)
            with pe.Fori(1, CH // 2 - 1) as i:
                for slot in range(2):
                    up_and_gate(i * 2 + (slot + 2), slot, 0)
                    down(i * 2 + slot, slot)
            pe.wait_ge(z_lo, 4)
            for slot in range(2):
                up_and_gate(CH + slot, slot, 1)
                down(CH - 2 + slot, slot)
            for slot in range(2):
                up_and_gate(CH + 2 + slot, slot, 1)
                if slot == 0:
                    pe.wait_ge(y_scaled, 2)
                    clear()
                down(CH + slot, slot)
            with pe.Fori(CH // 2 + 1, CH - 1) as i:
                for slot in range(2):
                    up_and_gate(i * 2 + (slot + 2), slot, 1)
                    down(i * 2 + slot, slot)
            for slot in range(2):
                down(2 * CH - 2 + slot, slot)


def kernel(**inputs):
    import numpy as np
    import concourse.bacc as bacc
    from concourse.bass_utils import run_bass_kernel_spmd

    a = {k[3:]: np.asarray(v) for k, v in inputs.items()}
    f32 = np.float32

    theta = f32(1.0) / np.power(f32(10000.0), np.arange(DH // 2, dtype=f32) / f32(DH // 2))
    freqs = np.arange(T, dtype=f32)[:, None] * theta[None, :]
    cos_t = np.cos(np.concatenate([freqs, freqs], 1)).T
    sin = np.sin(freqs).T
    sin_t = np.concatenate([sin, -sin], 0)
    row, key = np.arange(64)[:, None], np.arange(128)[None, :]
    open_ = (key >= row + 1) & (key <= row + WIN)
    mask = np.zeros((2, 128, 4, 128), f32)
    for g in range(2):
        for c in range(2):
            for b in range(4):
                seen = open_ & (key >= WIN) if g == b == c == 0 else open_
                mask[g, 64 * c:64 * c + 64, b] = np.where(seen, 0.0, -1e30)
    from concourse import mybir as _mybir
    mask = mask.transpose(1, 0, 2, 3).reshape(128, 2, 512).astype(_mybir.dt.np(_mybir.dt.bfloat16))
    sel = np.zeros((CH, 128, 128), f32)
    for c in range(CH):
        for i in range(128):
            n = c * 128 + i
            n -= SHARED * 128
            for r in ((n // FI, E + n // FI) if n >= 0 else (2 * E,)):
                sel[c, r, i] = 1.0
    tie = np.tile(np.arange(E, 0, -1, dtype=f32), (128, NB))

    def by_pair(w):
        return w.reshape(PAIRS, 2 * DH, -1).transpose(0, 2, 1)

    w_qkv = np.concatenate([by_pair(a["attn_w" + m]) for m in "qkv"], 2)
    w_qkv = w_qkv.reshape(PAIRS, KD, 128, PW).transpose(0, 2, 1, 3)
    gap = 32 - R
    b_qkv = np.concatenate([np.pad(by_pair(a["attn_" + m + "B"]), ((0, 0), (0, gap), (0, 0)))
                            for m in "qkv"], 1)
    a_qkv = np.concatenate([np.pad(a["attn_" + m + "A"], ((0, gap), (0, 0))) for m in "qkv"])
    w_o = a["attn_wo"].T.reshape(PAIRS, 2, DH, D).transpose(0, 2, 1, 3)
    a_o = a["attn_oA"].reshape(R, PAIRS, 2 * DH).transpose(1, 0, 2)

    def chunks(experts, shared):
        w = np.concatenate([shared, np.zeros((D, SHARED * 128 - 2 * FI), f32),
                            experts.transpose(1, 0, 2).reshape(D, E * FI)], 1)
        return w.reshape(KD, 128, CH, 128).transpose(2, 1, 0, 3).reshape(CH, 128, KD * 128)

    w_up = np.concatenate([chunks(a["ffn_w1"], a["ffn_sw1"]), chunks(a["ffn_w3"], a["ffn_sw3"]),
                           sel], 2)
    w_down = np.concatenate([a["ffn_sw2"], np.zeros((SHARED * 128 - 2 * FI, D), f32),
                             a["ffn_w2"].reshape(E * FI, D)]).reshape(CH, 128, D)

    arrays = {
        "x": a["attn_x"].reshape(T, D), "cos_t": cos_t, "sin_t": sin_t, "mask": mask,
        "ident": np.eye(128, dtype=f32), "c_col": a["c"].reshape(KD, 128).T,
        "w_mod": a["wmod"].reshape(KD, 128, 6 * D).transpose(1, 0, 2),
        "norm_w": a["attn_norm_w"].reshape(KD, 128).T,
        "w_qkv": w_qkv, "b_qkv": b_qkv, "a_qkv": a_qkv, "w_o": w_o, "a_o": a_o,
        "b_o": a["attn_oB"].T,
        "gate_w": a["ffn_gate_w"].T.reshape(KD, 128, E).transpose(1, 0, 2),
        "w_up": w_up, "w_down": w_down, "tie": tie,
    }
    nc = bacc.Bacc("TRN2", target_bir_lowering=False, num_devices=1)
    args, given = {}, {}
    for name, array in arrays.items():
        array = np.ascontiguousarray(array)
        given[f"in_{name}"] = array
        args[name] = nc.dram_tensor(f"in_{name}", array.shape, mybir.dt.from_np(array.dtype),
                                    kind="ExternalInput").ap()
    args["out"] = nc.dram_tensor("out_y", (T, D), mybir.dt.float32, kind="ExternalOutput").ap()
    build(nc, **args)
    result = run_bass_kernel_spmd(nc, [given], core_ids=[0])
    return result.results[0]["out_y"].reshape(1, T, D)
```

```python
import concourse.bass as bass
from concourse import mybir
from contextlib import ExitStack

T = 1024
D = 256
KD = D // 128
H = 16
DH = 128
WIN = 64
R = 16
PAIRS = H // 2
PW = 3 * 2 * DH
NB = T // 128
E = 8
FI = 176
CH = 14
SHARED = 3
GK = 2 * E + 1
UPW = 5 * 128
SCALE = DH ** -0.5
LORA_SCALE = 1.0 / R
LN_EPS = 1e-5
RMS_EPS = 1e-6

PARTS = [0, 2, 4, 6, 1, 3, 5, 7]

PE_STEP = [("S", 0), ("S", 1), ("Q", 0), ("Q", 1), ("T", 0), ("V", 0), ("O", 0), ("Q", 2),
           ("G", 0), ("T", 1), ("S", 2), ("O", 1), ("X", 0), ("P", 0), ("Q", 3), ("V", 1),
           ("T", 2), ("S", 3), ("G", 1), ("Q", 4), ("X", 1), ("O", 2), ("Q", 5), ("W", 0),
           ("T", 3), ("W", 1), ("G", 2), ("V", 2), ("X", 2), ("Q", 6), ("O", 3), ("Q", 7),
           ("X", 3), ("V", 3), ("W", 2), ("W", 3)]
ACT_STEP = [("E", 0), ("Q", 0), ("Q", 1), ("T", 0), ("E", 1), ("V", 0), ("O", 0), ("Q", 2),
            ("T", 1), ("E", 2), ("X", 0), ("GH", 0), ("Q", 3), ("V", 1), ("T", 2), ("O", 1),
            ("Q", 4), ("PH", 0), ("X", 1), ("E", 3), ("O", 2), ("Q", 5), ("GH", 1), ("T", 3),
            ("X", 2), ("V", 2), ("Q", 6), ("GH", 2), ("O", 3), ("Q", 7), ("X", 3), ("V", 3),
            ("GR", 0)]
DVE_STEP = [("M", 0), ("QC", 6), ("M", 1), ("QC", 7), ("N", 0), ("QA", 0), ("QA", 1), ("QR", 0),
            ("G", 0), ("QA", 2), ("N", 1), ("M", 2), ("QR", 1), ("P", 0), ("XL", 0), ("M", 3),
            ("QR", 2), ("G", 1), ("QA", 3), ("XL", 1), ("QA", 4), ("N", 2), ("W", 0), ("N", 3),
            ("W", 1), ("G", 2), ("QR", 3), ("QA", 5), ("QR", 4), ("XL", 2), ("QA", 6), ("QR", 5),
            ("XL", 3), ("QA", 7), ("GT", 0), ("W", 2), ("W", 3)]
POOL_STEP = [("QB", 0), ("QB", 1), ("PG", 0), ("QB", 2), ("GL", 0), ("QB", 3), ("QB", 4),
             ("QB", 5), ("GL", 1), ("QB", 6), ("PL", 0), ("GL", 2), ("QB", 7)]
PE_LAST = [("S", 0), ("S", 1), ("T", 0), ("S", 2), ("T", 1), ("S", 3), ("O", 0), ("T", 2),
           ("O", 1), ("X", 0), ("T", 3), ("X", 1), ("O", 2), ("O", 3), ("W", 0), ("W", 1),
           ("X", 2), ("X", 3), ("W", 2), ("W", 3), ("Z", 0), ("Z", 1)]
ACT_LAST = [("E", 0), ("E", 1), ("T", 0), ("T", 1), ("E", 2), ("O", 0), ("E", 3), ("O", 1),
            ("X", 0), ("T", 2), ("X", 1), ("T", 3), ("O", 2), ("O", 3), ("X", 2), ("X", 3),
            ("ZR", 0), ("U", 0), ("ZH", 0), ("ZH", 1), ("U", 1)]
DVE_LAST = [("M", 0), ("M", 1), ("QC", 6), ("QC", 7), ("N", 0), ("M", 2), ("N", 1), ("M", 3),
            ("XL", 0), ("N", 2), ("XL", 1), ("N", 3), ("W", 0), ("W", 1), ("XL", 2), ("XL", 3),
            ("ZV", 0), ("W", 2), ("W", 3), ("ZN", 0), ("ZL", 0), ("ZL", 1)]
FILL_KINDS = "QVGP"
FILL_AT = {e: j for j, e in enumerate(e for e in PE_STEP if e[0] in FILL_KINDS)}
FILL_AT_6 = {e: j for j, e in enumerate(e for e in FILL_AT if e[0] != "G")}
AHEAD = ([("G", m) for m in range(3)]
         + [("Q", 0), ("Q", 1), ("V", 0), ("Q", 2), ("Q", 3), ("V", 1), ("Q", 4), ("Q", 5), ("V", 2),
            ("Q", 6), ("Q", 7), ("V", 3), ("P", 0), ("G1", 0), ("G1", 1), ("G1", 2)])
FILLS_AHEAD = len(AHEAD)
FILLS = len(FILL_AT)


def build(nc, x, cos_t, sin_t, mask, ident, c_col, w_mod, norm_w, w_qkv, w_o, lora_pairs, lora_all,
          gate_w, w_up, w_down, tie, out):
    f32, f32r, bf16 = mybir.dt.float32, mybir.dt.float32r, mybir.dt.bfloat16
    ALU, ACT, AX = mybir.AluOpType, mybir.ActivationFunctionType, mybir.AxisListType

    ctx = ExitStack()
    with ctx:
        def sb(name, shape, dt=f32):
            return ctx.enter_context(nc.sbuf_tensor(name, shape, dt))

        def sem(name):
            return ctx.enter_context(nc.semaphore(name))

        x_sb = sb("x_sb", [128, NB, D])
        res = sb("res", [128, NB, D])
        hi_t = sb("hi_t", [128, KD, T], f32r)
        lo_t = sb("lo_t", [128, KD, T], f32r)
        cos_sb = sb("cos_sb", [128, T])
        sin_sb = sb("sin_sb", [128, T])
        mask_sb = sb("mask_sb", [128, 2, 512], bf16)
        id_sb = sb("id_sb", [128, 128])
        w_raw = sb("w_raw", [128, 2, KD, PW])
        w_hi = sb("w_hi", [128, 2, KD, PW], f32r)
        w_lo = sb("w_lo", [128, 2, KD, PW], f32r)
        lora_raw = sb("lora_raw", [96, 4 * D])
        lora_p = sb("lora_p", [96, 4 * D], f32r)
        lora_c = sb("lora_c", [96, 4 * D], f32r)
        wo_raw = sb("wo_raw", [128, 2, 2, D])
        wo_hi = sb("wo_hi", [128, 2, 2, D], f32r)
        wo_lo = sb("wo_lo", [128, 2, 2, D], f32r)
        q_t = sb("q_t", [128, 2, 2, T])
        k_t = sb("k_t", [128, 2, 2, WIN + T])
        v_sb = sb("v_sb", [128, 2, NB, 2 * DH])
        v_off = sb("v_off", [128, 2, NB, 2 * DH])
        qk_raw = sb("qk_raw", [128, 4, 512])
        rot_a = sb("rot_a", [128, 2, 512])
        rot_b = sb("rot_b", [128, 2, 512])
        probs = sb("probs", [128, 2, 512])
        probs_t = sb("probs_t", [128, 2, 512])
        o_norm = sb("o_norm", [128, 2, 512])
        o_hi = sb("o_hi", [128, 2, 512], f32r)
        o_lo = sb("o_lo", [128, 2, 512], f32r)
        neg_max = sb("neg_max", [128, 2, 4])
        row_sum = sb("row_sum", [128, 2, 4])
        row_inv = sb("row_inv", [128, 2, 4])
        mod_b = sb("mod_b", [128, 2, D])
        mod_c = sb("mod_c", [128, 2, KD])
        small = sb("small", [128, 488])
        gate_t = w_hi[0:GK, :, 1, 0:512]
        g_hi = w_hi[:, 0, 1, 512:512 + NB * E]
        wm_sb = v_off[:, :, :, :].rearrange("p s b d -> p (s b d)")[:, 0:KD * 6 * D].rearrange(
            "p (k n) -> p k n", k=KD)
        c_rep = v_sb[:, 1, 0, 0:KD * 128].rearrange("p (k n) -> p k n", k=KD)
        sq_out = v_sb[:, 0, :, :]
        sgn_g = v_sb[:, 1, 2:4, :].rearrange("p b d -> p (b d)")
        mod_a = v_sb[:, 1, 4:6, :]
        h_norm = q_t[:, 0, :, :].rearrange("p h t -> p (h t)").rearrange("p (b d) -> p b d", d=D)
        stats = small[:, 0:6 * NB].rearrange("p (b s) -> p b s", s=6)
        mean_var = small[:, 48:48 + 2 * NB].rearrange("p (b s) -> p b s", s=2)
        rstd = small[:, 64:72]
        tmp8 = small[:, 72:80]
        nw_sb = small[:, 80:82]
        c_sb = small[:, 82:84]
        sil_c = small[:, 86:88]
        ssq = small[:, 88:96]
        rms = small[:, 96:104]
        shift = small[:, 104:112]
        lora_all_raw = probs[0:96, :, :].rearrange("p s n -> p (s n)")
        sin_swapped = probs_t[:, :, :].rearrange("p s n -> p (s n)")
        q_swapped = o_norm
        lg = small[:, 96:160]
        sc = small[:, 160:224]
        oh1 = small[:, 224:288]
        oh2 = small[:, 288:352]
        t64 = small[:, 352:416]
        tie_sb = small[:, 416:480]
        m8 = small[:, 480:488]
        g_cat = q_t[:, 1, 0, 0:NB * GK].rearrange("p (b g) -> p b g", g=GK)
        h2_t = k_t[:, :, :, 0:T].rearrange("p s h t -> p (s h) t")[:, 0:KD, :]
        gw_sb = small[:, 352:368].rearrange("p (k e) -> p k e", k=KD)
        z_sb = q_t[:, 0, :, :].rearrange("p h t -> p (h t)").rearrange("p (b d) -> p b d", d=D)
        y_out = v_sb[:, 0, :, :]
        zero_bf = v_off[:, 0, 0, 0:64].bitcast(bf16)

        bank = [ctx.enter_context(nc.psum_tensor(f"bank{i}", [128, 512], f32)) for i in range(8)]
        S_BANK = bank[0:2]

        def unit_bank(kind, n, last):
            if last:
                return bank[{"T": 2 + 4 * (n % 2), "O": 3 + 4 * (n % 2)}.get(kind, 4 + n % 2)]
            return bank[{"T": 2, "O": 3, "X": 4, "W": 5 - n % 2}[kind]]

        FILL_BANK = bank[6:8]
        LG_BANK = bank[0]

        (ld_x, ld_tab, ld_mod_a, ld_mod_b, ld_mod_c, ld_small, ld_lora, ld_lora_all, ld_c, ld_id,
         ld_mask) = (
            sem("ld_x"), sem("ld_tab"), sem("ld_mod_a"), sem("ld_mod_b"), sem("ld_mod_c"),
            sem("ld_small"),
            sem("ld_lora"), sem("ld_lora_all"), sem("ld_c"), sem("ld_id"), sem("ld_mask"))
        ld_raw = [sem("ld_raw0"), sem("ld_raw1")]
        ld_wo = [sem("ld_wo0"), sem("ld_wo1")]
        ld_up = [sem(f"ld_up{i}") for i in range(4)]
        ld_down = [sem(f"ld_down{i}") for i in range(4)]
        v_moved = [sem("v_moved0"), sem("v_moved1")]
        zeroed, silu_c, c_spread, mod_ready, mod_kept, rows_kept, cols_kept = (
            sem("zeroed"), sem("silu_c"), sem("c_spread"), sem("mod_ready"), sem("mod_kept"),
            sem("rows_kept"), sem("cols_kept"))
        stats_done, var_done, std_done, rstd_done = (
            sem("stats_done"), sem("var_done"), sem("std_done"), sem("rstd_done"))
        h_done, squared, ms_done, rms_done, h_normed = (
            sem("h_done"), sem("squared"), sem("ms_done"), sem("rms_done"), sem("h_normed"))
        h_turned, h_hi, h_lo = sem("h_turned"), sem("h_hi"), sem("h_lo")
        x_normed, x_normed_act, shifted, h_scaled, rot_b_half = (
            sem("x_normed"), sem("x_normed_act"), sem("shifted"), sem("h_scaled"),
            sem("rot_b_half"))
        q_swap_done = sem("q_swap_done")

        scored, masked, maxed, exped = sem("scored"), sem("masked"), sem("maxed"), sem("exped")
        p_turned, p_kept, summed = sem("p_turned"), sem("p_kept"), sem("summed")
        o_ready, o_kept, o_turned = sem("o_ready"), sem("o_kept"), sem("o_turned")
        oh_kept, ol_kept, w_ready, w_added = (
            sem("oh_kept"), sem("ol_kept"), sem("w_ready"), sem("w_added"))
        filled = sem("filled")
        fill_kept = [sem("fill_kept0"), sem("fill_kept1")]
        rot_a_done, rot_b_done, rotated = sem("rot_a_done"), sem("rot_b_done"), sem("rotated")
        lora_hi, lora_lo, all_hi, all_lo = (
            sem("lora_hi"), sem("lora_lo"), sem("all_hi"), sem("all_lo"))
        w_hi_done, w_lo_done = sem("w_hi_done"), sem("w_lo_done")
        wo_gated, wo_hi_done, wo_lo_done = sem("wo_gated"), sem("wo_hi_done"), sem("wo_lo_done")
        res_done, z_done, z_turned, z_kept, z_hi, z_lo = (
            sem("res_done"), sem("z_done"), sem("z_turned"), sem("z_kept"), sem("z_hi"), sem("z_lo"))
        logits, lg_done, lg_exp, gating, gates_done, g_turned, gates_kept, g_hi_done = (
            sem("logits"), sem("lg_done"), sem("lg_exp"), sem("gating"), sem("gates_done"),
            sem("g_turned"), sem("gates_kept"), sem("g_hi_done"))
        up_ready, silu_done, mul_done, act_done, act_hi, act_lo = (
            sem("up_ready"), sem("silu_done"), sem("mul_done"), sem("act_done"), sem("act_hi"),
            sem("act_lo"))
        up_w_hi, up_w_lo, down_w_hi, down_w_lo = (
            sem("up_w_hi"), sem("up_w_lo"), sem("down_w_hi"), sem("down_w_lo"))
        down_done, y_scaled, y_done, stored = (
            sem("down_done"), sem("y_scaled"), sem("y_done"), sem("stored"))

        block = ctx.enter_context(nc.Block())

        def steps(eng, order, last_order, step):
            with eng.Fori(0, PAIRS // 2 - 1) as i:
                for slot in range(2):
                    step(i * 2 + slot, slot, i, order, FILL_AT)
            step(PAIRS - 2, 0, PAIRS // 2 - 1, [e for e in order if e[0][0] != "G"], FILL_AT_6)
            step(PAIRS - 1, 1, PAIRS // 2 - 1, last_order, {})

        def fill(p, j):
            at = FILLS_AHEAD + j
            bank_no = p * (FILLS // 2)
            return (FILL_BANK[at % 2][:, :], fill_kept[at % 2], bank_no + (at // 2 + 1),
                    bank_no + (at // 2 + 2), p * FILLS + (at + 1))

        def ahead(kind, n):
            return fill(0, AHEAD.index((kind, n)) - FILLS_AHEAD)

        def per_column(rows, row, n):
            return rows[:, row:row + 1, :].broadcast_to([128, n, D])

        def lo_of_weights(eng, count, slot, m):
            eng.wait_ge(w_hi_done, count)
            cols = slice(m * 256, m * 256 + 256)
            eng.tensor_tensor(out=w_lo[:, slot, :, cols], in0=w_raw[:, slot, :, cols],
                               in1=w_hi[:, slot, :, cols].bitcast(f32), op=ALU.subtract) \
                .then_inc(w_lo_done, 1)
            eng.wait_ge(w_lo_done, count)

        def gate_wo(eng, count, of, slot):
            eng.wait_ge(of[1], of[3])
            eng.tensor_tensor(out=wo_raw[:, slot], in0=wo_raw[:, slot],
                               in1=mod_b[:, 0:1].broadcast_to([128, 2, D]), op=ALU.mult) \
                .then_inc(wo_gated, 1)
            eng.wait_ge(wo_gated, count)

        def place(t, slot):
            head, cols = t // 2 % 2, (t % 2) * 512
            if t < 4:
                return q_t[:, slot, head, cols:cols + 512]
            return k_t[:, slot, head, WIN + cols:WIN + cols + 512]

        def raw_up(s):
            return w_raw[:, s % 2, s // 2, 0:UPW]

        def raw_down(s):
            return wo_raw[:, s % 2, s // 2]

        @block.sync
        def _(sp):
            sp.dma_start(x_sb[:, :, :], x.rearrange("(b p) d -> p b d", p=128)).then_inc(ld_x, 16)
            sp.dma_start(wm_sb[:, :, 0:2 * D], w_mod[:, :, 0:2 * D]).then_inc(ld_mod_a, 16)

            def load_pair(p, slot):
                sp.dma_start(w_raw[:, slot], w_qkv[bass.ds(p, 1)].rearrange("o p k n -> (o p) k n")) \
                    .then_inc(ld_raw[slot], 16)

            def load_wo(p, slot):
                sp.dma_start(wo_raw[:, slot], w_o[bass.ds(p, 1)].rearrange("o p h n -> (o p) h n")) \
                    .then_inc(ld_wo[slot], 16)

            def load_lora(n):
                sp.dma_start(lora_raw[:, :], lora_pairs[bass.ds(n, 1)].rearrange("o r n -> (o r) n")) \
                    .then_inc(ld_lora, 16)

            def move_values(slot):
                sp.dma_start(v_off[0:64, slot, 1:NB], v_sb[64:128, slot, 0:NB - 1]) \
                    .then_inc(v_moved[slot], 16)
                sp.dma_start(v_off[64:128, slot, :], v_sb[0:64, slot, :]).then_inc(v_moved[slot], 16)

            load_lora(0)
            sp.dma_start(wm_sb[:, :, 3 * D:5 * D], w_mod[:, :, 3 * D:5 * D]).then_inc(ld_mod_b, 16)
            load_pair(0, 0)
            for at in (2 * D, 5 * D):
                sp.dma_start(wm_sb[:, :, at:at + D], w_mod[:, :, at:at + D]).then_inc(ld_mod_c, 16)
            sp.dma_start(id_sb[:, :], ident).then_inc(ld_id, 16)
            for dst, src in ((nw_sb, norm_w), (tie_sb, tie), (gw_sb, gate_w)):
                sp.dma_start(dst, src).then_inc(ld_small, 16)
            for dst, src in ((cos_sb[:, :], cos_t), (sin_sb[:, :], sin_t),
                             (sin_swapped[0:64], sin_t[64:128]), (sin_swapped[64:128], sin_t[0:64])):
                sp.dma_start(dst, src).then_inc(ld_tab, 16)
            sp.wait_ge(lora_lo, 1)
            load_lora(1)
            load_wo(0, 0)
            load_pair(1, 1)
            load_wo(1, 1)
            sp.dma_start(mask_sb[:, :, :], mask).then_inc(ld_mask, 16)
            sp.wait_ge(lora_lo, 2)
            load_lora(2)
            _, kept, _, value, _ = ahead("V", 3)
            sp.wait_ge(kept, value)
            sp.wait_ge(mod_ready, 3)
            move_values(0)

            def step(p, slot, half, order, at):
                kinds = {k for k, _ in order}
                if "G" in kinds:
                    sp.wait_ge(lora_lo, p + 3)
                    load_lora(p + 3)
                    sp.wait_ge(w_lo_done, p * 3 + 3)
                    load_pair(p + 2, slot)
                    sp.wait_ge(wo_lo_done, p + 1)
                    load_wo(p + 2, slot)
                if "V" in kinds:
                    _, kept, _, value, _ = fill(p, at["V", 3])
                    sp.wait_ge(kept, value)
                    move_values(1 - slot)

            steps(sp, PE_STEP, [], step)

            def load_up(c, s):
                sp.dma_start(raw_up(s), w_up[bass.ds(c, 1)].rearrange("o p n -> (o p) n")) \
                    .then_inc(ld_up[s], 16)

            def load_down(c, s):
                sp.dma_start(raw_down(s), w_down[bass.ds(c, 1)].rearrange("o p n -> (o p) n")) \
                    .then_inc(ld_down[s], 16)

            sp.wait_ge(w_lo_done, 3 * PAIRS)
            sp.wait_ge(wo_lo_done, PAIRS)
            for s in range(4):
                load_up(s, s)
                load_down(s, s)

            def next_chunk(n, c, s):
                sp.wait_ge(up_w_lo, n - 3)
                load_up(c, s)
                sp.wait_ge(down_w_lo, n - 3)
                load_down(c, s)

            with sp.Fori(1, 3) as i:
                for s in range(4):
                    next_chunk(i * 4 + s, i * 4 + s, s)
            for s in range(4):
                next_chunk(12 + s, (12 + s) % CH, s)
            with sp.Fori(4, 7) as i:
                for s in range(4):
                    next_chunk(i * 4 + s, i * 4 + (s - CH), s)
            for j in range(NB // 2):
                sp.wait_ge(y_done, j + 1)
                sp.dma_start(out[j * 256:j * 256 + 256].rearrange("(b p) d -> p b d", p=128),
                             y_out[:, 2 * j:2 * j + 2]).then_inc(stored, 16)
            sp.wait_ge(stored, 16 * NB // 2)

        @block.gpsimd
        def _(pool):
            pool.memset(k_t[:, :, :, 0:WIN], 0.0).then_inc(zeroed, 1)
            pool.wait_ge(zeroed, 1)

            def lo_of_wo(count, slot):
                pool.wait_ge(wo_hi_done, count)
                pool.tensor_tensor(out=wo_lo[:, slot], in0=wo_raw[:, slot],
                                   in1=wo_hi[:, slot].bitcast(f32), op=ALU.subtract) \
                    .then_inc(wo_lo_done, 1)
                pool.wait_ge(wo_lo_done, count)

            def rotate_b(count, half_count, of, free, i, cols):
                pool.wait_ge(of[1], of[3])
                pool.wait_ge(rotated, free)
                pool.tensor_tensor(out=rot_b[0:64, i % 2], in0=qk_raw[64:128, i % 4],
                                   in1=sin_sb[64:128, cols], op=ALU.mult).then_inc(rot_b_half, 1)
                pool.wait_ge(rot_b_half, half_count)
                pool.tensor_tensor(out=rot_b[64:128, i % 2], in0=qk_raw[0:64, i % 4],
                                   in1=sin_sb[0:64, cols], op=ALU.mult).then_inc(rot_b_done, 1)
                pool.wait_ge(rot_b_done, count)

            pool.wait_ge(all_hi, 1)
            pool.tensor_tensor(out=lora_c[64:96], in0=lora_all_raw[64:96],
                               in1=lora_c[64:96].bitcast(f32), op=ALU.subtract).then_inc(all_lo, 1)
            pool.wait_ge(all_lo, 1)
            pool.wait_ge(lora_hi, 1)
            pool.tensor_tensor(out=lora_p[32:64], in0=lora_raw[32:64],
                               in1=lora_p[32:64].bitcast(f32), op=ALU.subtract).then_inc(lora_lo, 1)
            pool.wait_ge(lora_lo, 1)
            for m in range(3):
                lo_of_weights(pool, m + 1, 0, m)
            pool.wait_ge(mod_ready, 3)
            pool.memset(v_off[0:64, :, 0, :], 0.0).then_inc(zeroed, 1)
            pool.wait_ge(zeroed, 2)
            pool.wait_ge(ld_tab, 64)
            for i, t in enumerate(PARTS):
                of, cols = ahead("Q", i), slice((t % 2) * 512, (t % 2) * 512 + 512)
                if i % 2:
                    rotate_b(i + 1, (i + 1) // 2, of, i + 3, i, cols)
                else:
                    pool.wait_ge(q_swap_done, i // 2 + 1)
                    pool.wait_ge(rotated, i + 3)
                    pool.tensor_tensor(out=rot_b[:, 0], in0=q_swapped[:, i // 2 % 2],
                                       in1=sin_swapped[:, cols], op=ALU.mult).then_inc(rot_b_done, 1)
                    pool.wait_ge(rot_b_done, i + 1)
            lo_of_wo(1, 0)
            pool.wait_ge(lora_hi, 3)
            pool.tensor_tensor(out=lora_p[32:64], in0=lora_raw[32:64],
                               in1=lora_p[32:64].bitcast(f32), op=ALU.subtract).then_inc(lora_lo, 1)
            pool.wait_ge(lora_lo, 3)

            def step(p, slot, half, order, at):
                for kind, n in order:
                    if kind == "QB":
                        half = PARTS[n] % 2 * 512
                        rotate_b(p * 8 + (9 + n), p * 8 + (5 + n), fill(p, at["Q", n]),
                                 p * 8 + (11 + n), n, slice(half, half + 512))
                    if kind == "GL":
                        lo_of_weights(pool, p * 3 + (7 + n), slot, n)
                    if kind == "PG":
                        gate_wo(pool, p + 2, fill(p, at["P", 0]), 1 - slot)
                    if kind == "PL":
                        lo_of_wo(p + 2, 1 - slot)

            steps(pool, POOL_STEP, [], step)
            pool.wait_ge(scored, 4 * PAIRS - 3)
            pool.memset(zero_bf, 0.0).then_inc(zeroed, 1)
            pool.wait_ge(zeroed, 3)

            def lo_of_up(count, s):
                pool.wait_ge(up_w_hi, count)
                pool.tensor_tensor(out=w_lo[:, s % 2, 0, 0:UPW], in0=raw_up(s),
                                   in1=w_hi[:, s % 2, 0, 0:UPW].bitcast(f32), op=ALU.subtract) \
                    .then_inc(up_w_lo, 1)
                pool.wait_ge(up_w_lo, count)

            def lo_of_down(count, s):
                pool.wait_ge(down_w_hi, count)
                pool.tensor_tensor(out=wo_lo[:, s % 2, 0], in0=raw_down(s),
                                   in1=wo_hi[:, s % 2, 0].bitcast(f32), op=ALU.subtract) \
                    .then_inc(down_w_lo, 1)
                pool.wait_ge(down_w_lo, count)

            for s in range(2):
                lo_of_up(1 + s, s)
            with pool.Fori(0, CH // 2 - 1) as i:
                for s in range(4):
                    lo_of_up(i * 4 + (3 + s), (2 + s) % 4)
                    lo_of_down(i * 4 + (1 + s), s)
            for s in range(2):
                lo_of_up(2 * CH - 1 + s, 2 + s)
                lo_of_down(2 * CH - 3 + s, s)
            for s in range(2):
                lo_of_down(2 * CH - 1 + s, 2 + s)

        @block.scalar
        def _(act):
            act.dma_start(c_sb, c_col).then_inc(ld_c, 16)
            act.dma_start(lora_all_raw, lora_all).then_inc(ld_lora_all, 16)
            act.sem_inc(exped, 2)
            act.sem_inc(p_turned, 2)
            act.sem_inc(fill_kept[0], 1)
            act.sem_inc(fill_kept[1], 1)
            act.sem_inc(p_kept, 1)
            act.sem_inc(o_kept, 1)

            def split_lora_hi(n, used):
                act.wait_ge(ld_lora, n * 16 + 16)
                if used is not None:
                    act.wait_ge(filled, used)
                act.activation(lora_p[:, :], lora_raw[:, :], ACT.Copy).then_inc(lora_hi, 1)

            act.wait_ge(ld_c, 16)
            act.activation(sil_c, c_sb, ACT.Silu).then_inc(silu_c, 1)
            act.wait_ge(zeroed, 1)
            act.activation(small[:, 84:85], k_t[:, 0, 0, 0:1], ACT.Sqrt)
            act.wait_ge(ld_lora_all, 16)
            act.activation(lora_c[:, :], lora_all_raw, ACT.Copy).then_inc(all_hi, 1)
            split_lora_hi(0, None)
            act.wait_ge(var_done, 1)
            act.activation(rstd, tmp8, ACT.Sqrt).then_inc(std_done, 1)
            act.wait_ge(mod_ready, 1)
            act.activation(mod_a[:, 0], bank[0][:, 0:D], ACT.Copy).then_inc(rows_kept, 1)
            act.activation(mod_a[:, 1], bank[0][:, D:2 * D], ACT.Identity, bias=1.0) \
                .then_inc(rows_kept, 1)
            act.wait_ge(shifted, 1)
            for b in range(4, NB):
                act.activation(res[:, b], x_sb[:, b], ACT.Identity, bias=shift[:, b:b + 1],
                               scale=rstd[:, b:b + 1]).then_inc(x_normed_act, 1)

            def hi_of_weights(of, slot, m):
                act.wait_ge(of[1], of[3])
                cols = slice(m * 256, m * 256 + 256)
                act.activation(w_hi[:, slot, :, cols], w_raw[:, slot, :, cols], ACT.Copy) \
                    .then_inc(w_hi_done, 1)

            def squares(half):
                act.wait_ge(h_done, 1 + half)
                for b in range(4 * half, 4 * half + 4):
                    act.activation(sq_out[:, b], res[:, b], ACT.Square,
                                   accum_out=ssq[:, b:b + 1]).then_inc(squared, 1)

            def root(half):
                act.wait_ge(ms_done, 2 * half + 1)
                at = slice(4 * half, 4 * half + 4)
                act.activation(rms[:, at], tmp8[:, at], ACT.Sqrt).then_inc(rms_done, 1)

            squares(0)
            root(0)
            hi_of_weights(ahead("G", 0), 0, 0)
            squares(1)
            hi_of_weights(ahead("G", 1), 0, 1)
            root(1)
            hi_of_weights(ahead("G", 2), 0, 2)

            def keep(of, dst, scale):
                act.wait_ge(filled, of[4])
                act.activation(dst, of[0], ACT.Copy, scale=scale).then_inc(of[1], 1)

            def keep_projection(of, i, free):
                act.wait_ge(rotated, free)
                keep(of, qk_raw[:, i % 4], SCALE if PARTS[i] < 4 else 1.0)

            def swap(of, i):
                act.wait_ge(of[1], of[3])
                if i >= 4:
                    act.wait_ge(rot_b_done, i - 3)
                act.activation(q_swapped[0:64, i // 2 % 2], qk_raw[64:128, i % 4], ACT.Copy)
                act.activation(q_swapped[64:128, i // 2 % 2], qk_raw[0:64, i % 4], ACT.Copy) \
                    .then_inc(q_swap_done, 1)

            def keep_values(of, v, slot):
                keep(of, v_sb[:, slot, 2 * v:2 * v + 2].rearrange("p b d -> p (b d)"), 1.0)

            def hi_of_wo(count, slot):
                act.wait_ge(wo_gated, count)
                act.activation(wo_hi[:, slot], wo_raw[:, slot], ACT.Copy).then_inc(wo_hi_done, 1)

            act.wait_ge(ld_small, 48)
            for n in range(4):
                k, half = n % 2, n // 2
                act.wait_ge(h_turned, n + 1)
                act.activation(hi_t[:, k, half * 512:half * 512 + 512], bank[2 + n][:, :],
                               ACT.Identity, scale=nw_sb[:, k:k + 1]).then_inc(h_hi, 1)
            split_lora_hi(1, 3)
            act.wait_ge(squared, NB)
            for kind, n in AHEAD[3:]:
                if kind == "Q":
                    i = n
                    act.wait_ge(rotated, i + 1)
                    keep(ahead(kind, n), qk_raw[:, i % 4], SCALE if PARTS[n] < 4 else 1.0)
                    if i % 2 == 0:
                        swap(ahead(kind, n), i)
                if kind == "V":
                    keep_values(ahead(kind, n), n, 0)
            for m in range(3):
                hi_of_weights(ahead("G1", m), 1, m)
            hi_of_wo(1, 0)
            split_lora_hi(2, FILLS_AHEAD)

            def root_after(half):
                act.wait_ge(var_done, 2 + half)
                at = slice(4 * half, 4 * half + 4)
                act.activation(rstd[:, at], tmp8[:, at], ACT.Sqrt).then_inc(std_done, 1)

            def keep_z(n):
                k, half = n % 2, n // 2
                cols = slice(half * 512, half * 512 + 512)
                act.wait_ge(z_turned, n + 1)
                act.activation(h2_t[:, k, cols], FILL_BANK[k][:, :], ACT.Identity,
                               bias=mod_c[:, 0, k:k + 1], scale=mod_c[:, 1, k:k + 1]) \
                    .then_inc(z_kept, 1)

            def hi_of_z(n):
                k, half = n % 2, n // 2
                cols = slice(half * 512, half * 512 + 512)
                act.activation(hi_t[:, k, cols], FILL_BANK[k][:, :], ACT.Identity,
                               bias=mod_c[:, 0, k:k + 1], scale=mod_c[:, 1, k:k + 1]) \
                    .then_inc(z_hi, 1)

            def hi_of_up(count, s):
                act.wait_ge(ld_up[s], count)
                act.activation(w_hi[:, s % 2, 0, 0:UPW], raw_up(s), ACT.Copy).then_inc(up_w_hi, 1)

            def step(p, slot, half, order, at):
                act.activation(small[:, 84:85], id_sb[:, 0:1], ACT.Exp)
                if at:
                    act.wait_ge(scored, p * 4 + 1)
                for kind, n in order:
                    unit = p * 4 + n
                    if kind == "Q":
                        keep_projection(fill(p, at[kind, n]), n, p * 8 + (9 + n))
                    if kind == "V":
                        keep_values(fill(p, at[kind, n]), n, 1 - slot)
                    if kind == "PH":
                        hi_of_wo(p + 2, 1 - slot)
                    if kind == "GH":
                        hi_of_weights(fill(p, at["G", n]), slot, n)
                    if kind == "GR":
                        last_one = max(j for e, j in at.items() if e[0] in "GP")
                        split_lora_hi(p + 3, fill(p, last_one)[4])
                    if kind == "E":
                        act.wait_ge(maxed, unit + 1)
                        for b in range(4):
                            last = act.activation(probs[:, n % 2, b * 128:b * 128 + 128],
                                                  probs[:, n % 2, b * 128:b * 128 + 128], ACT.Exp,
                                                  bias=neg_max[:, n % 2, b:b + 1],
                                                  accum_out=row_sum[:, n % 2, b:b + 1])
                        last.then_inc(exped, 1)
                    if kind == "T":
                        act.wait_ge(p_turned, unit + 3)
                        act.activation(probs_t[:, n % 2], unit_bank("T", n, not at)[:, :], ACT.Copy) \
                            .then_inc(p_kept, 1)
                    if kind == "O":
                        act.wait_ge(o_ready, unit + 1)
                        act.wait_ge(summed, unit + 1)
                        result = unit_bank("O", n, not at)
                        for b in range(4):
                            last = act.activation(o_norm[:, n % 2, b * 128:b * 128 + 128],
                                                  result[:, b * 128:b * 128 + 128], ACT.Identity,
                                                  scale=row_inv[:, n % 2, b:b + 1])
                        last.then_inc(o_kept, 1)
                    if kind == "X":
                        act.wait_ge(o_turned, unit + 1)
                        act.activation(o_hi[:, n % 2], unit_bank("X", n, not at)[:, :], ACT.Copy) \
                            .then_inc(oh_kept, 1)
                    if kind == "U":
                        hi_of_up(16, n)
                    if kind == "ZR":
                        root_after(n)
                    if kind == "ZH":
                        keep_z(n)
                        hi_of_z(n)

            steps(act, ACT_STEP, ACT_LAST, step)

            def hi_of_down(count, s):
                act.wait_ge(ld_down[s], count)
                act.activation(wo_hi[:, s % 2, 0], raw_down(s), ACT.Copy).then_inc(down_w_hi, 1)

            def silu(c, slot):
                act.wait_ge(up_ready, c + 1)
                act.activation(qk_raw[:, slot], bank[2 + 2 * slot][:, :], ACT.Silu) \
                    .then_inc(silu_done, 1)

            def hi(c, slot):
                act.wait_ge(act_done, c + 1)
                act.activation(o_hi[:, slot], probs[:, slot], ACT.Copy).then_inc(act_hi, 1)

            root_after(1)
            for c in range(2):
                silu(c, c)
                hi_of_up(16, 2 + c)
            for n in range(2, 4):
                keep_z(n)
            for n in range(2, 4):
                hi_of_z(n)
            for c in range(2):
                hi(c, c)
                hi_of_down(16, c)
            act.wait_ge(lg_done, 1)
            act.activation(sc, lg, ACT.Exp).then_inc(lg_exp, 1)
            silu(2, 0)
            hi_of_up(32, 0)
            act.wait_ge(gates_done, 1)
            act.activation(g_hi, t64, ACT.Copy).then_inc(g_hi_done, 1)
            for n in range(2):
                act.wait_ge(g_turned, n + 1)
                act.activation(gate_t[:, n], FILL_BANK[n][0:GK, :], ACT.Copy) \
                    .then_inc(gates_kept, 1)
            act.wait_ge(down_done, 1)
            hi(2, 0)
            hi_of_down(16, 2)

            def chunk(c, s, up_count, down_count):
                silu(c, s % 2)
                if up_count is not None:
                    hi_of_up(up_count, (s + 2) % 4)
                act.wait_ge(act_done, c + 1)
                act.wait_ge(down_done, c - 1)
                hi(c, s % 2)
                hi_of_down(down_count, s)

            chunk(3, 3, 32, 16)
            with act.Fori(1, CH // 2 - 1) as i:
                for s in range(4):
                    chunk(i * 4 + s, s, i * 16 + (16 + 16 * ((s + 2) // 4)), i * 16 + 16)
            for s in range(4):
                chunk(2 * CH - 4 + s, s, 16 * CH // 2 if s < 2 else None, 16 * CH // 2)

        @block.vector
        def _(dve):
            dve.sem_inc(ol_kept, 1)
            dve.sem_inc(w_added, 2)
            dve.sem_inc(masked, 2)
            dve.sem_inc(rotated, 4)

            def mean_and_variance(source, blocks, base):
                for b in blocks:
                    dve.bn_stats(stats[:, b], source[:, b]).then_inc(stats_done, 1)
                dve.wait_ge(stats_done, base + len(blocks))
                for b in blocks:
                    dve.bn_aggr(mean_var[:, b], stats[:, b]).then_inc(stats_done, 1)
                dve.wait_ge(stats_done, base + 2 * len(blocks))
                at = slice(blocks[0], blocks[-1] + 1)
                dve.tensor_scalar(out=tmp8[:, at], in0=mean_var[:, at, 1], scalar1=LN_EPS,
                                  scalar2=None, op0=ALU.add).then_inc(var_done, 1)

            def invert(at, count):
                dve.wait_ge(std_done, count)
                dve.reciprocal(rstd[:, at], rstd[:, at]).then_inc(rstd_done, 1)
                dve.wait_ge(rstd_done, count)

            def normalise(dst, source, blocks, done):
                for b in blocks:
                    dve.tensor_scalar(out=dst[:, b], in0=source[:, b],
                                      scalar1=mean_var[:, b, 0:1], scalar2=rstd[:, b:b + 1],
                                      op0=ALU.subtract, op1=ALU.mult).then_inc(done, 1)

            dve.wait_ge(silu_c, 1)
            dve.tensor_copy(c_rep, sil_c.rearrange("p (k o) -> p k o", o=1)
                            .broadcast_to([128, KD, 128])).then_inc(c_spread, 1)
            dve.wait_ge(ld_x, 16)
            mean_and_variance(x_sb, range(NB), 0)

            def split_lora_lo(n):
                dve.wait_ge(lora_hi, n + 1)
                dve.tensor_tensor(out=lora_p[32:64], in0=lora_raw[32:64],
                                  in1=lora_p[32:64].bitcast(f32), op=ALU.subtract) \
                    .then_inc(lora_lo, 1)

            invert(slice(0, NB), 1)
            dve.scalar_tensor_tensor(out=shift, in0=mean_var[:, :, 0], scalar=-1.0, in1=rstd,
                                     op0=ALU.mult, op1=ALU.mult).then_inc(shifted, 1)
            normalise(res, x_sb, range(4), x_normed)
            dve.wait_ge(rows_kept, 2)
            def fold(of, loaded, slot, m):
                dve.wait_ge(ld_raw[slot], loaded)
                dve.wait_ge(filled, of[4])
                view = w_raw[:, slot, :, m * 256:m * 256 + 256]
                dve.scalar_tensor_tensor(out=view, in0=of[0].rearrange("p (k n) -> p k n", k=KD),
                                         scalar=LORA_SCALE, in1=view, op0=ALU.mult, op1=ALU.add) \
                    .then_inc(of[1], 1)

            def fold_wo(of, loaded, slot):
                dve.wait_ge(ld_wo[slot], loaded)
                dve.wait_ge(filled, of[4])
                view = wo_raw[:, slot]
                dve.scalar_tensor_tensor(out=view, in0=of[0].rearrange("p (h n) -> p h n", h=2),
                                         scalar=LORA_SCALE, in1=view, op0=ALU.mult, op1=ALU.add) \
                    .then_inc(of[1], 1)

            def rotate_a(of, free, i):
                half = PARTS[i] % 2 * 512
                dve.wait_ge(of[1], of[3])
                dve.wait_ge(rotated, free)
                dve.tensor_tensor(out=rot_a[:, i % 2], in0=qk_raw[:, i % 4],
                                  in1=cos_sb[:, half:half + 512], op=ALU.mult) \
                    .then_inc(rot_a_done, 1)

            def rotate(count, i, slot):
                dve.wait_ge(rot_a_done, count)
                dve.wait_ge(rot_b_done, count)
                dve.tensor_tensor(out=place(PARTS[i], slot), in0=rot_a[:, i % 2], in1=rot_b[:, i % 2],
                                  op=ALU.add).then_inc(rotated, 1)

            def scale_h(half):
                view = res[:, 4 * half:4 * half + 4]
                dve.wait_ge((x_normed, x_normed_act)[half], 4)
                dve.tensor_tensor(out=view, in0=view, in1=per_column(mod_a, 1, 4), op=ALU.mult) \
                    .then_inc(h_scaled, 1)

            def shift_h(half):
                view = res[:, 4 * half:4 * half + 4]
                dve.wait_ge(h_scaled, 1 + half)
                dve.tensor_tensor(out=view, in0=view, in1=per_column(mod_a, 0, 4), op=ALU.add) \
                    .then_inc(h_done, 1)

            def mean_square(half):
                at = slice(4 * half, 4 * half + 4)
                dve.wait_ge(squared, 4 * half + 4)
                dve.tensor_scalar(out=tmp8[:, at], in0=ssq[:, at], scalar1=1.0 / D, scalar2=RMS_EPS,
                                  op0=ALU.mult, op1=ALU.add).then_inc(ms_done, 1)

            def normalise_h(half):
                at = slice(4 * half, 4 * half + 4)
                dve.wait_ge(rms_done, 1 + half)
                dve.reciprocal(rms[:, at], rms[:, at]).then_inc(ms_done, 1)
                dve.wait_ge(ms_done, 2 * half + 2)
                for b in range(4 * half, 4 * half + 4):
                    dve.tensor_scalar(out=h_norm[:, b], in0=res[:, b], scalar1=rms[:, b:b + 1],
                                      scalar2=None, op0=ALU.mult).then_inc(h_normed, 1)

            scale_h(0)
            shift_h(0)
            scale_h(1)
            fold(ahead("G", 0), 16, 0, 0)
            mean_square(0)
            shift_h(1)
            fold(ahead("G", 1), 16, 0, 1)
            normalise_h(0)
            dve.wait_ge(mod_ready, 2)
            dve.tensor_copy(mod_c[:, 0], bank[5][:, 0:KD])
            dve.tensor_scalar(out=mod_c[:, 1], in0=bank[5][:, KD:2 * KD], scalar1=1.0, scalar2=None,
                              op0=ALU.add).then_inc(cols_kept, 1)
            mean_square(1)
            fold(ahead("G", 2), 16, 0, 2)
            normalise_h(1)

            def lo_of_h(n):
                k, half = n % 2, n // 2
                cols = slice(half * 512, half * 512 + 512)
                dve.wait_ge(h_hi, n + 1)
                dve.scalar_tensor_tensor(out=lo_t[:, k, cols], in0=bank[2 + n][:, :],
                                         scalar=nw_sb[:, k:k + 1],
                                         in1=hi_t[:, k, cols].bitcast(f32), op0=ALU.mult,
                                         op1=ALU.subtract).then_inc(h_lo, 1)

            for n in range(4):
                lo_of_h(n)
            split_lora_lo(1)
            dve.wait_ge(mod_ready, 3)
            gates = mod_b[:, :].rearrange("p a d -> p (a d)")
            dve.tensor_scalar(out=sgn_g, in0=bank[1][:, :], scalar1=0.0, scalar2=2.0,
                              op0=ALU.is_ge, op1=ALU.mult).then_inc(mod_kept, 1)
            dve.wait_ge(mod_kept, 1)
            dve.scalar_tensor_tensor(out=gates, in0=sgn_g, scalar=-1.0, in1=bank[1][:, :],
                                     op0=ALU.add, op1=ALU.mult).then_inc(mod_kept, 1)
            dve.wait_ge(mod_kept, 2)
            dve.tensor_scalar(out=gates, in0=gates, scalar1=0.25, scalar2=None,
                              op0=ALU.max).then_inc(mod_kept, 1)
            dve.wait_ge(mod_kept, 3)
            dve.scalar_tensor_tensor(out=gates, in0=sgn_g, scalar=-1.0, in1=gates, op0=ALU.add,
                                     op1=ALU.mult).then_inc(mod_kept, 1)
            dve.wait_ge(mod_kept, 4)
            dve.wait_ge(ld_mask, 16)
            dve.wait_ge(ld_tab, 64)
            for i in range(8):
                if i == 7:
                    fold_wo(ahead("P", 0), 16, 0)
                if i >= 2:
                    rotate(i - 1, i - 2, 0)
                if i == 7:
                    fold(ahead("G1", 0), 16, 1, 0)
                rotate_a(ahead("Q", i), i + 3, i)
                view = res[:, 4 * (i // 2 % 2):4 * (i // 2 % 2) + 4]
                if i in (0, 2):
                    dve.tensor_tensor(out=view, in0=view, in1=per_column(mod_b, 0, 4),
                                      op=ALU.mult).then_inc(res_done, 1)
                if i in (1, 3):
                    dve.wait_ge(res_done, i)
                    dve.tensor_tensor(out=view, in0=view, in1=x_sb[:, 4 * (i // 2):4 * (i // 2) + 4],
                                      op=ALU.add).then_inc(res_done, 1)
            fold(ahead("G1", 1), 16, 1, 1)
            gate_wo(dve, 1, ahead("P", 0), 0)
            fold(ahead("G1", 2), 16, 1, 2)
            for m in range(3):
                lo_of_weights(dve, m + 4, 1, m)
            dve.wait_ge(res_done, 4)

            def variance_after(half):
                blocks = range(4 * half, 4 * half + 4)
                dve.wait_ge(w_added, 4 * PAIRS + 2 * half)
                mean_and_variance(res, blocks, 2 * NB + 8 * half)

            def normalise_after(half):
                blocks = range(4 * half, 4 * half + 4)
                invert(slice(4 * half, 4 * half + 4), 2 + half)
                normalise(z_sb, res, blocks, z_done)

            def lo_of_z(n):
                k, half = n % 2, n // 2
                cols = slice(half * 512, half * 512 + 512)
                dve.wait_ge(z_hi, n + 1)
                dve.tensor_tensor(out=lo_t[:, k, cols], in0=h2_t[:, k, cols],
                                  in1=hi_t[:, k, cols].bitcast(f32), op=ALU.subtract) \
                    .then_inc(z_lo, 1)

            def step(p, slot, half, order, at):
                if at:
                    dve.wait_ge(scored, p * 4 + 1)
                for kind, n in order:
                    unit = p * 4 + n
                    if kind == "M":
                        dve.wait_ge(scored, unit + 1)
                        dve.wait_ge(p_turned, unit + 1)
                        dve.tensor_tensor(out=probs[:, n % 2], in0=S_BANK[n % 2][:, :],
                                          in1=mask_sb[:, n // 2], op=ALU.add).then_inc(masked, 1)
                        dve.wait_ge(masked, unit + 3)
                        dve.tensor_reduce(out=neg_max[:, n % 2],
                                          in_=probs[:, n % 2].rearrange("p (b k) -> p b k", b=4),
                                          axis=AX.X, op=ALU.max, negate=True).then_inc(maxed, 1)
                    if kind == "N":
                        dve.wait_ge(exped, unit + 3)
                        dve.reciprocal(row_inv[:, n % 2], row_sum[:, n % 2]).then_inc(summed, 1)
                    if kind == "XL":
                        dve.wait_ge(oh_kept, unit + 1)
                        dve.tensor_tensor(out=o_lo[:, n % 2], in0=unit_bank("X", n, not at)[:, :],
                                          in1=o_hi[:, n % 2].bitcast(f32), op=ALU.subtract) \
                            .then_inc(ol_kept, 1)
                    if kind == "W":
                        dve.wait_ge(w_ready, unit + 1)
                        dve.wait_ge(w_added, unit + 2)
                        view = res[:, 2 * n:2 * n + 2].rearrange("p b d -> p (b d)")
                        dve.tensor_tensor(out=view, in0=unit_bank("W", n, not at)[:, :], in1=view,
                                          op=ALU.add).then_inc(w_added, 1)
                    if kind == "QA":
                        rotate_a(fill(p, at["Q", n]), p * 8 + (11 + n), n)
                    if kind == "QR":
                        rotate(p * 8 + (9 + n), n, 1 - slot)
                    if kind == "QC":
                        rotate(p * 8 + (1 + n), n, slot)
                    if kind == "P":
                        fold_wo(fill(p, at["P", 0]), half * 16 + (16 + 16 * slot), 1 - slot)
                    if kind == "G":
                        fold(fill(p, at["G", n]), half * 16 + 32, slot, n)
                    if kind == "GT":
                        split_lora_lo(p + 3)
                    if kind == "ZV":
                        variance_after(n)
                    if kind == "ZN":
                        normalise_after(n)
                    if kind == "ZL":
                        lo_of_z(n)

            steps(dve, DVE_STEP, DVE_LAST, step)

            variance_after(1)
            normalise_after(1)

            def multiply(c, slot):
                dve.wait_ge(silu_done, c + 1)
                if isinstance(c, int) and c < SHARED:
                    dve.tensor_tensor(out=probs[:, slot], in0=qk_raw[:, slot],
                                      in1=bank[3 + 2 * slot][:, :], op=ALU.mult).then_inc(act_done, 1)
                else:
                    dve.tensor_tensor(out=rot_a[:, slot], in0=qk_raw[:, slot],
                                      in1=bank[3 + 2 * slot][:, :], op=ALU.mult).then_inc(mul_done, 1)
                    dve.wait_ge(mul_done, c + (1 - SHARED))
                    dve.tensor_tensor(out=probs[:, slot], in0=rot_a[:, slot],
                                      in1=bank[6 + slot][:, :], op=ALU.mult).then_inc(act_done, 1)

            def lo(c, slot):
                dve.wait_ge(act_hi, c + 1)
                dve.tensor_tensor(out=o_lo[:, slot], in0=probs[:, slot],
                                  in1=o_hi[:, slot].bitcast(f32), op=ALU.subtract) \
                    .then_inc(act_lo, 1)

            for c in range(2):
                multiply(c, c)
            for c in range(2):
                lo(c, c)

            def by_block(view):
                return view.rearrange("p (b e) -> p b e", e=E)

            def spread(view):
                return view.rearrange("p (b o) -> p b o", o=1).broadcast_to([128, NB, E])

            done = [0]

            def then_wait(ins):
                done[0] += 1
                ins.then_inc(gating, 1)
                dve.wait_ge(gating, done[0])

            dve.wait_ge(logits, 1)
            then_wait(dve.tensor_reduce(out=m8, in_=by_block(LG_BANK[:, 0:NB * E]), axis=AX.X,
                                        op=ALU.max))
            dve.tensor_tensor(out=by_block(lg), in0=by_block(LG_BANK[:, 0:NB * E]), in1=spread(m8),
                              op=ALU.subtract).then_inc(lg_done, 1)
            dve.wait_ge(lg_exp, 1)
            then_wait(dve.tensor_reduce(out=m8, in_=by_block(sc), axis=AX.X, op=ALU.add))
            then_wait(dve.reciprocal(m8, m8))
            then_wait(dve.tensor_tensor(out=by_block(sc), in0=by_block(sc), in1=spread(m8),
                                        op=ALU.mult))
            for left, one_hot in ((sc, oh1), (lg, oh2)):
                then_wait(dve.tensor_reduce(out=m8, in_=by_block(left), axis=AX.X, op=ALU.max))
                then_wait(dve.tensor_tensor(out=by_block(t64), in0=by_block(left), in1=spread(m8),
                                            op=ALU.is_equal))
                then_wait(dve.tensor_tensor(out=t64, in0=t64, in1=tie_sb, op=ALU.mult))
                then_wait(dve.tensor_reduce(out=m8, in_=by_block(t64), axis=AX.X, op=ALU.max))
                then_wait(dve.tensor_tensor(out=by_block(one_hot), in0=by_block(t64),
                                            in1=spread(m8), op=ALU.is_equal))
                if left is sc:
                    then_wait(dve.scalar_tensor_tensor(out=lg, in0=oh1, scalar=-2.0, in1=sc,
                                                       op0=ALU.mult, op1=ALU.add))
            then_wait(dve.tensor_tensor(out=oh1, in0=oh1, in1=oh2, op=ALU.add))
            then_wait(dve.tensor_tensor(out=sc, in0=sc, in1=oh1, op=ALU.mult))
            then_wait(dve.tensor_reduce(out=m8, in_=by_block(sc), axis=AX.X, op=ALU.add))
            then_wait(dve.reciprocal(m8, m8))
            dve.tensor_tensor(out=by_block(t64), in0=by_block(sc), in1=spread(m8), op=ALU.mult) \
                .then_inc(gates_done, 1)
            dve.wait_ge(g_hi_done, 1)
            high = by_block(g_hi.bitcast(f32))
            dve.tensor_copy(g_cat[:, :, 0:E], high)
            dve.tensor_tensor(out=g_cat[:, :, E:2 * E], in0=by_block(t64), in1=high,
                              op=ALU.subtract)
            dve.memset(g_cat[:, :, 2 * E:GK], 1.0).then_inc(gates_done, 1)

            for n in range(2, 4):
                lo_of_z(n)

            def chunk(c, slot):
                multiply(c, slot)
                lo(c, slot)

            def output(half):
                dve.wait_ge(down_done, CH * (half + 1))
                for j in range(2):
                    b = 4 * half + 2 * j
                    dve.tensor_tensor(out=y_out[:, b:b + 2],
                                      in0=bank[j][:, :].rearrange("p (b d) -> p b d", b=2),
                                      in1=per_column(mod_b, 1, 2), op=ALU.mult).then_inc(y_scaled, 1)
                for j in range(2):
                    b = 4 * half + 2 * j
                    dve.wait_ge(y_scaled, 2 * half + 1 + j)
                    dve.tensor_tensor(out=y_out[:, b:b + 2], in0=y_out[:, b:b + 2],
                                      in1=res[:, b:b + 2], op=ALU.add).then_inc(y_done, 1)

            for c in range(2, 4):
                chunk(c, c % 2)
            with dve.Fori(2, CH // 2 + 1) as i:
                for slot in range(2):
                    chunk(i * 2 + slot, slot)
            output(0)
            with dve.Fori(CH // 2 + 1, CH) as i:
                for slot in range(2):
                    chunk(i * 2 + slot, slot)
            output(1)

        @block.tensor
        def _(pe):
            def three(dst, lhs, rhs, contraction, **more):
                n = 0
                for at in contraction:
                    for a, b in ((0, 0), (0, 1), (1, 0)):
                        n += 1
                        last = pe.matmul(dst, lhs(a, at), rhs(b, at), start=n == 1,
                                         stop=n == 3 * len(contraction), **more)
                return last

            t_parts, w_parts, wo_parts, o_parts = (
                (hi_t, lo_t), (w_hi, w_lo), (wo_hi, wo_lo), (o_hi, o_lo))

            def modulation(dst, col, n):
                for k in range(KD):
                    last = pe.matmul(dst, c_rep[:, k], wm_sb[:, k, col:col + n], start=k == 0,
                                     stop=k == KD - 1)
                return last

            def lora(of, loaded, m):
                pe.wait_ge(lora_lo, loaded)
                pe.wait_ge(of[1], of[2])
                for k in range(KD):
                    last = pe.matmul(of[0][:, k * 256:k * 256 + 256],
                                     lora_c[:, m * 256 + k * 128:m * 256 + k * 128 + 128],
                                     lora_p[:, m * 256:m * 256 + 256], start=True, stop=True)
                last.then_inc(filled, 1)

            def lora_wo(of, loaded):
                pe.wait_ge(lora_lo, loaded)
                pe.wait_ge(of[1], of[2])
                for h in range(2):
                    last = pe.matmul(of[0][:, h * 256:h * 256 + 256],
                                     lora_p[:, 768 + h * 128:768 + h * 128 + 128],
                                     lora_c[:, 768:1024], start=True, stop=True)
                last.then_inc(filled, 1)

            def project(of, slot, t):
                head, half = t // 2 % 2, t % 2
                col = (t // 4) * 256 + head * 128
                pe.wait_ge(of[1], of[2])
                three(of[0], lambda a, k: w_parts[a][:, slot, k, col:col + 128],
                      lambda b, k: t_parts[b][:, k, half * 512:half * 512 + 512], range(KD)) \
                    .then_inc(filled, 1)

            def values(of, slot, v):
                pe.wait_ge(of[1], of[2])
                for i in range(2):
                    at = (2 * v + i) * 128
                    last = three(of[0][:, i * 256:i * 256 + 256],
                                 lambda a, k: t_parts[a][:, k, at:at + 128],
                                 lambda b, k: w_parts[b][:, slot, k, 512:768], range(KD))
                last.then_inc(filled, 1)

            pe.wait_ge(ld_mod_a, 16)
            pe.wait_ge(c_spread, 1)
            modulation(bank[0][:, :], 0, 512).then_inc(mod_ready, 1)
            pe.wait_ge(ld_mod_b, 16)
            for j in range(2 * KD):
                col = 3 * D + j * 128
                for k in range(KD):
                    last = pe.matmul(bank[5][:, j:j + 1], wm_sb[:, k, col:col + 128],
                                     sil_c[:, k:k + 1], start=k == 0, stop=k == KD - 1)
            last.then_inc(mod_ready, 1)
            pe.wait_ge(all_lo, 1)
            lora(ahead("G", 0), 1, 0)
            lora(ahead("G", 1), 1, 1)
            pe.wait_ge(ld_mod_c, 32)
            modulation(bank[1][:, 0:D], 2 * D, D)
            modulation(bank[1][:, D:2 * D], 5 * D, D).then_inc(mod_ready, 1)
            lora(ahead("G", 2), 1, 2)
            pe.wait_ge(ld_id, 16)

            def turn_h(n):
                k, half = n % 2, n // 2
                pe.wait_ge(h_normed, 4 * half + 4)
                for b in range(4):
                    last = pe.transpose(bank[2 + n][:, b * 128:b * 128 + 128],
                                        h_norm[:, 4 * half + b, k * 128:k * 128 + 128], id_sb[:, :])
                last.then_inc(h_turned, 1)

            turn_h(0)
            turn_h(1)
            turn_h(2)
            pe.wait_ge(cols_kept, 1)
            turn_h(3)
            for kind, n in AHEAD[3:]:
                of = ahead(kind, n)
                if (kind, n) == ("Q", 0):
                    pe.wait_ge(w_lo_done, 3)
                    pe.wait_ge(h_lo, 2)
                if (kind, n) == ("Q", 4):
                    pe.wait_ge(h_lo, 4)
                if kind == "Q":
                    project(of, 0, PARTS[n])
                if kind == "V":
                    values(of, 0, n)
                if kind == "P":
                    lora_wo(of, 2)
                if kind == "G1":
                    lora(of, 2, n)
            pe.wait_ge(ld_mask, 16)
            pe.wait_ge(zeroed, 2)

            def turn_z(n):
                k, half = n % 2, n // 2
                pe.wait_ge(z_done, 4 * half + 4)
                if half:
                    pe.wait_ge(z_hi, k + 1)
                else:
                    pe.wait_ge((p_kept, o_kept)[k], 4 * PAIRS + 1)
                for b in range(4):
                    last = pe.transpose(FILL_BANK[k][:, b * 128:b * 128 + 128],
                                        z_sb[:, 4 * half + b, k * 128:k * 128 + 128], id_sb[:, :])
                last.then_inc(z_turned, 1)

            def step(p, slot, half, order, at):
                for kind, n in order:
                    unit, group, head = p * 4 + n, n // 2, n % 2
                    free = unit + (1 if at or n == 0 else 0)
                    if kind in FILL_KINDS:
                        of = fill(p, at[kind, n])
                    if kind == "S":
                        if n % 2 == 0:
                            pe.wait_ge(rotated, p * 8 + (8 + 2 * n))
                        pe.wait_ge(masked, unit + 1)
                        for b in range(4):
                            for c in range(2):
                                q0 = (group * 8 + 2 * b + c) * 64
                                last = pe.matmul(
                                    S_BANK[n % 2][64 * c:64 * c + 64, b * 128:b * 128 + 128],
                                    q_t[:, slot, head, q0:q0 + 64],
                                    k_t[:, slot, head, q0:q0 + 128], start=True, stop=True)
                        last.then_inc(scored, 1)
                    if kind == "T":
                        pe.wait_ge(exped, unit + 3)
                        pe.wait_ge(p_kept, free)
                        for b in range(4):
                            last = pe.transpose(unit_bank("T", n, not at)[:, b * 128:b * 128 + 128],
                                                probs[:, n % 2, b * 128:b * 128 + 128], id_sb[:, :])
                        last.then_inc(p_turned, 1)
                    if kind == "O":
                        if n == 0:
                            pe.wait_ge(v_moved[slot], half * 32 + 32)
                        pe.wait_ge(p_kept, unit + 2)
                        pe.wait_ge(o_kept, free)
                        result = unit_bank("O", n, not at)
                        for b in range(4):
                            for c, source in enumerate((v_off, v_sb)):
                                q0 = b * 128 + 64 * c
                                last = pe.matmul(
                                    result[64 * c:64 * c + 64, b * 128:b * 128 + 128],
                                    probs_t[:, n % 2, q0:q0 + 64],
                                    source[:, slot, group * 4 + b, head * 128:head * 128 + 128],
                                    start=True, stop=True)
                        last.then_inc(o_ready, 1)
                    if kind == "X":
                        pe.wait_ge(o_kept, unit + 2)
                        pe.wait_ge(ol_kept, free)
                        if n % 2 == 0:
                            pe.wait_ge(w_added, unit + 2)
                        elif not at:
                            pe.wait_ge(w_added, unit + 1)
                        for b in range(4):
                            last = pe.transpose(unit_bank("X", n, not at)[:, b * 128:b * 128 + 128],
                                                o_norm[:, n % 2, b * 128:b * 128 + 128],
                                                id_sb[:, :])
                        last.then_inc(o_turned, 1)
                    if kind == "W":
                        if n == 0:
                            pe.wait_ge(wo_lo_done, p + 1)
                        pe.wait_ge(ol_kept, p * 4 + (2 * group + 3))
                        pe.wait_ge(w_added, unit + 1)
                        for i in range(2):
                            col = (2 * (n % 2) + i) * 128
                            last = three(unit_bank("W", n, not at)[:, i * 256:i * 256 + 256],
                                         lambda a, h: o_parts[a][:, h, col:col + 128],
                                         lambda b, h: wo_parts[b][:, slot, h], range(2))
                        last.then_inc(w_ready, 1)
                    if kind == "Q":
                        if n == 0:
                            pe.wait_ge(w_lo_done, p * 3 + 6)
                        project(of, 1 - slot, PARTS[n])
                    if kind == "V":
                        values(of, 1 - slot, n)
                    if kind == "G":
                        lora(of, p + 3, n)
                    if kind == "P":
                        lora_wo(of, p + 3)
                    if kind == "Z":
                        turn_z(n)

            steps(pe, PE_STEP, PE_LAST, step)

            def clear():
                for j in range(2):
                    pe.matmul(bank[j][:, :], zero_bf, mask_sb[:, 0], start=True,
                              stop=False, skip_group_check=True)

            def up(c, slot, half):
                cols = slice(half * 512, half * 512 + 512)
                pe.wait_ge(up_w_lo, c + 1)
                for m in range(2):
                    last = three(bank[2 + 2 * slot + m][:, :],
                                 lambda a, k: w_parts[a][:, slot, 0, m * 256 + k * 128:
                                                         m * 256 + k * 128 + 128],
                                 lambda b, k: t_parts[b][:, k, cols], range(KD))
                return last

            def gate(slot, half):
                return pe.matmul(bank[6 + slot][:, :], w_hi[0:GK, slot, 0, 512:UPW],
                                 gate_t[:, half], start=True, stop=True)

            def up_and_gate(c, slot, half):
                pe.wait_ge(act_done, c - 1)
                up(c, slot, half)
                gate(slot, half).then_inc(up_ready, 1)

            def down(c, slot):
                pe.wait_ge(down_w_lo, c + 1)
                pe.wait_ge(act_lo, c + 1)
                for b in range(4):
                    dst = bank[b // 2][:, (b % 2) * 256:(b % 2) * 256 + 256]
                    for a, w in ((0, 0), (0, 1), (1, 0)):
                        last = pe.matmul(dst, o_parts[a][:, slot, b * 128:b * 128 + 128],
                                         wo_parts[w][:, slot, 0], start=False, stop=True,
                                         skip_group_check=True)
                last.then_inc(down_done, 1)

            pe.wait_ge(zeroed, 3)
            pe.wait_ge(z_lo, 2)
            up(0, 0, 0).then_inc(up_ready, 1)
            pe.wait_ge(w_added, 4 * PAIRS + 2)
            up(1, 1, 0).then_inc(up_ready, 1)
            for half in range(2):
                if half == 0:
                    turn_z(2)
                    turn_z(3)
                if half == 1:
                    pe.wait_ge(z_kept, 4)
                for b in range(4 * half, 4 * half + 4):
                    for k in range(KD):
                        last = pe.matmul(LG_BANK[:, b * E:b * E + E],
                                         h2_t[:, k, b * 128:b * 128 + 128], gw_sb[:, k],
                                         start=k == 0, stop=k == KD - 1)
            last.then_inc(logits, 1)
            pe.wait_ge(act_done, 1)
            up(2, 0, 0).then_inc(up_ready, 1)
            pe.wait_ge(lg_done, 1)
            clear()
            down(0, 0)
            pe.wait_ge(act_done, 2)
            up(3, 1, 0)
            down(1, 1)
            pe.wait_ge(gates_done, 2)
            pe.wait_ge(z_hi, 4)
            for n in range(2):
                for b in range(4):
                    last = pe.transpose(FILL_BANK[n][0:GK, b * 128:b * 128 + 128],
                                        g_cat[:, 4 * n + b], id_sb[:, :])
                last.then_inc(g_turned, 1)
            pe.wait_ge(gates_kept, 2)
            gate(1, 0).then_inc(up_ready, 1)
            with pe.Fori(1, CH // 2 - 1) as i:
                for slot in range(2):
                    up_and_gate(i * 2 + (slot + 2), slot, 0)
                    down(i * 2 + slot, slot)
            pe.wait_ge(z_lo, 4)
            for slot in range(2):
                up_and_gate(CH + slot, slot, 1)
                down(CH - 2 + slot, slot)
            for slot in range(2):
                up_and_gate(CH + 2 + slot, slot, 1)
                if slot == 0:
                    pe.wait_ge(y_scaled, 2)
                    clear()
                down(CH + slot, slot)
            with pe.Fori(CH // 2 + 1, CH - 1) as i:
                for slot in range(2):
                    up_and_gate(i * 2 + (slot + 2), slot, 1)
                    down(i * 2 + slot, slot)
            for slot in range(2):
                down(2 * CH - 2 + slot, slot)


def kernel(**inputs):
    import numpy as np
    import concourse.bacc as bacc
    from concourse.bass_utils import run_bass_kernel_spmd

    a = {k[3:]: np.asarray(v) for k, v in inputs.items()}
    f32 = np.float32

    theta = f32(1.0) / np.power(f32(10000.0), np.arange(DH // 2, dtype=f32) / f32(DH // 2))
    freqs = np.arange(T, dtype=f32)[:, None] * theta[None, :]
    cos_t = np.cos(np.concatenate([freqs, freqs], 1)).T
    sin = np.sin(freqs).T
    sin_t = np.concatenate([sin, -sin], 0)
    row, key = np.arange(64)[:, None], np.arange(128)[None, :]
    open_ = (key >= row + 1) & (key <= row + WIN)
    mask = np.zeros((2, 128, 4, 128), f32)
    for g in range(2):
        for c in range(2):
            for b in range(4):
                seen = open_ & (key >= WIN) if g == b == c == 0 else open_
                mask[g, 64 * c:64 * c + 64, b] = np.where(seen, 0.0, -1e30)
    from concourse import mybir as _mybir
    mask = mask.transpose(1, 0, 2, 3).reshape(128, 2, 512).astype(_mybir.dt.np(_mybir.dt.bfloat16))
    sel = np.zeros((CH, 128, 128), f32)
    for c in range(CH):
        for i in range(128):
            n = c * 128 + i
            n -= SHARED * 128
            for r in ((n // FI, E + n // FI) if n >= 0 else (2 * E,)):
                sel[c, r, i] = 1.0
    tie = np.tile(np.arange(E, 0, -1, dtype=f32), (128, NB))

    def by_pair(w):
        return w.reshape(PAIRS, 2 * DH, -1).transpose(0, 2, 1)

    w_qkv = np.concatenate([by_pair(a["attn_w" + m]) for m in "qkv"], 2)
    w_qkv = w_qkv.reshape(PAIRS, KD, 128, PW).transpose(0, 2, 1, 3)

    def groups(w):
        pad = [(0, 0)] * (w.ndim - 2) + [(0, 32 - R), (0, 0)]
        return np.concatenate([np.pad(w, pad)] * 3, w.ndim - 2)

    none = np.zeros((1, 96, 2 * DH), f32)
    b_pairs = [np.concatenate([groups(by_pair(a["attn_" + m + "B"])), none]) for m in "qkv"]
    a_o = groups(a["attn_oA"].reshape(R, PAIRS, 2 * DH).transpose(1, 0, 2))
    lora_pairs = np.concatenate(b_pairs + [np.concatenate([none, a_o])], 2)
    lora_all = np.concatenate([groups(a["attn_" + m + "A"]) for m in "qkv"]
                              + [groups(a["attn_oB"].T)], 1)
    w_o = a["attn_wo"].T.reshape(PAIRS, 2, DH, D).transpose(0, 2, 1, 3)

    def chunks(experts, shared):
        w = np.concatenate([shared, np.zeros((D, SHARED * 128 - 2 * FI), f32),
                            experts.transpose(1, 0, 2).reshape(D, E * FI)], 1)
        return w.reshape(KD, 128, CH, 128).transpose(2, 1, 0, 3).reshape(CH, 128, KD * 128)

    w_up = np.concatenate([chunks(a["ffn_w1"], a["ffn_sw1"]), chunks(a["ffn_w3"], a["ffn_sw3"]),
                           sel], 2)
    w_down = np.concatenate([a["ffn_sw2"], np.zeros((SHARED * 128 - 2 * FI, D), f32),
                             a["ffn_w2"].reshape(E * FI, D)]).reshape(CH, 128, D)

    arrays = {
        "x": a["attn_x"].reshape(T, D), "cos_t": cos_t, "sin_t": sin_t, "mask": mask,
        "ident": np.eye(128, dtype=f32), "c_col": a["c"].reshape(KD, 128).T,
        "w_mod": a["wmod"].reshape(KD, 128, 6 * D).transpose(1, 0, 2),
        "norm_w": a["attn_norm_w"].reshape(KD, 128).T,
        "w_qkv": w_qkv, "w_o": w_o, "lora_pairs": lora_pairs, "lora_all": lora_all,
        "gate_w": a["ffn_gate_w"].T.reshape(KD, 128, E).transpose(1, 0, 2),
        "w_up": w_up, "w_down": w_down, "tie": tie,
    }
    nc = bacc.Bacc("TRN2", target_bir_lowering=False, num_devices=1)
    args, given = {}, {}
    for name, array in arrays.items():
        array = np.ascontiguousarray(array)
        given[f"in_{name}"] = array
        args[name] = nc.dram_tensor(f"in_{name}", array.shape, mybir.dt.from_np(array.dtype),
                                    kind="ExternalInput").ap()
    args["out"] = nc.dram_tensor("out_y", (T, D), mybir.dt.float32, kind="ExternalOutput").ap()
    build(nc, **args)
    result = run_bass_kernel_spmd(nc, [given], core_ids=[0])
    return result.results[0]["out_y"].reshape(1, T, D)
```
